# Optimizing a Trainium2 kernel written in Bass

```python
import numpy as np
import jax
import jax.numpy as jnp

def _softmax(x, axis=-1):
    return jax.nn.softmax(x, axis=axis)

def _gelu(x):
    return jax.nn.gelu(x, approximate=True)

def _silu(x):
    return jax.nn.silu(x)

def _sigmoid(x):
    return jax.nn.sigmoid(x)

def _layernorm(x, axis=-1, eps=1e-05):
    m = jnp.mean(x, axis=axis, keepdims=True)
    v = jnp.var(x, axis=axis, keepdims=True)
    return (x - m) / jnp.sqrt(v + eps)

def _scatter_add(tgt, idx, src, axis=0):
    return tgt.at[idx].add(src)

def _segment_sum(src, seg, n):
    return jax.ops.segment_sum(src, seg, n)
kernel_name = 'mk_flamingo_gated_d4_seqx_r8_621cad'

def setup_inputs(seed: int=0):
    np.random.seed(seed)
    _w = jnp.asarray

    def _rec_inputs():
        import jax
        import jax.numpy as jnp
        _rk = jax.random.key(seed)
        x = 7.22e-05 + 1 * jax.random.normal(jax.random.fold_in(_rk, 1), (16, 64, 128), jnp.float32)
        _lenS = 64 - jax.random.randint(jax.random.fold_in(_rk, 7), (16,), 0, max(1, 64 // 4) + 1, jnp.int32)
        _lenS2 = 64 - jax.random.randint(jax.random.fold_in(_rk, 8), (16,), 0, max(1, 64 // 4) + 1, jnp.int32)
        _ctx_1024P = jax.random.normal(jax.random.fold_in(_rk, 11), (16, 16, 128), jnp.float32)
        _ctx_1024c = jax.random.dirichlet(jax.random.fold_in(_rk, 511), 0.3 * jnp.ones((16,), jnp.float32), (16, 64))
        _ctx_1024t = jnp.einsum('bsk,bkd->bsd', _ctx_1024c, _ctx_1024P)
        _ctx_1024t = _ctx_1024t * jax.lax.rsqrt(jnp.mean(jnp.square(_ctx_1024t)) + 1e-12) * 0.953939
        ctx_1024 = 4.13588e-05 + 0.999923 * (_ctx_1024t + 0.3 * jax.random.normal(jax.random.fold_in(_rk, 611), (16, 64, 128), jnp.float32))
        _validS = jnp.arange(64)[None, :] < _lenS[:, None]
        _validS2 = jnp.arange(64)[None, :] < _lenS2[:, None]
        _causal = jnp.tril(jnp.ones((64, 64), dtype=bool))
        mask_1x1xSxS2_ik0 = jnp.where(jnp.broadcast_to(_validS2[0:1, None, None, :], (1, 1, 64, 64)), 0, 1).astype(jnp.int32)
        _g = jax.random.normal(jax.random.fold_in(_rk, 9001), (2, 4), jnp.float32)
        _g = jnp.sign(_g) * jnp.maximum(jnp.abs(_g), 1.0) + (_g == 0) * 1.0
        g_xattn = _g[0]
        g_ffn = _g[1]
        return (x, ctx_1024, mask_1x1xSxS2_ik0, g_xattn, g_ffn)
    x, ctx_1024, mask_1x1xSxS2_ik0, g_xattn, g_ffn = _rec_inputs()

    def _L0_xattn_setup():
        import jax, jax.numpy as jnp
        import numpy as np
        import math
        B, S, D, H = (4, 256, 128, 16)
        DK = D // H

        def _rope_tables(seq_len, dim, dtype=jnp.float32):
            inv_freq = 1.0 / 10000.0 ** (jnp.arange(0, dim, 2, dtype=jnp.float32) / dim)
            t = jnp.arange(seq_len, dtype=jnp.float32)
            freqs = jnp.einsum('i,j->ij', t, inv_freq)
            emb = jnp.concatenate([freqs, freqs], axis=-1)
            return (jnp.cos(emb).astype(dtype)[None, None], jnp.sin(emb).astype(dtype)[None, None])

        def _apply_rope(x, cos, sin):
            x_rot = jnp.concatenate([-x[..., 1::2], x[..., ::2]], axis=-1)
            return x * cos + x_rot * sin
        key = jax.random.key(seed)
        ks = jax.random.split(key, 12)
        scale = 1.0 / math.sqrt(D)
        inp = {'query': jax.random.normal(ks[0], (B, S, D), jnp.float32), 'key': jax.random.normal(ks[1], (B, S, D), jnp.float32), 'value': jax.random.normal(ks[2], (B, S, D), jnp.float32), 'mask': jnp.tril(jnp.ones((S, S), jnp.int32))[None, None], 'w_q': jax.random.normal(ks[3], (D, D), jnp.float32) * scale, 'b_q': jnp.zeros((D,), jnp.float32), 'w_k': jax.random.normal(ks[4], (D, D), jnp.float32) * scale, 'b_k': jnp.zeros((D,), jnp.float32), 'w_v': jax.random.normal(ks[5], (D, D), jnp.float32) * scale, 'b_v': jnp.zeros((D,), jnp.float32), 'w_o': jax.random.normal(ks[6], (D, D), jnp.float32) * scale, 'b_o': jnp.zeros((D,), jnp.float32)}
        return inp
    _L0_xattn_all = _L0_xattn_setup()
    _L0_xattn_in = {k: v for k, v in _L0_xattn_all.items() if k in ('w_q', 'b_q', 'w_k', 'b_k', 'w_v', 'b_v', 'w_o', 'b_o')}
    del _L0_xattn_all

    def _L0_ffn_setup():
        import jax, jax.numpy as jnp
        import numpy as np
        EPS = 1e-09
        key = jax.random.key(seed)
        k1, k2, k3, k4 = jax.random.split(key, 4)
        B, T, H, D, E = (2, 256, 128, 128, 8)
        x = jax.random.normal(k1, (B, T, H), dtype=jnp.float32)
        gate_w = jax.random.normal(k2, (E, H), dtype=jnp.float32) * 0.02
        gate_up_proj = jax.random.normal(k3, (E, H, 2 * D), dtype=jnp.float32) * 0.02
        down_proj = jax.random.normal(k4, (E, D, H), dtype=jnp.float32) * 0.02
        return {'x': x, 'gate_w': gate_w, 'gate_up_proj': gate_up_proj, 'down_proj': down_proj}
    _L0_ffn_all = _L0_ffn_setup()
    _L0_ffn_in = {k: v for k, v in _L0_ffn_all.items() if k in ('gate_w', 'gate_up_proj', 'down_proj')}
    del _L0_ffn_all

    def _L1_xattn_setup():
        import jax, jax.numpy as jnp
        import numpy as np
        D_MODEL = 128
        H = 16
        D_K = D_MODEL // H
        B, S = (4, 256)
        key = jax.random.key(seed)
        ks = jax.random.split(key, 12)
        std = 1.0 / np.sqrt(D_MODEL)
        inp = {'q': jax.random.normal(ks[0], (B, S, D_MODEL), dtype=jnp.float32), 'k': jax.random.normal(ks[1], (B, S, D_MODEL), dtype=jnp.float32), 'v': jax.random.normal(ks[2], (B, S, D_MODEL), dtype=jnp.float32), 'mask': jnp.tril(jnp.ones((S, S), dtype=jnp.int32))[None, None], 'w_q': jax.random.normal(ks[3], (D_MODEL, D_MODEL), dtype=jnp.float32) * std, 'b_q': jax.random.normal(ks[4], (D_MODEL,), dtype=jnp.float32) * std, 'w_k': jax.random.normal(ks[5], (D_MODEL, D_MODEL), dtype=jnp.float32) * std, 'b_k': jax.random.normal(ks[6], (D_MODEL,), dtype=jnp.float32) * std, 'w_v': jax.random.normal(ks[7], (D_MODEL, D_MODEL), dtype=jnp.float32) * std, 'b_v': jax.random.normal(ks[8], (D_MODEL,), dtype=jnp.float32) * std, 'w_o': jax.random.normal(ks[9], (D_MODEL, D_MODEL), dtype=jnp.float32) * std, 'b_o': jax.random.normal(ks[10], (D_MODEL,), dtype=jnp.float32) * std}
        return inp
    _L1_xattn_all = _L1_xattn_setup()
    _L1_xattn_in = {k: v for k, v in _L1_xattn_all.items() if k in ('w_q', 'b_q', 'w_k', 'b_k', 'w_v', 'b_v', 'w_o', 'b_o')}
    del _L1_xattn_all

    def _L1_ffn_setup():
        import jax, jax.numpy as jnp
        import numpy as np
        NUM_HEADS = 16
        TOP_K = 2
        key = jax.random.key(seed)
        ks = jax.random.split(key, 5)
        B, S, D, E = (4, 256, 128, 8)
        scale = 0.02
        return {'x': jax.random.normal(ks[0], (B, S, D), dtype=jnp.float32), 'W_qkv': jax.random.normal(ks[1], (D, 3 * D), dtype=jnp.float32) * scale, 'b_qkv': jnp.zeros((3 * D,), dtype=jnp.float32), 'W_gate': jax.random.normal(ks[2], (D, E), dtype=jnp.float32) * scale, 'b_gate': jnp.zeros((E,), dtype=jnp.float32), 'W_experts': jax.random.normal(ks[3], (E, D, D), dtype=jnp.float32) * scale, 'b_experts': jnp.zeros((E, D), dtype=jnp.float32)}
    _L1_ffn_all = _L1_ffn_setup()
    _L1_ffn_in = {k: v for k, v in _L1_ffn_all.items() if k in ('W_qkv', 'b_qkv', 'W_gate', 'b_gate', 'W_experts', 'b_experts')}
    del _L1_ffn_all

    def _L2_xattn_setup():
        import jax, jax.numpy as jnp
        import numpy as np
        B, T, N_EMBD, N_HEAD = (2, 256, 128, 16)
        HEAD = N_EMBD // N_HEAD
        WINDOW = 64
        key = jax.random.key(seed)
        kq, kk, kv, kw = jax.random.split(key, 4)
        q = jax.random.normal(kq, (B, T, N_EMBD), dtype=jnp.float32)
        k = jax.random.normal(kk, (B, T, N_EMBD), dtype=jnp.float32)
        v = jax.random.normal(kv, (B, T, N_EMBD), dtype=jnp.float32)
        W_proj = jax.random.normal(kw, (N_EMBD, N_EMBD), dtype=jnp.float32) * (1.0 / np.sqrt(N_EMBD))
        b_proj = jnp.zeros((N_EMBD,), dtype=jnp.float32)
        return {'q': q, 'k': k, 'v': v, 'W_proj': W_proj, 'b_proj': b_proj}
    _L2_xattn_all = _L2_xattn_setup()
    _L2_xattn_in = {k: v for k, v in _L2_xattn_all.items() if k in ('W_proj', 'b_proj')}
    del _L2_xattn_all

    def _L2_ffn_setup():
        import jax, jax.numpy as jnp
        import numpy as np
        import math
        B, S, D = (4, 256, 128)
        E, DFF = (16, 256)
        CAP_FACTOR = 2.0
        ROUTER_HIDDEN = 128
        CAPACITY = int(math.ceil(S * CAP_FACTOR / E))
        key = jax.random.key(seed)
        ks = jax.random.split(key, 6)

        def uinit(k, shape, fan_in):
            bound = math.sqrt(3.0) * math.sqrt(1.0 / 3.0) / math.sqrt(fan_in)
            return jax.random.uniform(k, shape, jnp.float32, -bound, bound)
        return {'hidden_states': jax.random.normal(ks[0], (B, S, D), jnp.float32), 'router_w1': jax.random.normal(ks[1], (D, ROUTER_HIDDEN), jnp.float32) / math.sqrt(D), 'router_w2': jax.random.normal(ks[2], (ROUTER_HIDDEN, E), jnp.float32) / math.sqrt(ROUTER_HIDDEN), 'w1': uinit(ks[3], (E, D, DFF), D), 'w2': uinit(ks[4], (E, D, DFF), D), 'w3': uinit(ks[5], (E, DFF, D), DFF)}
    _L2_ffn_all = _L2_ffn_setup()
    _L2_ffn_in = {k: v for k, v in _L2_ffn_all.items() if k in ('router_w1', 'router_w2', 'w1', 'w2', 'w3')}
    del _L2_ffn_all

    def _L3_xattn_setup():
        import jax, jax.numpy as jnp
        import numpy as np
        B, T, D = (8, 256, 128)
        key = jax.random.key(seed)
        k1, k2 = jax.random.split(key)
        return {'key': jax.random.normal(k1, (B, T, D), dtype=jnp.float32), 'value': jax.random.normal(k2, (B, T, D), dtype=jnp.float32)}
    _L3_xattn_all = _L3_xattn_setup()
    _L3_xattn_in = {k: v for k, v in _L3_xattn_all.items() if k in ()}
    del _L3_xattn_all

    def _L3_ffn_setup():
        import jax, jax.numpy as jnp
        import numpy as np
        B, S, D = (1, 256, 128)
        I = 256
        E = 8
        K = 2
        LIMIT = 7.0
        ALPHA = 1.702
        EPS = 1e-05

        def _swiglu(h):
            x_glu = jnp.minimum(h[..., ::2], LIMIT)
            x_lin = jnp.clip(h[..., 1::2], -LIMIT, LIMIT)
            return x_glu * jax.nn.sigmoid(ALPHA * x_glu) * (x_lin + 1.0)

        def _moe(t, gate_w, gate_b, mlp1_w, mlp1_b, mlp2_w, mlp2_b):
            T = t.shape[0]
            logits = t @ gate_w + gate_b
            top_v, top_i = jax.lax.top_k(logits, K)
            probs = jax.nn.softmax(top_v, axis=-1)
            w = jnp.zeros((T, E), t.dtype).at[jnp.arange(T)[:, None], top_i].set(probs)

            def body(acc, ew):
                w1, b1, w2, b2, we = ew
                h = _swiglu(t @ w1 + b1)
                y = h @ w2 + b2
                return (acc + we[:, None] * y, None)
            acc0 = jnp.zeros((T, t.shape[1]), t.dtype)
            acc, _ = jax.lax.scan(body, acc0, (mlp1_w, mlp1_b, mlp2_w, mlp2_b, w.T))
            return acc
        key = jax.random.key(seed)
        ks = jax.random.split(key, 4)
        s = 0.02
        return {'x': jax.random.normal(ks[0], (B, S, D), jnp.float32), 'norm_scale': jnp.ones((D,), jnp.float32), 'gate_w': jax.random.normal(ks[1], (D, E), jnp.float32) * s, 'gate_b': jnp.zeros((E,), jnp.float32), 'mlp1_w': jax.random.normal(ks[2], (E, D, 2 * I), jnp.float32) * s, 'mlp1_b': jnp.zeros((E, 2 * I), jnp.float32), 'mlp2_w': jax.random.normal(ks[3], (E, I, D), jnp.float32) * s, 'mlp2_b': jnp.zeros((E, D), jnp.float32)}
    _L3_ffn_all = _L3_ffn_setup()
    _L3_ffn_in = {k: v for k, v in _L3_ffn_all.items() if k in ('norm_scale', 'gate_w', 'gate_b', 'mlp1_w', 'mlp1_b', 'mlp2_w', 'mlp2_b')}
    del _L3_ffn_all
    return {'x': x, 'ctx_1024': ctx_1024, 'mask_1x1xSxS2_ik0': mask_1x1xSxS2_ik0, 'g_xattn': g_xattn, 'g_ffn': g_ffn, 'L0_xattn_w_q': _L0_xattn_in['w_q'], 'L0_xattn_b_q': _L0_xattn_in['b_q'], 'L0_xattn_w_k': _L0_xattn_in['w_k'], 'L0_xattn_b_k': _L0_xattn_in['b_k'], 'L0_xattn_w_v': _L0_xattn_in['w_v'], 'L0_xattn_b_v': _L0_xattn_in['b_v'], 'L0_xattn_w_o': _L0_xattn_in['w_o'], 'L0_xattn_b_o': _L0_xattn_in['b_o'], 'L0_ffn_gate_w': _L0_ffn_in['gate_w'], 'L0_ffn_gate_up_proj': _L0_ffn_in['gate_up_proj'], 'L0_ffn_down_proj': _L0_ffn_in['down_proj'], 'L1_xattn_w_q': _L1_xattn_in['w_q'], 'L1_xattn_b_q': _L1_xattn_in['b_q'], 'L1_xattn_w_k': _L1_xattn_in['w_k'], 'L1_xattn_b_k': _L1_xattn_in['b_k'], 'L1_xattn_w_v': _L1_xattn_in['w_v'], 'L1_xattn_b_v': _L1_xattn_in['b_v'], 'L1_xattn_w_o': _L1_xattn_in['w_o'], 'L1_xattn_b_o': _L1_xattn_in['b_o'], 'L1_ffn_W_qkv': _L1_ffn_in['W_qkv'], 'L1_ffn_b_qkv': _L1_ffn_in['b_qkv'], 'L1_ffn_W_gate': _L1_ffn_in['W_gate'], 'L1_ffn_b_gate': _L1_ffn_in['b_gate'], 'L1_ffn_W_experts': _L1_ffn_in['W_experts'], 'L1_ffn_b_experts': _L1_ffn_in['b_experts'], 'L2_xattn_W_proj': _L2_xattn_in['W_proj'], 'L2_xattn_b_proj': _L2_xattn_in['b_proj'], 'L2_ffn_router_w1': _L2_ffn_in['router_w1'], 'L2_ffn_router_w2': _L2_ffn_in['router_w2'], 'L2_ffn_w1': _L2_ffn_in['w1'], 'L2_ffn_w2': _L2_ffn_in['w2'], 'L2_ffn_w3': _L2_ffn_in['w3'], 'L3_ffn_norm_scale': _L3_ffn_in['norm_scale'], 'L3_ffn_gate_w': _L3_ffn_in['gate_w'], 'L3_ffn_gate_b': _L3_ffn_in['gate_b'], 'L3_ffn_mlp1_w': _L3_ffn_in['mlp1_w'], 'L3_ffn_mlp1_b': _L3_ffn_in['mlp1_b'], 'L3_ffn_mlp2_w': _L3_ffn_in['mlp2_w'], 'L3_ffn_mlp2_b': _L3_ffn_in['mlp2_b']}

def reference(x, ctx_1024, mask_1x1xSxS2_ik0, g_xattn, g_ffn, L0_xattn_w_q, L0_xattn_b_q, L0_xattn_w_k, L0_xattn_b_k, L0_xattn_w_v, L0_xattn_b_v, L0_xattn_w_o, L0_xattn_b_o, L0_ffn_gate_w, L0_ffn_gate_up_proj, L0_ffn_down_proj, L1_xattn_w_q, L1_xattn_b_q, L1_xattn_w_k, L1_xattn_b_k, L1_xattn_w_v, L1_xattn_b_v, L1_xattn_w_o, L1_xattn_b_o, L1_ffn_W_qkv, L1_ffn_b_qkv, L1_ffn_W_gate, L1_ffn_b_gate, L1_ffn_W_experts, L1_ffn_b_experts, L2_xattn_W_proj, L2_xattn_b_proj, L2_ffn_router_w1, L2_ffn_router_w2, L2_ffn_w1, L2_ffn_w2, L2_ffn_w3, L3_ffn_norm_scale, L3_ffn_gate_w, L3_ffn_gate_b, L3_ffn_mlp1_w, L3_ffn_mlp1_b, L3_ffn_mlp2_w, L3_ffn_mlp2_b):
    import jax
    import jax.numpy as jnp

    def _L0_xattn_ref(query, key, value, mask, w_q, b_q, w_k, b_k, w_v, b_v, w_o, b_o):
        import jax, jax.numpy as jnp
        import numpy as np
        import math
        B, S, D, H = (4, 256, 128, 16)
        DK = D // H

        def _rope_tables(seq_len, dim, dtype=jnp.float32):
            inv_freq = 1.0 / 10000.0 ** (jnp.arange(0, dim, 2, dtype=jnp.float32) / dim)
            t = jnp.arange(seq_len, dtype=jnp.float32)
            freqs = jnp.einsum('i,j->ij', t, inv_freq)
            emb = jnp.concatenate([freqs, freqs], axis=-1)
            return (jnp.cos(emb).astype(dtype)[None, None], jnp.sin(emb).astype(dtype)[None, None])

        def _apply_rope(x, cos, sin):
            x_rot = jnp.concatenate([-x[..., 1::2], x[..., ::2]], axis=-1)
            return x * cos + x_rot * sin
        b, s, _ = query.shape

        def proj(x, w, bias):
            return (x @ w.T + bias).reshape(b, -1, H, DK).transpose(0, 2, 1, 3)
        Q = proj(query, w_q, b_q)
        K = proj(key, w_k, b_k)
        V = proj(value, w_v, b_v)
        cos, sin = _rope_tables(s, DK, Q.dtype)
        Q = _apply_rope(Q, cos, sin)
        K = _apply_rope(K, cos, sin)
        scores = jnp.einsum('bhqd,bhkd->bhqk', Q, K) / math.sqrt(DK)
        scores = jnp.where(mask == 0, jnp.asarray(-1000000000.0, scores.dtype), scores)
        attn = jax.nn.softmax(scores, axis=-1)
        ctx = jnp.einsum('bhqk,bhkd->bhqd', attn, V)
        ctx = ctx.transpose(0, 2, 1, 3).reshape(b, -1, D)
        return ctx @ w_o.T + b_o

    def _L0_ffn_ref(x, gate_w, gate_up_proj, down_proj):
        import jax, jax.numpy as jnp
        import numpy as np
        EPS = 1e-09
        B, T, H = x.shape
        E = gate_w.shape[0]
        top_k = 2
        hidden = x.reshape(-1, H)
        router_logits = hidden @ gate_w.T
        routing_weights = jax.nn.softmax(router_logits.astype(jnp.float32), axis=-1)
        topk_weights, topk_indices = jax.lax.top_k(routing_weights, top_k)
        topk_weights = topk_weights / (jnp.sum(topk_weights, axis=-1, keepdims=True) + EPS)
        N = hidden.shape[0]
        routed = jnp.zeros((N, E), dtype=router_logits.dtype)
        rows = jnp.arange(N)[:, None]
        routed = routed.at[rows, topk_indices].set(topk_weights.astype(router_logits.dtype))
        routed = routed / (jnp.sum(routed, axis=-1, keepdims=True) + EPS)
        routed = routed.astype(hidden.dtype)
        gate_up = jnp.einsum('th,ehq->teq', hidden, gate_up_proj)
        gate, up = jnp.split(gate_up, 2, axis=-1)
        expert_outputs = jnp.einsum('teq,eqh->teh', jax.nn.silu(gate) * up, down_proj)
        out = jnp.sum(expert_outputs * routed[:, :, None], axis=1)
        return out.reshape(B, T, H)

    def _L1_xattn_ref(q, k, v, mask, w_q, b_q, w_k, b_k, w_v, b_v, w_o, b_o):
        import jax, jax.numpy as jnp
        import numpy as np
        D_MODEL = 128
        H = 16
        D_K = D_MODEL // H
        B, S = (4, 256)
        b, s, _ = q.shape
        query = q @ w_q.T + b_q
        key_ = k @ w_k.T + b_k
        value = v @ w_v.T + b_v
        query = query.reshape(b, s, H, D_K).transpose(0, 2, 1, 3)
        key_ = key_.reshape(b, -1, H, D_K).transpose(0, 2, 1, 3)
        value = value.reshape(b, -1, H, D_K).transpose(0, 2, 1, 3)
        scores = jnp.einsum('bhqd,bhkd->bhqk', query, key_) / jnp.sqrt(jnp.float32(D_K))
        scores = jnp.where(mask == 0, jnp.float32(-1000000000.0), scores)
        attn = jax.nn.softmax(scores, axis=-1)
        out = jnp.einsum('bhqk,bhkd->bhqd', attn, value)
        out = out.transpose(0, 2, 1, 3).reshape(b, s, D_MODEL)
        return out @ w_o.T + b_o

    def _L1_ffn_ref(x, W_qkv, b_qkv, W_gate, b_gate, W_experts, b_experts):
        import jax, jax.numpy as jnp
        import numpy as np
        NUM_HEADS = 16
        TOP_K = 2
        B, S, D = x.shape
        H = NUM_HEADS
        hd = D // H
        E = W_gate.shape[-1]
        qkv = (x @ W_qkv + b_qkv).reshape(B, S, 3, H, hd)
        q, k, v = (qkv[:, :, 0], qkv[:, :, 1], qkv[:, :, 2])
        attn = jnp.einsum('bqhd,bkhd->bhqk', q, k) / jnp.sqrt(jnp.asarray(hd, x.dtype))
        attn = jax.nn.softmax(attn, axis=-1)
        attn_out = jnp.einsum('bhqk,bkhd->bqhd', attn, v).reshape(B, S, D)
        gate = jax.nn.softmax(x @ W_gate + b_gate, axis=-1)
        top_g, top_i = jax.lax.top_k(gate, TOP_K)
        combine = jnp.sum(jax.nn.one_hot(top_i, E, dtype=x.dtype) * top_g[..., None], axis=2)
        expert_out = jnp.einsum('bsd,edf->bsef', x, W_experts) + b_experts
        moe_out = jnp.einsum('bsef,bse->bsf', expert_out, combine)
        return attn_out + moe_out

    def _L2_xattn_ref(q, k, v, W_proj, b_proj):
        import jax, jax.numpy as jnp
        import numpy as np
        B, T, N_EMBD, N_HEAD = (2, 256, 128, 16)
        HEAD = N_EMBD // N_HEAD
        WINDOW = 64
        Bsz, Tlen, _ = q.shape
        qh = q.reshape(Bsz, Tlen, N_HEAD, HEAD).transpose(0, 2, 1, 3)
        kh = k.reshape(Bsz, Tlen, N_HEAD, HEAD).transpose(0, 2, 1, 3)
        vh = v.reshape(Bsz, Tlen, N_HEAD, HEAD).transpose(0, 2, 1, 3)
        scale = 1.0 / np.sqrt(HEAD)
        scores = jnp.einsum('bhqd,bhkd->bhqk', qh, kh) * scale
        idx = jnp.arange(Tlen)
        dist = jnp.abs(idx[None, :] - idx[:, None])
        scores = jnp.where(dist[None, None] > WINDOW, -jnp.inf, scores)
        attn = jax.nn.softmax(scores, axis=-1)
        y = jnp.einsum('bhqk,bhkd->bhqd', attn, vh)
        y = y.transpose(0, 2, 1, 3).reshape(Bsz, Tlen, N_EMBD)
        return y @ W_proj.T + b_proj

    def _L2_ffn_ref(hidden_states, router_w1, router_w2, w1, w2, w3):
        import jax, jax.numpy as jnp
        import numpy as np
        import math
        B, S, D = (4, 256, 128)
        E, DFF = (16, 256)
        CAP_FACTOR = 2.0
        ROUTER_HIDDEN = 128
        CAPACITY = int(math.ceil(S * CAP_FACTOR / E))
        b, s, d = hidden_states.shape
        e = w1.shape[0]
        cap = CAPACITY
        router_logits = jax.nn.silu(hidden_states @ router_w1) @ router_w2
        expert_probs = jax.nn.softmax(router_logits.transpose(0, 2, 1), axis=-1)
        expert_weights, token_indices = jax.lax.top_k(expert_probs, cap)
        expert_weights = expert_weights / (expert_weights.sum(-1, keepdims=True) + 1e-09)
        expert_inputs = jax.vmap(lambda h, i: h[i])(hidden_states, token_indices)
        gate = jax.nn.silu(jnp.einsum('becd,edf->becf', expert_inputs, w1))
        value = jnp.einsum('becd,edf->becf', expert_inputs, w2)
        expert_out = jnp.einsum('becf,efd->becd', gate * value, w3)
        weighted = expert_out * expert_weights[..., None]

        def combine(idx, vals):
            return jnp.zeros((s, d), vals.dtype).at[idx.reshape(-1)].add(vals.reshape(-1, d))
        output = jax.vmap(combine)(token_indices, weighted)
        return output

    def _L3_xattn_ref(key, value):
        import jax, jax.numpy as jnp
        import numpy as np
        B, T, D = (8, 256, 128)
        d = key.shape[-1]
        scale = 1.0 / jnp.sqrt(jnp.asarray(d, dtype=key.dtype))
        att_weights = jnp.einsum('btd,bsd->bts', key, value) * scale
        att_probs = jax.nn.softmax(att_weights, axis=-1)
        att_outputs = jnp.einsum('bts,bsd->btd', att_probs, value)
        return att_outputs

    def _L3_ffn_ref(x, norm_scale, gate_w, gate_b, mlp1_w, mlp1_b, mlp2_w, mlp2_b):
        import jax, jax.numpy as jnp
        import numpy as np
        B, S, D = (1, 256, 128)
        I = 256
        E = 8
        K = 2
        LIMIT = 7.0
        ALPHA = 1.702
        EPS = 1e-05

        def _swiglu(h):
            x_glu = jnp.minimum(h[..., ::2], LIMIT)
            x_lin = jnp.clip(h[..., 1::2], -LIMIT, LIMIT)
            return x_glu * jax.nn.sigmoid(ALPHA * x_glu) * (x_lin + 1.0)

        def _moe(t, gate_w, gate_b, mlp1_w, mlp1_b, mlp2_w, mlp2_b):
            T = t.shape[0]
            logits = t @ gate_w + gate_b
            top_v, top_i = jax.lax.top_k(logits, K)
            probs = jax.nn.softmax(top_v, axis=-1)
            w = jnp.zeros((T, E), t.dtype).at[jnp.arange(T)[:, None], top_i].set(probs)

            def body(acc, ew):
                w1, b1, w2, b2, we = ew
                h = _swiglu(t @ w1 + b1)
                y = h @ w2 + b2
                return (acc + we[:, None] * y, None)
            acc0 = jnp.zeros((T, t.shape[1]), t.dtype)
            acc, _ = jax.lax.scan(body, acc0, (mlp1_w, mlp1_b, mlp2_w, mlp2_b, w.T))
            return acc
        Bx, Sx, Dx = x.shape
        ms = jnp.mean(x * x, axis=-1, keepdims=True)
        t = (x * jax.lax.rsqrt(ms + EPS) * norm_scale).reshape(Bx * Sx, Dx)
        y = _moe(t, gate_w, gate_b, mlp1_w, mlp1_b, mlp2_w, mlp2_b)
        return x + y.reshape(Bx, Sx, Dx)
    x = x + jnp.tanh(g_xattn[0]) * _L0_xattn_ref(_layernorm(x, axis=-1), ctx_1024, ctx_1024, mask_1x1xSxS2_ik0, L0_xattn_w_q, L0_xattn_b_q, L0_xattn_w_k, L0_xattn_b_k, L0_xattn_w_v, L0_xattn_b_v, L0_xattn_w_o, L0_xattn_b_o)
    x = x + jnp.tanh(g_ffn[0]) * _L0_ffn_ref(_layernorm(x, axis=-1), L0_ffn_gate_w, L0_ffn_gate_up_proj, L0_ffn_down_proj)
    x = x + jnp.tanh(g_xattn[1]) * _L1_xattn_ref(_layernorm(x, axis=-1), ctx_1024, ctx_1024, mask_1x1xSxS2_ik0, L1_xattn_w_q, L1_xattn_b_q, L1_xattn_w_k, L1_xattn_b_k, L1_xattn_w_v, L1_xattn_b_v, L1_xattn_w_o, L1_xattn_b_o)
    x = x + jnp.tanh(g_ffn[1]) * _L1_ffn_ref(_layernorm(x, axis=-1), L1_ffn_W_qkv, L1_ffn_b_qkv, L1_ffn_W_gate, L1_ffn_b_gate, L1_ffn_W_experts, L1_ffn_b_experts)
    x = x + jnp.tanh(g_xattn[2]) * _L2_xattn_ref(_layernorm(x, axis=-1), ctx_1024, ctx_1024, L2_xattn_W_proj, L2_xattn_b_proj)
    x = x + jnp.tanh(g_ffn[2]) * _L2_ffn_ref(_layernorm(x, axis=-1), L2_ffn_router_w1, L2_ffn_router_w2, L2_ffn_w1, L2_ffn_w2, L2_ffn_w3)
    x = x + jnp.tanh(g_xattn[3]) * _L3_xattn_ref(_layernorm(x, axis=-1), ctx_1024)
    x = x + jnp.tanh(g_ffn[3]) * _L3_ffn_ref(_layernorm(x, axis=-1), L3_ffn_norm_scale, L3_ffn_gate_w, L3_ffn_gate_b, L3_ffn_mlp1_w, L3_ffn_mlp1_b, L3_ffn_mlp2_w, L3_ffn_mlp2_b)
    return x

_drawn_inputs = setup_inputs


def setup_inputs(seed=0):
    import zlib

    import numpy as np

    out = dict(_drawn_inputs(seed))
    spreads = {'L0_xattn_b_q': (0.0, 0.438),
     'L0_xattn_b_k': (0.0, 0.8),
     'L0_xattn_b_v': (0.0, 0.1),
     'L0_xattn_b_o': (0.0, 0.1),
     'L1_ffn_b_qkv': (0.0, 0.1),
     'L1_ffn_b_gate': (0.0, 0.336),
     'L1_ffn_b_experts': (0.0, 0.53),
     'L2_xattn_b_proj': (0.0, 0.1),
     'L3_ffn_norm_scale': (1.0, 0.6),
     'L3_ffn_gate_b': (0.0, 0.4),
     'L3_ffn_mlp1_b': (0.0, 0.8),
     'L3_ffn_mlp2_b': (0.0, 2.0)}
    factors = {'g_ffn': 27.272,
     'L0_ffn_gate_w': 8.0,
     'L0_ffn_gate_up_proj': 8.0,
     'L0_ffn_down_proj': 8.0,
     'L1_xattn_b_q': 2.751,
     'L1_xattn_b_k': 64.0,
     'L2_ffn_router_w1': 8.0,
     'L2_ffn_router_w2': 8.0,
     'L2_ffn_w1': 8.0,
     'L2_ffn_w2': 8.0,
     'L2_ffn_w3': 8.0,
     'L3_ffn_mlp1_w': 4.971,
     'L3_ffn_mlp2_w': 4.496}
    for name, (base, spread) in spreads.items():
        noise = np.random.default_rng([zlib.crc32(name.encode()), seed]).standard_normal(out[name].shape)
        drawn = base * np.exp(spread * noise) if base else spread * noise
        out[name] = jnp.asarray(drawn.astype(out[name].dtype))
    for name, factor in factors.items():
        out[name] = (out[name] * factor).astype(out[name].dtype)
    return out
```

```python
from contextlib import ExitStack

import numpy as np

import concourse.bass as bass
from concourse import mybir

ALU = mybir.AluOpType
ACT = mybir.ActivationFunctionType
AX = mybir.AxisListType.X
F32 = mybir.dt.float32
BF16 = mybir.dt.bfloat16
I32 = mybir.dt.int32

P = 128
B, S, D = 16, 64, 128
T = B * S
NT = T // P
HALF = T // 2
H, DK = 16, 8
PAIR = H // 2
VW = 2 * DK + 1
QUAD = PAIR // 2
VB = QUAD * 2 * VW
BIG = float(2 ** 30)
LN_EPS = 1e-5

MHA_GATE = (0, 1, 5, 2)
NM = len(MHA_GATE)
FFN_E = (8, 16, 8)
FFN_C = (1, 2, 2)
FFN_DMA = (2, 3, 2)
FFN_LN = (1, 5, 7)
TOP_C = 32

C_ID, C_ROT, C_DUP, C_PM, C_JM, C_COS, C_SIN, C_TRI = 0, 128, 256, 384, 392, 394, 458, 522
C_N = 586


def shape_constants():
    c = np.zeros((P, C_N), np.float32)
    c[:, C_ID:C_ID + P] = np.eye(P)
    for h in range(H):
        for j in range(DK // 2):
            c[h * DK + 2 * j + 1, C_ROT + h * DK + j] = -1.0
            c[h * DK + 2 * j, C_ROT + h * DK + DK // 2 + j] = 1.0
    for q in range(S):
        c[q, C_DUP + q] = c[q, C_DUP + S + q] = 1.0
    rows = np.arange(P)
    for pair in range(PAIR):
        c[:, C_PM + pair] = rows // (2 * DK) == pair
    for j2 in range(2):
        c[:, C_JM + j2] = ((rows // DK) % 2 == j2) / np.sqrt(np.float32(DK))
    inv = (1.0 / 10000.0 ** (np.arange(0, DK, 2, dtype=np.float32) / DK)).astype(np.float32)
    ang = np.arange(S, dtype=np.float32)[:, None] * inv[None, :]
    ang = np.concatenate([ang, ang], axis=-1).astype(np.float32)
    c[:, C_COS:C_COS + S] = np.cos(ang).T[rows % DK]
    c[:, C_SIN:C_SIN + S] = np.sin(ang).T[rows % DK]
    c[:, C_TRI:C_TRI + 64] = np.tril(np.ones((8, 8)), -1).reshape(1, 64)
    return c


def ffn_states():
    out_, pairs, experts, dmas = [], 0, 0, 0
    for f in range(3):
        out_.append((pairs, experts, dmas))
        pairs += 2 * FFN_E[f] * FFN_C[f]
        experts += FFN_E[f]
        dmas += 16 * FFN_DMA[f] * FFN_E[f] // 2
    return out_


def after(eng, sem, value):
    if not (isinstance(value, int) and value <= 0):
        eng.wait_ge(sem, value)


def build(nc, a, out, stop=99):
    with ExitStack() as ctx:
        def sb(name, shape, dt=F32):
            return ctx.enter_context(nc.sbuf_tensor(name, shape, dt))

        def sem(name):
            return ctx.enter_context(nc.semaphore(name))

        bank = [ctx.enter_context(nc.psum_tensor(f"bank{i}", [P, 512], F32)) for i in range(8)]

        const = sb("const", [P, C_N])
        ident = const[:, C_ID:C_ID + P]
        dup_bf = sb("dup_bf", [P, P], BF16)
        x_tok = sb("x_tok", [P, NT, D])
        x_norm = sb("x_norm", [P, NT, D])
        x_rms = sb("x_rms", [P, NT, D])
        xT = sb("xT", [P, T])
        stats = sb("stats", [P, NT, 6])
        mv = sb("mv", [P, NT, 2])
        var_eps = sb("var_eps", [P, NT])
        rstd = sb("rstd", [P, NT])
        minus_half = sb("minus_half", [P, NT])
        ctx_tok = sb("ctx_tok", [P, NT, D + 1])
        ctx_dup = sb("ctx_dup", [P, B, D])
        ctxT = sb("ctxT", [P, T])
        gates = sb("gates", [P, 8])
        biases = sb("biases", [P, 10])
        bq0, bk0, bq1, bk1, bqs, bks, rq0, rk0 = (biases[:, i:i + 1] for i in range(8))
        v_bias = sb("v_bias", [P, 3, D])
        w_raw = sb("w_raw", [P, 9, D])
        wT = sb("wT", [P, 8, D])
        wo_by_j2 = sb("wo_by_j2", [P, NM, 2, 64])
        w_qkv = sb("w_qkv", [P, 3 * D])
        w_out = sb("w_out", [65, NM, 2, D])
        bo_row = sb("bo_row", [65, 3, D])
        mask_i = sb("mask_i", [P, S], I32)
        mask_open = sb("mask_open", [P, S])
        row_open = sb("row_open", [P, 1])
        mask_low = sb("mask_low", [P, S], BF16)
        q_scale = sb("q_scale", [P, 2, 2, S])
        kT = sb("kT", [P, 3, T])
        qT = sb("qT", [P, T])
        rot_tmp = sb("rot_tmp", [P, HALF])
        v_blk = sb("v_blk", [P, NM, B, VB])
        q_blk = sb("q_blk", [P, 2, 2, S])
        k_blk = sb("k_blk", [P, 2, PAIR, S])
        row_max = sb("row_max", [P, 2, PAIR])
        shifted = sb("shifted", [P, 2, PAIR, S])
        probs = sb("probs", [P, 2, PAIR, S])
        probsT = sb("probsT", [P, 2, QUAD, P])
        inv_sum = sb("inv_sum", [P, 2, PAIR])
        o_norm = sb("o_norm", [P, 2, 2, PAIR, DK])
        oT = sb("oT", [65, 2, P])
        gate_raw = sb("gate_raw", [8, D])
        gate_w = sb("gate_w", [P, 3, 8])
        gate_b = sb("gate_b", [P, 2, 8])
        logits = sb("logits", [P, NT, 8])
        gt = sb("gt", [P, NT, 8, 8])
        eq = sb("eq", [P, NT, 8, 8])
        rank = sb("rank", [P, NT, 8])
        top = sb("top", [P, NT, 8])
        e_max = sb("e_max", [P, NT])
        e_sum = sb("e_sum", [P, NT])
        comb = sb("comb", [P, NT, 16])
        combT = sb("combT", [8, T])
        we1 = sb("we1", [P, 8, D])
        be = sb("be", [8, 2, D])
        b1_raw = sb("b1_raw", [8, 512])
        b1_col = sb("b1_col", [P, 2, 2, 8])
        ns_row = sb("ns_row", [P, D])
        w_up = sb("w_up", [P, 2, 512])
        w_dn = sb("w_dn", [P, 2, 2, D])
        act_out = sb("act_out", [P, 2, HALF])
        glu = sb("glu", [P, 2, HALF])
        gated = sb("gated", [P, 2, HALF])
        lin = sb("lin", [P, 2, HALF])
        hid = sb("hid", [P, 2, 2, HALF])
        rw1 = sb("rw1", [P, D])
        rw2 = sb("rw2", [P, 16])
        rw2_pad = sb("rw2_pad", [P, 8, P])
        r1 = sb("r1", [P, T])
        rp = sb("rp", [P, 2, S])
        rwork = sb("rwork", [P, 2, S])
        rtop = sb("rtop", [P, 2, 8])
        rsel = sb("rsel", [P, 2, 2, S])
        rcol = sb("rcol", [P, 2])
        s3 = sb("s3", [P, NT, S])
        p3 = sb("p3", [P, NT, P])
        p3T = sb("p3T", [P, NT, P])
        m3 = sb("m3", [P, NT])

        ld_const, ld_x, ld_ctx, ld_w, ld_small, ld_late = (sem(n) for n in (
            "const_loaded", "x_loaded", "ctx_loaded", "proj_loaded", "small_loaded", "late_loaded"))
        dve_done, pool_done, act_done = sem("dve_step_done"), sem("pool_step_done"), sem("act_step_done")
        gates_ready, consts_set = sem("gates_ready"), sem("consts_set")
        ctxT_psum, ctxT_ready = sem("ctxT_psum"), sem("ctxT_ready")
        wT_psum, wT_ready = sem("wT_psum"), sem("wT_ready")
        wo_psum, wo_ready = sem("wo_psum"), sem("wo_ready")
        rb_psum, rb_ready = sem("rot_bias_psum"), sem("rot_bias_ready")
        mask_ready, ro_psum, q_scale_ready = sem("mask_ready"), sem("row_open_psum"), sem("q_scale_ready")
        gw_psum, gw_ready = sem("gate_w_psum"), sem("gate_w_ready")
        b1_psum, b1_ready = sem("b1_psum"), sem("b1_ready")
        proj_psum, proj_ready = sem("proj_psum"), sem("proj_ready")
        v_psum, v_ready = sem("v_psum"), sem("v_ready")
        mv_ready, rstd_ready, xn_ready = sem("mv_ready"), sem("rstd_ready"), sem("xn_ready")
        xT_psum, xT_ready = sem("xT_psum"), sem("xT_ready")
        blocks_ready, scores_done, max_ready, shift_ready = (sem(n) for n in (
            "blocks_ready", "scores_done", "max_ready", "shift_ready"))
        exp_done, pT_psum, pT_ready, pv_done = (sem(n) for n in ("exp_done", "pT_psum", "pT_ready", "pv_done"))
        inv_ready, on_ready, oT_psum, oT_ready, y_psum, x_added = (sem(n) for n in (
            "inv_ready", "on_ready", "oT_psum", "oT_ready", "y_psum", "x_added"))
        logit_psum, comb_ready = sem("logit_psum"), sem("comb_ready")
        combT_psum, combT_ready, be_psum, be_added = (sem(n) for n in (
            "combT_psum", "combT_ready", "be_psum", "be_added"))
        e1_psum, e1_added = sem("expert1_psum"), sem("expert1_added")
        w_loaded = [sem("even_expert_loaded"), sem("odd_expert_loaded")]
        up_psum, up_free, act_ready, h_ready, down_psum, down_added = (sem(n) for n in (
            "up_psum", "up_free", "act_ready", "h_ready", "down_psum", "down_added"))
        glu_ready, gated_ready = sem("glu_ready"), sem("gated_ready")
        pad_ready, r1_psum, r1_ready, r2_psum, rsel_ready, rT_psum = (sem(n) for n in (
            "pad_ready", "r1_psum", "r1_ready", "r2_psum", "rsel_ready", "rT_psum"))
        s3_psum, s3_ready, p3_ready, p3T_psum, p3T_ready, o3_psum = (sem(n) for n in (
            "s3_psum", "s3_ready", "p3_ready", "p3T_psum", "p3T_ready", "o3_psum"))
        dve_to_act, act_to_dve = sem("shifted_logits_ready"), sem("exp_logits_ready")
        wo_split = sem("wo_split")
        v3_ready = sem("context_values_ready")
        x_final, stored = sem("x_final"), sem("stored")

        block = ctx.enter_context(nc.Block())

        def tok(ap, p=P):
            return ap.rearrange("b s d -> (b s) d").rearrange("(t p) d -> p t d", p=p)

        @block.sync
        def _(sp):
            sp.dma_start(x_tok[:, :, :], tok(a["x"])).then_inc(ld_x, 16)
            sp.dma_start(const[:, :], a["shape_constants"]).then_inc(ld_const, 16)
            sp.dma_start(ctx_tok[:, :, 0:D], tok(a["ctx_1024"])).then_inc(ld_ctx, 16)
            for half in range(2):
                sp.dma_start(ctx_dup[half * S:(half + 1) * S, :, :],
                             a["ctx_1024"].rearrange("b s d -> s b d")).then_inc(ld_ctx, 16)
            for i, n in enumerate(("L0_xattn_w_q", "L0_xattn_w_k", "L0_xattn_w_v", "L0_xattn_w_o", "L1_xattn_w_q",
                                   "L1_xattn_w_k", "L1_xattn_w_v", "L1_xattn_w_o", "L2_xattn_W_proj")):
                sp.dma_start(w_raw[:, i, :], a[n]).then_inc(ld_w, 16)
            expert = 0
            loaded = [0, 0]
            for f in range(3):
                def load(e, slot, counted):
                    after(sp, down_psum, 2 * (counted + e) - 2)
                    up, dn = w_up[:, slot, :], w_dn[:, slot, :, :]
                    if f == 0:
                        sp.dma_start(up[:, 0:2 * D], a["L0_ffn_gate_up_proj"][e, :, :]).then_inc(w_loaded[slot], 16)
                        sp.dma_start(dn[:, 0, :], a["L0_ffn_down_proj"][e, :, :]).then_inc(w_loaded[slot], 16)
                    if f == 1:
                        sp.dma_start(up[:, 0:256], a["L2_ffn_w1"][e, :, :]).then_inc(w_loaded[slot], 16)
                        sp.dma_start(up[:, 256:512], a["L2_ffn_w2"][e, :, :]).then_inc(w_loaded[slot], 16)
                        sp.dma_start(dn, a["L2_ffn_w3"][e, :, :].rearrange("(c p) d -> p c d", p=P))\
                            .then_inc(w_loaded[slot], 16)
                    if f == 2:
                        sp.dma_start(up, a["L3_ffn_mlp1_w"][e, :, :]).then_inc(w_loaded[slot], 16)
                        sp.dma_start(dn, a["L3_ffn_mlp2_w"][e, :, :].rearrange("(c p) d -> p c d", p=P))\
                            .then_inc(w_loaded[slot], 16)

                load(0, 0, expert)
                load(1, 1, expert)
                with sp.Fori(1, FFN_E[f] // 2) as ep:
                    load(2 * ep, 0, expert)
                    load(2 * ep + 1, 1, expert)
                expert += FFN_E[f]
            sp.wait_ge(x_final, 1)
            sp.dma_start(tok(out), x_tok[:, :, :]).then_inc(stored, 16)
            sp.wait_ge(stored, 16)

        @block.tensor
        def _(pe):
            def mm(o, l, r, start=True, stop=True):
                return nc.tensor.matmul(o, l, r, start=start, stop=stop)

            def transposes_of_x(n, src):
                for half in range(2):
                    pe.wait_ge(xn_ready, NT * n + 4 * half + 4)
                    for i in range(4):
                        last = nc.tensor.transpose(bank[6 + half][:, i * P:(i + 1) * P], src[:, 4 * half + i, :], ident)
                    last.then_inc(xT_psum, 1)

            pe.wait_ge(ld_const, 16)
            pe.wait_ge(ld_ctx, 48)
            for half in range(2):
                for i in range(4):
                    last = nc.tensor.transpose(bank[half][:, i * P:(i + 1) * P], ctx_tok[:, 4 * half + i, 0:D], ident)
                last.then_inc(ctxT_psum, 1)
            pe.wait_ge(ld_w, 16 * 9)
            for i, (w, rotated) in enumerate(((0, 0), (1, 0), (2, 0), (0, 1), (1, 1), (4, 0), (5, 0), (6, 0))):
                o = bank[2 + i // 4][:, (i % 4) * P:(i % 4 + 1) * P]
                if rotated:
                    last = mm(o, w_raw[:, w, :], const[:, C_ROT:C_ROT + P])
                else:
                    last = nc.tensor.transpose(o, w_raw[:, w, :], ident)
                if i % 4 == 3:
                    last.then_inc(wT_psum, 1)
            pe.wait_ge(wo_split, 1)
            for m in range(NM):
                for j2 in range(2):
                    last = nc.tensor.transpose(bank[4 + m // 2][0:64, ((m % 2) * 2 + j2) * P:((m % 2) * 2 + j2 + 1) * P],
                                               wo_by_j2[:, m, j2, :], ident)
            last.then_inc(wo_psum, 1)
            pe.wait_ge(ld_small, 16 * 14)
            for i in range(2):
                last = mm(bank[6][:, i:i + 1], const[:, C_ROT:C_ROT + P], biases[:, i:i + 1])
            last.then_inc(rb_psum, 1)
            pe.wait_ge(mask_ready, 1)
            pe.wait_ge(rb_ready, 1)
            mm(bank[6][:, 64:128], row_open[0:S, :].broadcast_to([S, P]), const[0:S, C_ID:C_ID + S]).then_inc(ro_psum, 1)
            pe.wait_ge(ld_late, 16 * 15)
            nc.tensor.transpose(bank[7][:, 0:8], gate_raw[:, :], const[0:8, C_ID:C_ID + 8]).then_inc(gw_psum, 1)
            pe.wait_ge(gw_ready, 1)
            for c in range(2):
                for k in range(2):
                    last = nc.tensor.transpose(bank[7][:, 16 + (2 * c + k) * 8:24 + (2 * c + k) * 8],
                                               b1_raw[:, 256 * c + k:256 * c + 256:2], const[0:8, C_ID:C_ID + 8])
            last.then_inc(b1_psum, 1)

            count = [0]

            def project(w, src, half):
                n = count[0]
                after(pe, proj_ready, n - 3)
                mm(bank[n % 4][:, :], w, src[:, half * HALF:(half + 1) * HALF]).then_inc(proj_psum, 1)
                count[0] += 1

            vcount = [0]

            def values(w, src):
                for g in range(4):
                    n = vcount[0]
                    after(pe, v_ready, n - 1)
                    for i in range(4):
                        o, first = bank[4 + n % 2][:, i * P:(i + 1) * P], (4 * g + i) * S
                        if first + P <= T:
                            last = mm(o, src[:, first:first + P], w)
                        else:
                            mm(o[0:S, :], src[:, first:first + S], w)
                            last = mm(o[S:P, :], src[:, 0:S], w)
                    last.then_inc(v_psum, 1)
                    vcount[0] += 1

            pe.wait_ge(ctxT_ready, 2)
            pe.wait_ge(wT_ready, 2)
            for half in range(2):
                project(wT[:, 1, :], ctxT, half)
                project(wT[:, 4, :], ctxT, half)
            for half in range(2):
                project(wT[:, 6, :], ctxT, half)
            pe.wait_ge(wo_ready, 2)
            values(wT[:, 2, :], ctxT)
            values(wT[:, 7, :], ctxT)
            pe.wait_ge(q_scale_ready, 1)
            pe.wait_ge(b1_ready, 1)

            def mha(m):
                pe.wait_ge(proj_ready, count[0])
                pe.wait_ge(v_ready, vcount[0])
                if m == 3:
                    pe.wait_ge(v3_ready, 2)

                def step(b, s, steady, tile_live):
                    gb = B * m + b

                    def live(lag):
                        return steady or 0 <= b - lag < B
                    if live(0):
                        pe.wait_ge(blocks_ready, 2 * gb + 2)
                        after(pe, shift_ready, gb - 1)
                        if m < 2:
                            mm(bank[s][:, :], dup_bf[:, :], mask_low[:, :].unsqueeze(1).broadcast_to([P, PAIR, S]),
                               stop=False)
                        mm(bank[s][:, :], q_blk[:, s, :, :], k_blk[:, s, :, :], start=m >= 2).then_inc(scores_done, 1)
                    if live(1):
                        u = 1 - s
                        pe.wait_ge(exp_done, gb)
                        after(pe, pT_ready, gb - 2)
                        for i in range(QUAD):
                            last = nc.tensor.transpose(bank[2 + u][:, i * P:(i + 1) * P],
                                                       probs[:, u, 2 * i:2 * i + 2, :], ident)
                        last.then_inc(pT_psum, 1)
                    if live(2):
                        pe.wait_ge(pT_ready, gb - 1)
                        after(pe, on_ready, gb - 3)
                        v = v_blk[:, m, b - 2, :].rearrange("p (i c) -> p i c", i=QUAD)
                        for i in range(QUAD):
                            last = mm(bank[4 + s][:, i * 2 * VW:(i + 1) * 2 * VW], probsT[:, s, i, :], v[:, i, :])
                        last.then_inc(pv_done, 1)
                    if live(3):
                        u = 1 - s
                        pe.wait_ge(on_ready, gb - 2)
                        after(pe, oT_ready, gb - 3)
                        nc.tensor.transpose(bank[6][:, u * P:(u + 1) * P], o_norm[:, u, :, :, :], ident)\
                            .then_inc(oT_psum, 1)
                    if s == 1 and tile_live:
                        pe.wait_ge(oT_ready, gb - 3)
                        after(pe, x_added, gy(b))
                        mm(bank[7][:, 0:D], oT[:, 0, :], w_out[:, m, 0, :], stop=False)
                        mm(bank[7][:, 0:D], oT[:, 1, :], w_out[:, m, 1, :], start=False).then_inc(y_psum, 1)

                def gy(b):
                    return tau_of[0] - 2 + NT * m
                tau_of = [0]
                for tau in (0, 1, 2):
                    tau_of[0] = tau
                    for s in range(2):
                        step(2 * tau + s, s, False, tau >= 2)
                with pe.Fori(3, NT) as tau:
                    tau_of[0] = tau
                    for s in range(2):
                        step(2 * tau + s, s, True, True)
                for tau in (NT, NT + 1):
                    tau_of[0] = tau
                    for s in range(2):
                        step(2 * tau + s, s, False, True)

            def router(i, w):
                for t in range(NT):
                    last = mm(bank[0][:, t * 8:(t + 1) * 8], xT[:, t * P:(t + 1) * P], w)
                last.then_inc(logit_psum, 1)

            def expert_biases(i):
                pe.wait_ge(comb_ready, (0, 2, 4)[i])
                for t in range(NT):
                    last = nc.tensor.transpose(bank[4 + t // 4][0:8, (t % 4) * P:(t % 4 + 1) * P], comb[:, t, 0:8], ident)
                last.then_inc(combT_psum, 1)
                pe.wait_ge(combT_ready, i)
                for t in range(NT):
                    last = mm(bank[6 + t // 4][:, (t % 4) * D:(t % 4 + 1) * D], combT[:, t * P:(t + 1) * P], be[:, i - 1, :])
                last.then_inc(be_psum, 1)

            def ffn(f, state):
                chunks = FFN_C[f]
                pair0, exp0, dma0 = state

                def up(e, k):
                    slot, half = k // 2, k % 2
                    if half == 0:
                        pe.wait_ge(w_loaded[slot], dma0 + 16 * FFN_DMA[f] * (e + 1))
                    for c in range(chunks):
                        n = (4 * e + k) * chunks + c
                        if f < 2:
                            after(pe, h_ready, pair0 + n - 1)
                        else:
                            after(pe, up_free, n - 1)
                        pb = 2 * ((k * chunks + c) % 2)
                        w = w_up[:, slot, :]
                        g, u = {0: (w[:, 0:128], w[:, 128:256]),
                                1: (w[:, c * 128:c * 128 + 128], w[:, 256 + c * 128:384 + c * 128]),
                                2: (w[:, 256 * c:256 * c + 256:2], w[:, 256 * c + 1:256 * c + 256:2])}[f]
                        src = xT[:, half * HALF:(half + 1) * HALF]
                        mm(bank[pb][:, :], g, src)
                        mm(bank[pb + 1][:, :], u, src).then_inc(up_psum, 1)

                def down(e, k, n_step):
                    pe.wait_ge(h_ready, pair0 + (4 * e + k + 1) * chunks)
                    after(pe, down_added, n_step - 1)
                    slot, y = k // 2, bank[4 + k % 2]
                    for i in range(4):
                        for c in range(chunks):
                            last = mm(y[:, i * D:(i + 1) * D], hid[:, k % 2, c, i * P:(i + 1) * P], w_dn[:, slot, c, :],
                                      start=c == 0, stop=c == chunks - 1)
                    last.then_inc(down_psum, 1)

                def body(e, first):
                    for k in range(4):
                        up(e, k)
                        if k > 0:
                            down(e, k - 1, 2 * exp0 + 4 * e + k - 1)
                        elif not first:
                            down(e - 1, 3, 2 * exp0 + 4 * e - 1)

                body(0, True)
                with pe.Fori(1, FFN_E[f] // 2) as e:
                    body(e, False)
                last_e = FFN_E[f] // 2 - 1
                down(last_e, 3, 2 * exp0 + 4 * last_e + 3)

            states = ffn_states()
            transposes_of_x(0, x_norm)
            pe.wait_ge(xT_ready, 2)
            for half in range(2):
                project(wT[:, 0, :], xT, half)
                project(wT[:, 3, :], xT, half)
            mha(0)
            if stop <= 1:
                return
            transposes_of_x(1, x_norm)
            pe.wait_ge(xT_ready, 4)
            router(0, gate_w[:, 0, :])
            pe.wait_ge(comb_ready, 1)
            ffn(0, states[0])
            if stop <= 2:
                return
            transposes_of_x(2, x_norm)
            pe.wait_ge(xT_ready, 6)
            for half in range(2):
                project(wT[:, 5, :], xT, half)
            mha(1)
            if stop <= 3:
                return
            transposes_of_x(3, x_norm)
            pe.wait_ge(xT_ready, 8)
            for half in range(2):
                project(w_qkv[:, 0:D], xT, half)
                project(w_qkv[:, D:2 * D], xT, half)
            values(w_qkv[:, 2 * D:3 * D], xT)
            mha(2)
            pe.wait_ge(x_added, 3 * NT)
            router(1, gate_w[:, 1, :])
            expert_biases(1)
            for t in range(NT):
                after(pe, e1_added, t - 1)
                for g in range(2):
                    last = mm(bank[2 * (t % 2) + g][:, :], xT[:, t * P:(t + 1) * P], we1[:, 4 * g:4 * g + 4, :])
                last.then_inc(e1_psum, 1)
            if stop <= 4:
                return
            transposes_of_x(4, x_norm)
            mha(3)
            if stop <= 5:
                return
            transposes_of_x(5, x_norm)
            pe.wait_ge(xT_ready, 12)
            for half in range(2):
                mm(bank[half][:, :], rw1[:, :], xT[:, half * HALF:(half + 1) * HALF]).then_inc(r1_psum, 1)
            pe.wait_ge(pad_ready, 8)
            pe.wait_ge(r1_ready, 2)
            for hf in range(2):
                for i in range(8):
                    last = mm(bank[2][:, hf * S:(hf + 1) * S], rw2_pad[:, i, :], r1[:, (8 * hf + i) * S:(8 * hf + i + 1) * S],
                              start=i == 0, stop=i == 7)
            last.then_inc(r2_psum, 1)
            pe.wait_ge(rsel_ready, 1)
            for hf in range(2):
                last = nc.tensor.transpose(bank[3][:, hf * P:(hf + 1) * P], rsel[:, hf, :, :], ident)
            last.then_inc(rT_psum, 1)
            pe.wait_ge(comb_ready, 3)
            ffn(1, states[1])
            if stop <= 6:
                return
            transposes_of_x(6, x_norm)
            pe.wait_ge(xT_ready, 14)
            for t in range(NT):
                last = mm(bank[t // 4][:, (t % 4) * P:(t % 4 + 1) * P], xT[:, t * P:(t + 1) * P],
                          ctxT[:, t * P:(t + 1) * P])
                if t % 4 == 3:
                    last.then_inc(s3_psum, 1)
            for g in range(2):
                pe.wait_ge(p3_ready, g + 1)
                for i in range(4):
                    last = nc.tensor.transpose(bank[2 + g][:, i * P:(i + 1) * P], p3[:, 4 * g + i, :], ident)
                last.then_inc(p3T_psum, 1)
            for t in range(NT):
                pe.wait_ge(p3T_ready, t // 4 + 1)
                last = mm(bank[4 + t // 3][:, (t % 3) * (D + 1):(t % 3 + 1) * (D + 1)], p3T[:, t, :], ctx_tok[:, t, :])
                if t % 3 == 2 or t == NT - 1:
                    last.then_inc(o3_psum, 1)
            if stop <= 7:
                return
            transposes_of_x(7, x_rms)
            pe.wait_ge(xT_ready, 16)
            router(2, gate_w[:, 2, :])
            expert_biases(2)
            pe.wait_ge(be_added, 2)
            ffn(2, states[2])

        @block.scalar
        def _(act):
            done = [0]

            def link(ins):
                done[0] += 1
                ins.then_inc(act_done, 1)
                act.wait_ge(act_done, done[0])

            def column(i, ap):
                act.dma_start(biases[:, i:i + 1], ap.rearrange("(p o) -> p o", o=1)).then_inc(ld_small, 16)
            column(0, a["L0_xattn_b_q"])
            column(1, a["L0_xattn_b_k"])
            column(2, a["L1_xattn_b_q"])
            column(3, a["L1_xattn_b_k"])
            column(4, a["L1_ffn_b_qkv"][0:D])
            column(5, a["L1_ffn_b_qkv"][D:2 * D])
            act.dma_start(gates[:, 0:4], a["g_xattn"].partition_broadcast(P)).then_inc(ld_small, 16)
            act.dma_start(gates[:, 4:8], a["g_ffn"].partition_broadcast(P)).then_inc(ld_small, 16)
            for half in range(2):
                act.dma_start(mask_i[half * S:(half + 1) * S, :], a["mask_1x1xSxS2_ik0"][0, 0, :, :])\
                    .then_inc(ld_small, 16)
            for i, n in enumerate(("L0_xattn_b_v", "L1_xattn_b_v")):
                act.dma_start(v_bias[:, i, :], a[n].partition_broadcast(P)).then_inc(ld_small, 16)
            act.dma_start(v_bias[:, 2, :], a["L1_ffn_b_qkv"][2 * D:3 * D].partition_broadcast(P)).then_inc(ld_small, 16)
            act.dma_start(w_qkv[:, :], a["L1_ffn_W_qkv"]).then_inc(ld_small, 16)
            for i, n in enumerate(("L0_xattn_b_o", "L1_xattn_b_o", "L2_xattn_b_proj")):
                act.dma_start(bo_row[64:65, i, :], a[n].rearrange("(o d) -> o d", o=1)).then_inc(ld_late, 16)
            act.dma_start(gate_raw[:, :], a["L0_ffn_gate_w"]).then_inc(ld_late, 16)
            act.dma_start(gate_w[:, 1, :], a["L1_ffn_W_gate"]).then_inc(ld_late, 16)
            act.dma_start(gate_w[:, 2, :], a["L3_ffn_gate_w"]).then_inc(ld_late, 16)
            act.dma_start(gate_b[:, 0, :], a["L1_ffn_b_gate"].partition_broadcast(P)).then_inc(ld_late, 16)
            act.dma_start(gate_b[:, 1, :], a["L3_ffn_gate_b"].partition_broadcast(P)).then_inc(ld_late, 16)
            act.dma_start(b1_raw[:, :], a["L3_ffn_mlp1_b"]).then_inc(ld_late, 16)
            act.dma_start(be[:, 0, :], a["L1_ffn_b_experts"]).then_inc(ld_late, 16)
            act.dma_start(be[:, 1, :], a["L3_ffn_mlp2_b"]).then_inc(ld_late, 16)
            act.dma_start(we1[:, :, :], a["L1_ffn_W_experts"].rearrange("e d f -> d e f")).then_inc(ld_late, 16)
            act.dma_start(ns_row[:, :], a["L3_ffn_norm_scale"].partition_broadcast(P)).then_inc(ld_late, 16)
            act.dma_start(rw1[:, :], a["L2_ffn_router_w1"]).then_inc(ld_late, 16)
            act.dma_start(rw2[:, :], a["L2_ffn_router_w2"]).then_inc(ld_late, 16)

            act.wait_ge(ld_small, 16 * 14)
            act.activation(gates[:, :], gates[:, :], ACT.Tanh).then_inc(gates_ready, 1)
            for half in range(2):
                act.wait_ge(ctxT_psum, half + 1)
                act.copy(ctxT[:, half * HALF:(half + 1) * HALF], bank[half][:, :]).then_inc(ctxT_ready, 1)
            for i in range(2):
                act.wait_ge(wT_psum, i + 1)
                act.copy(wT[:, 4 * i:4 * i + 4, :], bank[2 + i][:, :].rearrange("p (i d) -> p i d", i=4))\
                    .then_inc(wT_ready, 1)
            act.wait_ge(wo_psum, 1)
            act.wait_ge(gates_ready, 1)
            act.wait_ge(consts_set, 1)
            act.wait_ge(ld_late, 16 * 15)
            for m in range(NM):
                g = gates[0:64, MHA_GATE[m]:MHA_GATE[m] + 1]
                src = bank[4 + m // 2][0:64, (m % 2) * 256:(m % 2) * 256 + 256].rearrange("p (j d) -> p j d", j=2)
                ins = act.activation(w_out[0:64, m, :, :], src, ACT.Copy, scale=g)
                if m == 1:
                    ins.then_inc(wo_ready, 1)
            ins.then_inc(wo_ready, 1)
            for i, m in enumerate((0, 1, 3)):
                g = gates[64:65, MHA_GATE[m]:MHA_GATE[m] + 1]
                link(act.activation(w_out[64:65, m, 0, :], bo_row[64:65, i, :], ACT.Copy, scale=g))
            act.wait_ge(gw_psum, 1)
            act.copy(gate_w[:, 0, :], bank[7][:, 0:8]).then_inc(gw_ready, 1)

            def xT_halves(n):
                for half in range(2):
                    act.wait_ge(xT_psum, 2 * n + half + 1)
                    act.copy(xT[:, half * HALF:(half + 1) * HALF], bank[6 + half][:, :]).then_inc(xT_ready, 1)

            def mha(m):
                def step(b, s, steady, tau):
                    gb = B * m + b

                    def live(lag):
                        return steady or 0 <= b - lag < B
                    if live(0):
                        act.wait_ge(shift_ready, gb + 1)
                        after(act, pT_psum, gb - 1)
                        act.activation(probs[:, s, :, :], shifted[:, s, :, :], ACT.Exp).then_inc(exp_done, 1)
                    if live(1):
                        u = 1 - s
                        act.wait_ge(pT_psum, gb)
                        after(act, pv_done, gb - 2)
                        act.copy(probsT[:, u, :, :], bank[2 + u][:, :].rearrange("p (i q) -> p i q", i=QUAD))\
                            .then_inc(pT_ready, 1)
                    if live(3):
                        u = 1 - s
                        act.wait_ge(oT_psum, gb - 2)
                        if u == 0:
                            after(act, y_psum, NT * m + tau - 1 - (1 - s))
                        act.copy(oT[0:64, :, u * S:(u + 1) * S],
                                 bank[6][0:64, u * P:(u + 1) * P].rearrange("p (j q) -> p j q", j=2)).then_inc(oT_ready, 1)
                for tau in (0, 1, 2):
                    for s in range(2):
                        step(2 * tau + s, s, False, tau)
                with act.Fori(3, NT) as tau:
                    for s in range(2):
                        step(2 * tau + s, s, True, tau)
                for tau in (NT, NT + 1):
                    for s in range(2):
                        step(2 * tau + s, s, False, tau)

            def ffn(f, state):
                chunks = FFN_C[f]
                pair0 = state[0]

                def body(e):
                    for k in range(4 * chunks):
                        n = pair0 + 4 * chunks * e + k
                        u = k % 2
                        if f < 2:
                            act.wait_ge(up_psum, n + 1)
                            after(act, h_ready, n - 1)
                            act.activation(act_out[:, u, :], bank[2 * u][:, :], ACT.Silu).then_inc(act_ready, 1)
                        else:
                            act.wait_ge(glu_ready, n - pair0 + 1)
                            after(act, gated_ready, n - pair0 - 1)
                            act.activation(act_out[:, u, :], glu[:, u, :], ACT.Sigmoid, scale=1.702)\
                                .then_inc(act_ready, 1)

                body(0)
                with act.Fori(1, FFN_E[f] // 2) as e:
                    body(e)

            def exp_of_logits(k):
                act.wait_ge(dve_to_act, k)
                act.activation(logits[:, :, :], logits[:, :, :], ACT.Exp).then_inc(act_to_dve, 1)

            def combT_halves(i):
                act.wait_ge(combT_psum, i)
                for g in range(2):
                    ins = act.copy(combT[:, g * HALF:(g + 1) * HALF], bank[4 + g][0:8, :])
                ins.then_inc(combT_ready, 1)

            states = ffn_states()
            xT_halves(0)
            mha(0)
            if stop <= 1:
                return
            xT_halves(1)
            exp_of_logits(1)
            ffn(0, states[0])
            if stop <= 2:
                return
            xT_halves(2)
            mha(1)
            if stop <= 3:
                return
            xT_halves(3)
            mha(2)
            exp_of_logits(2)
            combT_halves(1)
            if stop <= 4:
                return
            xT_halves(4)
            mha(3)
            if stop <= 5:
                return
            xT_halves(5)
            for half in range(2):
                act.wait_ge(r1_psum, half + 1)
                act.activation(r1[:, half * HALF:(half + 1) * HALF], bank[half][:, :], ACT.Silu).then_inc(r1_ready, 1)
            act.wait_ge(dve_to_act, 3)
            act.activation(rp[:, :, :], rwork[:, :, :], ACT.Exp).then_inc(act_to_dve, 1)
            ffn(1, states[1])
            if stop <= 6:
                return
            xT_halves(6)
            for g in range(2):
                act.wait_ge(s3_ready, g + 1)
                for half in range(2):
                    rows = slice(half * S, (half + 1) * S)
                    ins = act.activation(p3[rows, 4 * g:4 * g + 4, half * S:(half + 1) * S],
                                         s3[rows, 4 * g:4 * g + 4, :], ACT.Exp, scale=float(1.0 / np.sqrt(D)))
                ins.then_inc(p3_ready, 1)
            for g in range(2):
                act.wait_ge(p3T_psum, g + 1)
                act.copy(p3T[:, 4 * g:4 * g + 4, :], bank[2 + g][:, :].rearrange("p (i q) -> p i q", i=4))\
                    .then_inc(p3T_ready, 1)
            if stop <= 7:
                return
            xT_halves(7)
            exp_of_logits(4)
            combT_halves(2)
            ffn(2, states[2])

        @block.gpsimd
        def _(pool):
            done = [0]

            def link(ins):
                done[0] += 1
                ins.then_inc(pool_done, 1)
                pool.wait_ge(pool_done, done[0])

            link(pool.memset(minus_half[:, :], -0.5))
            link(pool.memset(oT[64:65, :, :], 1.0))
            link(pool.memset(ctx_tok[:, :, D:D + 1], 1.0))
            link(pool.memset(o_norm[:, :, :, :, :], 0.0))
            link(pool.memset(p3[:, :, :], 0.0))
            link(pool.memset(v_blk[:, :, :, :], 0.0))
            ones = v_blk[:, :, :, :].rearrange("p m b (i j c) -> p (m b i) j c", i=QUAD, j=2)
            for j in range(2):
                link(pool.memset(ones[j * S:(j + 1) * S, :, j, VW - 1:VW], 1.0))
            link(pool.memset(rw2_pad[:, :, :], 0.0))
            ins = pool.memset(w_out[64:65, :, :, :], 0.0)
            ins.then_inc(consts_set, 1)

            def rstd_of(n):
                pool.wait_ge(mv_ready, n + 1)
                link(pool.tensor_scalar(var_eps[:, :], mv[:, :, 1], LN_EPS, None, ALU.add))
                pool.tensor_tensor(rstd[:, :], var_eps[:, :], minus_half[:, :], ALU.pow).then_inc(rstd_ready, 1)

            def mha(m, q_src, k_src, ready):
                ready()

                def step(b, s):
                    gb = B * m + b
                    cols = bass.ds(b * S, S)
                    after(pool, scores_done, gb - 1)
                    pool.tensor_tensor(q_blk[:, s, :, :], q_src[:, cols].unsqueeze(1).broadcast_to([P, 2, S]),
                                       q_scale[:, 0 if m < 2 else 1, :, :], ALU.mult).then_inc(blocks_ready, 1)
                    pool.tensor_tensor(k_blk[:, s, :, :], k_src[:, cols].unsqueeze(1).broadcast_to([P, PAIR, S]),
                                       const[:, C_PM:C_PM + PAIR].unsqueeze(2).broadcast_to([P, PAIR, S]), ALU.mult)\
                        .then_inc(blocks_ready, 1)
                for s in range(2):
                    step(s, s)
                with pool.Fori(1, NT) as tau:
                    for s in range(2):
                        step(2 * tau + s, s)

            rstd_of(0)

            def ready(n):
                def wait():
                    pool.wait_ge(proj_ready, n)
                    pool.wait_ge(q_scale_ready, 1)
                return wait
            mha(0, qT, kT[:, 0, :], ready(10))
            if stop <= 1:
                return
            rstd_of(1)
            rstd_of(2)
            pool.wait_ge(ld_ctx, 48)
            pool.wait_ge(rstd_ready, 3)
            for j in range(2):
                rows = slice(j * S, (j + 1) * S)
                dst = v_blk[rows, 3, :, :].rearrange("p b (i j c) -> p b i j c", i=QUAD, j=2)[:, :, :, j, 0:2 * DK]
                src = ctx_dup[rows, :, :].rearrange("p b (i j c) -> p b i j c", i=QUAD, j=2)[:, :, :, j, :]
                ins = pool.tensor_copy(dst, src)
                ins.then_inc(v3_ready, 1)
                pool.wait_ge(v3_ready, j + 1)
            pool.wait_ge(ld_late, 16 * 15)
            for i in range(8):
                pool.tensor_copy(rw2_pad[:, i, 16 * i:16 * i + 16], rw2[:, :]).then_inc(pad_ready, 1)
            mha(1, qT, kT[:, 1, :], ready(12))
            if stop <= 3:
                return
            rstd_of(3)
            mha(2, qT, kT[:, 2, :], ready(16))
            rstd_of(4)

            def ready3():
                pool.wait_ge(xT_ready, 10)
            mha(3, xT, ctxT, ready3)
            if stop <= 5:
                return
            rstd_of(5)
            rstd_of(6)
            rstd_of(7)
            pool.wait_ge(mv_ready, 9)
            link(pool.tensor_tensor(var_eps[:, :], mv[:, :, 0], mv[:, :, 0], ALU.mult))
            link(pool.tensor_tensor(var_eps[:, :], var_eps[:, :], mv[:, :, 1], ALU.add))
            link(pool.tensor_scalar(var_eps[:, :], var_eps[:, :], LN_EPS, None, ALU.add))
            pool.tensor_tensor(rstd[:, :], var_eps[:, :], minus_half[:, :], ALU.pow).then_inc(rstd_ready, 1)

            def body(e):
                for k in range(8):
                    n = 8 * e + k
                    u = k % 2
                    pool.wait_ge(act_ready, act0 + n + 1)
                    after(pool, h_ready, act0 + n - 1)
                    pool.tensor_tensor(gated[:, u, :], glu[:, u, :], act_out[:, u, :], ALU.mult).then_inc(gated_ready, 1)
            act0 = ffn_states()[2][0]
            body(0)
            with pool.Fori(1, FFN_E[2] // 2) as e:
                body(e)

        @block.vector
        def _(dve):
            v = nc.vector
            done = [0]

            def link(ins):
                done[0] += 1
                ins.then_inc(dve_done, 1)
                dve.wait_ge(dve_done, done[0])

            dve.wait_ge(ld_const, 16)
            v.tensor_copy(dup_bf[:, :], const[:, C_DUP:C_DUP + P])
            dve.wait_ge(ld_w, 16 * 9)
            for m, w in enumerate((w_raw[:, 3, :], w_raw[:, 7, :], ident, w_raw[:, 8, :])):
                ins = v.tensor_copy(wo_by_j2[:, m, :, :].rearrange("n j (p d) -> n j p d", d=DK),
                                    w.rearrange("n (p j d) -> n j p d", j=2, d=DK))
            ins.then_inc(wo_split, 1)
            dve.wait_ge(ld_small, 16 * 14)
            link(v.tensor_scalar(mask_open[:, :], mask_i[:, :], 0, None, ALU.not_equal))
            v.tensor_scalar(mask_low[:, :], mask_open[:, :], -1.0, BIG, ALU.add, ALU.mult)
            v.reduce_max(row_open[:, :], mask_open[:, :], AX).then_inc(mask_ready, 1)
            dve.wait_ge(rb_psum, 1)
            v.tensor_copy(biases[:, 6:8], bank[6][:, 0:2]).then_inc(rb_ready, 1)
            dve.wait_ge(rb_ready, 1)
            dve.wait_ge(ro_psum, 1)
            for j2 in range(2):
                v.tensor_scalar(q_scale[:, 0, j2, :], bank[6][:, 64:128], const[:, C_JM + j2:C_JM + j2 + 1], None, ALU.mult)
            for j2 in range(2):
                ins = v.tensor_copy(q_scale[:, 1, j2, :], const[:, C_JM + j2:C_JM + j2 + 1].broadcast_to([P, S]))
            ins.then_inc(q_scale_ready, 1)
            dve.wait_ge(ld_late, 16 * 15)
            dve.wait_ge(b1_psum, 1)
            b1_src = bank[7][:, 16:48].rearrange("p (c k e) -> p c k e", c=2, k=2)
            v.tensor_copy(b1_col[:, :, 0, :], b1_src[:, :, 0, :])
            v.tensor_scalar(b1_col[:, :, 1, :], b1_src[:, :, 1, :], 1.0, None, ALU.add).then_inc(b1_ready, 1)

            count = [0]

            def rotated(dst, half, b_col, r_col):
                def table(c):
                    return const[:, c:c + S].unsqueeze(1).broadcast_to([P, HALF // S, S])

                def split(ap):
                    return ap.rearrange("p (b s) -> p b s", s=S)
                d = dst[:, half * HALF:(half + 1) * HALF]
                n = count[0]
                dve.wait_ge(proj_psum, n + 1)
                link(v.scalar_tensor_tensor(split(d), split(bank[n % 4][:, :]), b_col, table(C_COS), ALU.add, ALU.mult))
                dve.wait_ge(proj_psum, n + 2)
                link(v.scalar_tensor_tensor(split(rot_tmp[:, :]), split(bank[(n + 1) % 4][:, :]), r_col, table(C_SIN),
                                            ALU.add, ALU.mult))
                v.tensor_tensor(d, d, rot_tmp[:, :], ALU.add).then_inc(proj_ready, 2)
                count[0] += 2

            def biased(dst, half, b_col):
                n = count[0]
                dve.wait_ge(proj_psum, n + 1)
                v.tensor_scalar(dst[:, half * HALF:(half + 1) * HALF], bank[n % 4][:, :], b_col, None, ALU.add)\
                    .then_inc(proj_ready, 1)
                count[0] += 1

            vcount = [0]

            def values(m, bias_i):
                dve.wait_ge(consts_set, 1)
                for g in range(4):
                    n = vcount[0]
                    dve.wait_ge(v_psum, n + 1)
                    src = bank[4 + n % 2][:, :].rearrange("p (b i j c) -> p b i j c", b=4, i=QUAD, j=2)
                    for j in range(2):
                        rows = slice(j * S, (j + 1) * S)
                        bias = v_bias[rows, bias_i, :].rearrange("p (i j c) -> p i j c", i=QUAD, j=2)[:, :, j, :]
                        parts = ((0, 4, 4 * g),) if j == 0 else ((0, 4, 4 * g + 1),) if g < 3 else ((0, 3, 13), (3, 4, 0))
                        for i0, i1, b0 in parts:
                            dst = v_blk[rows, m, b0:b0 + i1 - i0, :].rearrange("p b (i j c) -> p b i j c", i=QUAD, j=2)
                            ins = v.tensor_tensor(dst[:, :, :, j, 0:2 * DK], src[rows, i0:i1, :, j, :],
                                                  bias.unsqueeze(1).broadcast_to([S, i1 - i0, QUAD, 2 * DK]), ALU.add)
                    ins.then_inc(v_ready, 1)
                    vcount[0] += 1

            def layer_norm(n):
                for t in range(NT):
                    ins = v.bn_stats(stats[:, t, :], x_tok[:, t, :])
                link(ins)
                for t in range(NT):
                    ins = v.bn_aggr(mv[:, t, :], stats[:, t, :])
                ins.then_inc(mv_ready, 1)
                dve.wait_ge(mv_ready, n + 1)
                dve.wait_ge(rstd_ready, n + 1)
                for t in range(NT):
                    v.tensor_scalar(x_norm[:, t, :], x_tok[:, t, :], mv[:, t, 0:1], rstd[:, t:t + 1],
                                    ALU.subtract, ALU.mult).then_inc(xn_ready, 1)

            def mha(m):
                def step(b, s, steady, tau, tile_live):
                    gb = B * m + b

                    def live(lag):
                        return steady or 0 <= b - lag < B
                    if live(0):
                        scores = bank[s][:, :].rearrange("p (h k) -> p h k", h=PAIR)
                        dve.wait_ge(scores_done, gb + 1)
                        v.reduce_max(row_max[:, s, :], scores, AX).then_inc(max_ready, 1)
                        dve.wait_ge(max_ready, gb + 1)
                        after(dve, exp_done, gb - 1)
                        v.tensor_tensor(shifted[:, s, :, :], scores,
                                        row_max[:, s, :].unsqueeze(2).broadcast_to([P, PAIR, S]), ALU.subtract)\
                            .then_inc(shift_ready, 1)
                    if live(2):
                        dve.wait_ge(pv_done, gb - 1)
                        o = bank[4 + s][:, 0:VB].rearrange("p (h c) -> p h c", h=PAIR)
                        v.reciprocal(inv_sum[:, s, :], o[:, :, VW - 1]).then_inc(inv_ready, 1)
                        dve.wait_ge(inv_ready, gb - 1)
                        after(dve, oT_psum, gb - 3)
                        for j2 in range(2):
                            rows = slice(j2 * S, (j2 + 1) * S)
                            ins = v.tensor_tensor(o_norm[rows, s, 0, :, :], o[rows, :, j2 * DK:(j2 + 1) * DK],
                                                  inv_sum[rows, s, :].unsqueeze(2).broadcast_to([S, PAIR, DK]), ALU.mult)
                        ins.then_inc(on_ready, 1)
                    if s == 1 and tile_live:
                        dve.wait_ge(y_psum, NT * m + tau - 1)
                        xs = x_tok[:, bass.ds(tau - 2, 1), :].rearrange("p o d -> p (o d)")
                        v.tensor_tensor(xs, xs, bank[7][:, 0:D], ALU.add).then_inc(x_added, 1)
                for tau in (0, 1, 2):
                    for s in range(2):
                        step(2 * tau + s, s, False, tau, tau >= 2)
                with dve.Fori(3, NT) as tau:
                    for s in range(2):
                        step(2 * tau + s, s, True, tau, True)
                for tau in (NT, NT + 1):
                    for s in range(2):
                        step(2 * tau + s, s, False, tau, True)
                dve.wait_ge(x_added, NT * (m + 1))

            def add_all(out_, x_, y_, op=ALU.add):
                return v.tensor_tensor(out_, x_, y_, op)

            def top2_router(i, k, bias_i):
                dve.wait_ge(logit_psum, i + 1)
                src = bank[0][:, 0:NT * 8].rearrange("p (t e) -> p t e", t=NT)
                if bias_i is None:
                    link(v.tensor_copy(logits[:, :, :], src))
                else:
                    link(v.tensor_tensor(logits[:, :, :], src,
                                         gate_b[:, bias_i, :].unsqueeze(1).broadcast_to([P, NT, 8]), ALU.add))
                mine = logits[:, :, :].unsqueeze(3).broadcast_to([P, NT, 8, 8])
                other = logits[:, :, :].unsqueeze(2).broadcast_to([P, NT, 8, 8])
                tri = const[:, C_TRI:C_TRI + 64].rearrange("p (e f) -> p e f", e=8).unsqueeze(1).broadcast_to([P, NT, 8, 8])
                v.tensor_tensor(gt[:, :, :, :], other, mine, ALU.is_gt)
                v.reduce_max(e_max[:, :], logits[:, :, :], AX)
                link(v.tensor_tensor(eq[:, :, :, :], other, mine, ALU.is_equal))
                v.tensor_tensor(logits[:, :, :], logits[:, :, :], e_max[:, :].unsqueeze(2).broadcast_to([P, NT, 8]),
                                ALU.subtract).then_inc(dve_to_act, 1)
                link(v.tensor_tensor(eq[:, :, :, :], eq[:, :, :, :], tri, ALU.mult))
                link(v.tensor_tensor(gt[:, :, :, :], gt[:, :, :, :], eq[:, :, :, :], ALU.add))
                link(v.reduce_sum(rank[:, :, :], gt[:, :, :, :], AX))
                link(v.tensor_scalar(top[:, :, :], rank[:, :, :], 1.5, None, ALU.is_lt))
                dve.wait_ge(act_to_dve, k)

                def share(eps):
                    link(v.reduce_sum(e_sum[:, :], logits[:, :, :], AX))
                    if eps:
                        link(v.tensor_scalar(e_sum[:, :], e_sum[:, :], eps, None, ALU.add))
                    link(v.reciprocal(e_sum[:, :], e_sum[:, :]))
                    link(v.tensor_tensor(logits[:, :, :], logits[:, :, :],
                                         e_sum[:, :].unsqueeze(2).broadcast_to([P, NT, 8]), ALU.mult))
                if i < 2:
                    share(0)
                link(v.tensor_tensor(logits[:, :, :], logits[:, :, :], top[:, :, :], ALU.mult))
                if i == 0:
                    share(1e-9)
                    share(1e-9)
                if i == 2:
                    share(0)
                gate = gates[:, (4, 5, 7)[i]:(4, 5, 7)[i] + 1]
                ins = v.tensor_scalar(comb[:, :, 0:8], logits[:, :, :], gate, None, ALU.mult)
                ins.then_inc(comb_ready, 1)
                dve.wait_ge(comb_ready, (1, 2, 4)[i])

            def add_biases(i):
                dve.wait_ge(be_psum, i)
                for g in range(2):
                    xs = x_tok[:, 4 * g:4 * g + 4, :]
                    ins = v.tensor_tensor(xs, xs, bank[6 + g][:, :].rearrange("p (t d) -> p t d", t=4), ALU.add)
                ins.then_inc(be_added, 1)
                dve.wait_ge(be_added, i)

            def ffn(f, state):
                chunks = FFN_C[f]
                pair0, exp0, _ = state

                def hidden(e, k, c):
                    u = (k * chunks + c) % 2
                    n = pair0 + (4 * e + k) * chunks + c
                    dve.wait_ge(act_ready if f < 2 else gated_ready, n + 1 if f < 2 else n + 1 - pair0)
                    if c == 0:
                        after(dve, down_psum, 2 * exp0 + 4 * e + k - 1)
                    dst = hid[:, k % 2, c, :]
                    if f < 2:
                        v.tensor_tensor(dst, act_out[:, u, :], bank[2 * u + 1][:, :], ALU.mult).then_inc(h_ready, 1)
                    else:
                        dve.wait_ge(up_free, n + 1 - pair0)
                        v.scalar_tensor_tensor(dst, lin[:, u, :], -6.0, gated[:, u, :], ALU.max, ALU.mult)\
                            .then_inc(h_ready, 1)

                def clamp(e, k, c):
                    u = (k * chunks + c) % 2
                    n = pair0 + (4 * e + k) * chunks + c
                    slot = k // 2
                    dve.wait_ge(up_psum, n + 1)
                    bg = b1_col[:, c, 0, bass.ds(2 * e + slot, 1)]
                    bl = b1_col[:, c, 1, bass.ds(2 * e + slot, 1)]
                    v.tensor_scalar(glu[:, u, :], bank[2 * u][:, :], bg, 7.0, ALU.add, ALU.min).then_inc(glu_ready, 1)
                    after(dve, h_ready, n - 1)
                    v.tensor_scalar(lin[:, u, :], bank[2 * u + 1][:, :], bl, 8.0, ALU.add, ALU.min).then_inc(up_free, 1)

                def accumulate(e, k):
                    n = 2 * exp0 + 4 * e + k
                    slot, half = k // 2, k % 2
                    dve.wait_ge(down_psum, n + 1)
                    after(dve, down_added, n - 1)
                    for i in range(4):
                        t = 4 * half + i
                        ins = v.scalar_tensor_tensor(x_tok[:, t, :], bank[4 + half][:, i * D:(i + 1) * D],
                                                     comb[:, t, bass.ds(2 * e + slot, 1)], x_tok[:, t, :], ALU.mult, ALU.add)
                    ins.then_inc(down_added, 1)

                def body(e, first):
                    for k in range(4):
                        for c in range(chunks):
                            if f < 2:
                                hidden(e, k, c)
                            else:
                                clamp(e, k, c)
                                if c == 1:
                                    hidden(e, k, 0)
                                elif k > 0:
                                    hidden(e, k - 1, 1)
                                elif not first:
                                    hidden(e - 1, 3, 1)
                        if k > 0:
                            accumulate(e, k - 1)
                        elif not first:
                            accumulate(e - 1, 3)
                body(0, True)
                with dve.Fori(1, FFN_E[f] // 2) as e:
                    body(e, False)
                if f == 2:
                    hidden(FFN_E[f] // 2 - 1, 3, 1)
                accumulate(FFN_E[f] // 2 - 1, 3)
                dve.wait_ge(down_added, 2 * (exp0 + FFN_E[f]))

            def finish():
                v.tensor_copy(row_open[:, :], x_tok[:, 0, 0:1]).then_inc(x_final, 1)

            states = ffn_states()
            for half in range(2):
                rotated(kT[:, 0, :], half, bk0, rk0)
            for half in range(2):
                biased(kT[:, 1, :], half, bk1)
            values(0, 0)
            values(1, 1)
            dve.wait_ge(ld_x, 16)
            layer_norm(0)
            for half in range(2):
                rotated(qT, half, bq0, rq0)
            mha(0)
            if stop <= 1:
                return finish()
            layer_norm(1)
            top2_router(0, 1, None)
            ffn(0, states[0])
            if stop <= 2:
                return finish()
            layer_norm(2)
            for half in range(2):
                biased(qT, half, bq1)
            mha(1)
            if stop <= 3:
                return finish()
            layer_norm(3)
            for half in range(2):
                biased(qT, half, bqs)
                biased(kT[:, 2, :], half, bks)
            values(2, 2)
            mha(2)
            top2_router(1, 2, 0)
            add_biases(1)
            for t in range(NT):
                dve.wait_ge(e1_psum, t + 1)
                for e in range(8):
                    ins = v.scalar_tensor_tensor(x_tok[:, t, :], bank[2 * (t % 2) + e // 4][:, (e % 4) * D:(e % 4 + 1) * D],
                                                 comb[:, t, e:e + 1], x_tok[:, t, :], ALU.mult, ALU.add)
                    if e < 7:
                        link(ins)
                ins.then_inc(e1_added, 1)
                dve.wait_ge(e1_added, t + 1)
            if stop <= 4:
                return finish()
            layer_norm(4)
            mha(3)
            if stop <= 5:
                return finish()
            layer_norm(5)
            dve.wait_ge(r2_psum, 1)
            src = bank[2][:, 0:2 * S].rearrange("p (f s) -> p f s", f=2)

            def over_tokens(ap):
                return ap.unsqueeze(2).broadcast_to([P, 2, S])
            link(v.reduce_max(rcol[:, :], src, AX))
            v.tensor_tensor(rwork[:, :, :], src, over_tokens(rcol[:, :]), ALU.subtract).then_inc(dve_to_act, 1)
            dve.wait_ge(act_to_dve, 3)
            link(v.reduce_sum(rcol[:, :], rp[:, :, :], AX))
            link(v.reciprocal(rcol[:, :], rcol[:, :]))
            link(v.tensor_tensor(rp[:, :, :], rp[:, :, :], over_tokens(rcol[:, :]), ALU.mult))
            link(v.tensor_copy(rwork[:, :, :], rp[:, :, :]))
            for _ in range(TOP_C // 8):
                for f in range(2):
                    ins = v.max(rtop[:, f, :], rwork[:, f, :])
                link(ins)
                for f in range(2):
                    ins = v.match_replace(rwork[:, f, :], rtop[:, f, :], rwork[:, f, :], -1.0)
                link(ins)
            link(v.tensor_scalar(rwork[:, :, :], rwork[:, :, :], 0.0, None, ALU.is_lt))
            link(v.tensor_tensor(rp[:, :, :], rp[:, :, :], rwork[:, :, :], ALU.mult))
            link(v.reduce_sum(rcol[:, :], rp[:, :, :], AX))
            link(v.tensor_scalar(rcol[:, :], rcol[:, :], 1e-9, None, ALU.add))
            link(v.reciprocal(rcol[:, :], rcol[:, :]))
            link(v.tensor_scalar(rcol[:, :], rcol[:, :], gates[:, 6:7], None, ALU.mult))
            for c in range(2):
                ins = v.tensor_tensor(rsel[:, :, c, :], rp[:, :, :], over_tokens(rcol[:, :]), ALU.mult)
            ins.then_inc(rsel_ready, 1)
            dve.wait_ge(rT_psum, 1)
            for odd in range(2):
                rows = slice(odd * S, (odd + 1) * S)
                src = bank[3][rows, 0:2 * P].rearrange("p (t o e) -> p t o e", o=2, e=16)[:, :, odd, :]
                ins = v.tensor_copy(comb[rows, :, :], src)
            ins.then_inc(comb_ready, 1)
            dve.wait_ge(comb_ready, 3)
            ffn(1, states[1])
            if stop <= 6:
                return finish()
            layer_norm(6)
            for g in range(2):
                dve.wait_ge(s3_psum, g + 1)
                src = bank[g][:, :].rearrange("p (t k) -> p t k", t=4)
                for half in range(2):
                    rows = slice(half * S, (half + 1) * S)
                    ins = v.reduce_max(m3[rows, 4 * g:4 * g + 4], src[rows, :, half * S:(half + 1) * S], AX)
                link(ins)
                for half in range(2):
                    rows = slice(half * S, (half + 1) * S)
                    ins = v.tensor_tensor(s3[rows, 4 * g:4 * g + 4, :], src[rows, :, half * S:(half + 1) * S],
                                          m3[rows, 4 * g:4 * g + 4].unsqueeze(2).broadcast_to([S, 4, S]), ALU.subtract)
                ins.then_inc(s3_ready, 1)
            for t in range(NT):
                o = bank[4 + t // 3][:, (t % 3) * (D + 1):(t % 3 + 1) * (D + 1)]
                dve.wait_ge(o3_psum, t // 3 + 1)
                link(v.reciprocal(m3[:, t:t + 1], o[:, D:D + 1]))
                link(v.tensor_scalar(m3[:, t:t + 1], m3[:, t:t + 1], gates[:, 3:4], None, ALU.mult))
                ins = v.scalar_tensor_tensor(x_tok[:, t, :], o[:, 0:D], m3[:, t:t + 1], x_tok[:, t, :], ALU.mult, ALU.add)
            link(ins)
            if stop <= 7:
                return finish()
            for t in range(NT):
                ins = v.bn_stats(stats[:, t, :], x_tok[:, t, :])
            link(ins)
            for t in range(NT):
                ins = v.bn_aggr(mv[:, t, :], stats[:, t, :])
            ins.then_inc(mv_ready, 1)
            dve.wait_ge(mv_ready, 8)
            dve.wait_ge(rstd_ready, 8)
            for t in range(NT):
                ins = v.tensor_scalar(x_norm[:, t, :], x_tok[:, t, :], mv[:, t, 0:1], rstd[:, t:t + 1],
                                      ALU.subtract, ALU.mult)
            link(ins)
            for t in range(NT):
                ins = v.bn_stats(stats[:, t, :], x_norm[:, t, :])
            link(ins)
            for t in range(NT):
                ins = v.bn_aggr(mv[:, t, :], stats[:, t, :])
            ins.then_inc(mv_ready, 1)
            dve.wait_ge(rstd_ready, 9)
            for t in range(NT):
                v.scalar_tensor_tensor(x_rms[:, t, :], x_norm[:, t, :], rstd[:, t:t + 1], ns_row[:, :],
                                       ALU.mult, ALU.mult).then_inc(xn_ready, 1)
            for t in range(NT):
                ins = v.scalar_tensor_tensor(x_tok[:, t, :], x_norm[:, t, :], gates[:, 7:8], x_tok[:, t, :],
                                             ALU.mult, ALU.add)
            link(ins)
            top2_router(2, 4, 1)
            add_biases(2)
            ffn(2, states[2])
            finish()


INS = ['x', 'ctx_1024', 'mask_1x1xSxS2_ik0', 'g_xattn', 'g_ffn', 'L0_xattn_w_q', 'L0_xattn_b_q', 'L0_xattn_w_k',
       'L0_xattn_b_k', 'L0_xattn_w_v', 'L0_xattn_b_v', 'L0_xattn_w_o', 'L0_xattn_b_o', 'L0_ffn_gate_w',
       'L0_ffn_gate_up_proj', 'L0_ffn_down_proj', 'L1_xattn_w_q', 'L1_xattn_b_q', 'L1_xattn_w_k', 'L1_xattn_b_k',
       'L1_xattn_w_v', 'L1_xattn_b_v', 'L1_xattn_w_o', 'L1_xattn_b_o', 'L1_ffn_W_qkv', 'L1_ffn_b_qkv',
       'L1_ffn_W_gate', 'L1_ffn_b_gate', 'L1_ffn_W_experts', 'L1_ffn_b_experts', 'L2_xattn_W_proj',
       'L2_xattn_b_proj', 'L2_ffn_router_w1', 'L2_ffn_router_w2', 'L2_ffn_w1', 'L2_ffn_w2', 'L2_ffn_w3',
       'L3_ffn_norm_scale', 'L3_ffn_gate_w', 'L3_ffn_gate_b', 'L3_ffn_mlp1_w', 'L3_ffn_mlp1_b', 'L3_ffn_mlp2_w',
       'L3_ffn_mlp2_b']


def kernel(**inputs):
    import concourse.bacc as bacc
    from concourse.bass_utils import run_bass_kernel_spmd

    nc = bacc.Bacc("TRN2", target_bir_lowering=False, num_devices=1)
    arrays, aps = {}, {}
    data = {name: np.ascontiguousarray(inputs[name]) for name in INS}
    data["shape_constants"] = shape_constants()
    for name, array in data.items():
        arrays[f"in_{name}"] = array
        aps[name] = nc.dram_tensor(f"in_{name}", array.shape, mybir.dt.from_np(array.dtype), kind="ExternalInput").ap()
    out = nc.dram_tensor("out_x", (B, S, D), F32, kind="ExternalOutput").ap()
    build(nc, aps, out)
    result = run_bass_kernel_spmd(nc, [arrays], core_ids=[0])
    return result.results[0]["out_x"]
```

```python
from contextlib import ExitStack

import numpy as np

import concourse.bass as bass
from concourse import mybir

ALU = mybir.AluOpType
ACT = mybir.ActivationFunctionType
AX = mybir.AxisListType.X
F32 = mybir.dt.float32
F32R = mybir.dt.float32r
BF16 = mybir.dt.bfloat16
I32 = mybir.dt.int32

P = 128
B, S, D = 16, 64, 128
T = B * S
NT = T // P
HALF = T // 2
H, DK = 16, 8
PAIR = H // 2
VW = 2 * DK + 1
QUAD = PAIR // 2
VB = QUAD * 2 * VW
BIG = float(2 ** 30)
LN_EPS = 1e-5

MHA_GATE = (0, 1, 5, 2)
NM = len(MHA_GATE)
NEXT_LN = (1, 3, 4, 5)
FILL, DRAIN = 4, 4
FFN_E = (8, 16, 8)
FFN_C = (1, 2, 2)
UP_DMA = (1, 2, 1)
FFN_SPLITS = (2, 2, 1)
SPLIT_UP_AT = (0, 1, 2)
RING = 4
DOWN_LAG = (2, 3, 3)
TOP_C = 32

C_ID, C_ROT, C_DUP, C_PM, C_JM, C_COS, C_SIN, C_TRI = 0, 128, 256, 384, 392, 394, 458, 522
C_N = 586


ROWS_N = 24 + 4 * D
FEATURE_N = 32 + 4 * D
EXPERT_N = 3 * D + 512


def packs(inp):
    def cat(arrays):
        return np.ascontiguousarray(np.concatenate(arrays, axis=-1))
    b_qkv = inp["L1_ffn_b_qkv"]
    return {
        "projections": np.ascontiguousarray(np.stack(
            [inp[n] for n in ("L0_xattn_w_q", "L0_xattn_w_k", "L0_xattn_w_v", "L0_xattn_w_o", "L1_xattn_w_q",
                              "L1_xattn_w_k", "L1_xattn_w_v", "L1_xattn_w_o", "L2_xattn_W_proj")], axis=1)),
        "bias_columns": np.ascontiguousarray(np.stack(
            [inp[n] for n in ("L0_xattn_b_q", "L0_xattn_b_k", "L1_xattn_b_q", "L1_xattn_b_k")]
            + [b_qkv[0:D], b_qkv[D:2 * D]], axis=1)),
        "rows": cat([inp["g_xattn"], inp["g_ffn"], inp["L1_ffn_b_gate"], inp["L3_ffn_gate_b"],
                     inp["L3_ffn_norm_scale"], inp["L0_xattn_b_v"], inp["L1_xattn_b_v"], b_qkv[2 * D:3 * D]]),
        "output_biases": cat([inp["L0_xattn_b_o"], inp["L1_xattn_b_o"], inp["L2_xattn_b_proj"]]),
        "by_feature": cat([inp["L1_ffn_W_gate"], inp["L3_ffn_gate_w"], inp["L2_ffn_router_w2"],
                           inp["L2_ffn_router_w1"], inp["L1_ffn_W_qkv"]]),
        "by_expert": cat([inp["L0_ffn_gate_w"], inp["L1_ffn_b_experts"], inp["L3_ffn_mlp2_b"], inp["L3_ffn_mlp1_b"]]),
    }


UNPACKED = ("x", "ctx_1024", "mask_1x1xSxS2_ik0", "L0_ffn_gate_up_proj", "L0_ffn_down_proj", "L1_ffn_W_experts",
            "L2_ffn_w1", "L2_ffn_w2", "L2_ffn_w3", "L3_ffn_mlp1_w", "L3_ffn_mlp2_w")


def shape_constants():
    c = np.zeros((P, C_N), np.float32)
    c[:, C_ID:C_ID + P] = np.eye(P)
    for h in range(H):
        for j in range(DK // 2):
            c[h * DK + 2 * j + 1, C_ROT + h * DK + j] = -1.0
            c[h * DK + 2 * j, C_ROT + h * DK + DK // 2 + j] = 1.0
    for q in range(S):
        c[q, C_DUP + q] = c[q, C_DUP + S + q] = 1.0
    rows = np.arange(P)
    for pair in range(PAIR):
        c[:, C_PM + pair] = rows // (2 * DK) == pair
    for j2 in range(2):
        c[:, C_JM + j2] = ((rows // DK) % 2 == j2) / np.sqrt(np.float32(DK))
    inv = (1.0 / 10000.0 ** (np.arange(0, DK, 2, dtype=np.float32) / DK)).astype(np.float32)
    ang = np.arange(S, dtype=np.float32)[:, None] * inv[None, :]
    ang = np.concatenate([ang, ang], axis=-1).astype(np.float32)
    c[:, C_COS:C_COS + S] = np.cos(ang).T[rows % DK]
    c[:, C_SIN:C_SIN + S] = np.sin(ang).T[rows % DK]
    c[:, C_TRI:C_TRI + 64] = np.tril(np.ones((8, 8)), -1).reshape(1, 64)
    return c


def ffn_states():
    out, pairs, experts, dmas, splits = [], 0, 0, 0, 0
    for f in range(3):
        out.append((pairs, experts, dmas, splits))
        pairs += 2 * FFN_E[f] * FFN_C[f]
        experts += FFN_E[f]
        dmas += 16 * UP_DMA[f] * FFN_E[f] // 2
        splits += FFN_SPLITS[f] * FFN_E[f]
    return out


def run_experts(eng, f, body):
    body(0, True, False)
    with eng.Fori(1, FFN_E[f] // 2 - 1) as e:
        body(e, False, False)
    body(FFN_E[f] // 2 - 1, False, True)


def run_tiles(eng, tile_step):
    for tau in range(FILL):
        tile_step(tau, False)
    with eng.Fori(FILL, NT) as tau:
        tile_step(tau, True)
    for tau in range(NT, NT + DRAIN):
        tile_step(tau, False)


def after(eng, sem, value):
    if not (isinstance(value, int) and value <= 0):
        eng.wait_ge(sem, value)


def build(nc, a, comb_dram, out):
    with ExitStack() as ctx:
        def sb(name, shape, dt=F32):
            return ctx.enter_context(nc.sbuf_tensor(name, shape, dt))

        def sem(name):
            return ctx.enter_context(nc.semaphore(name))

        bank = [ctx.enter_context(nc.psum_tensor(f"bank{i}", [P, 512], F32)) for i in range(8)]

        const = sb("const", [P, C_N])
        ident = const[:, C_ID:C_ID + P]
        dup_bf = sb("dup_bf", [P, P], BF16)
        x_tok = sb("x_tok", [P, NT, D])
        x_norm = sb("x_norm", [P, NT, D])
        xn_slot = sb("xn_slot", [P, D])
        xT = sb("xT", [P, T])
        stats = sb("stats", [P, NT, 6])
        mv = sb("mv", [P, NT, 2])
        var_eps = sb("var_eps", [P, NT])
        rstd = sb("rstd", [P, NT])
        stats_slot = sb("stats_slot", [P, 6])
        mv_slot = sb("mv_slot", [P, 2])
        eps_col = sb("eps_col", [P, 1])
        fourteen = sb("fourteen", [P, 1])
        var_slot = sb("var_slot", [P, 1])
        rstd_slot = sb("rstd_slot", [P, 1])
        minus_half = sb("minus_half", [P, NT])
        ctx_tok = sb("ctx_tok", [P, NT, D + 1])
        ctxT = sb("ctxT", [P, T])
        row_pack = sb("row_pack", [P, ROWS_N])
        gates = row_pack[:, 0:8]
        gate_b = row_pack[:, 8:24].rearrange("p (l e) -> p l e", l=2)
        ns_row = row_pack[:, 24:24 + D]
        v_bias = row_pack[:, 24 + D:24 + 4 * D].rearrange("p (l d) -> p l d", l=3)
        by_feature = sb("by_feature", [P, 8 + FEATURE_N])
        gate_w = by_feature[:, 0:24].rearrange("p (l e) -> p l e", l=3)
        rw2 = by_feature[:, 24:40]
        rw1 = by_feature[:, 40:40 + D]
        w_qkv = by_feature[:, 40 + D:40 + 4 * D]
        by_expert = sb("by_expert", [8, EXPERT_N])
        gate_raw = by_expert[:, 0:D]
        be = by_expert[:, D:3 * D].rearrange("e (l d) -> e l d", l=2)
        b1_raw = by_expert[:, 3 * D:3 * D + 512]
        biases = sb("biases", [P, 10])
        bq0, bk0, bq1, bk1, bqs, bks, rq0, rk0 = (biases[:, i:i + 1] for i in range(8))
        w_raw = sb("w_raw", [P, 9, D])
        wT = sb("wT", [P, 8, D])
        wo_by_j2 = sb("wo_by_j2", [P, NM, 2, 64])
        w_out = sb("w_out", [65, NM, 2, D])
        bo_row = sb("bo_row", [65, 3, D])
        mask_i = sb("mask_i", [P, S], I32)
        mask_open = sb("mask_open", [P, S])
        row_open = sb("row_open", [P, 1])
        mask_low = sb("mask_low", [P, S], BF16)
        q_scale = sb("q_scale", [P, 2, 2, S])
        kT = sb("kT", [P, 2, T])
        qT = sb("qT", [P, T])
        x_rms = kT[:, 1, :].rearrange("p (t d) -> p t d", d=D)
        rot_tmp = sb("rot_tmp", [P, HALF])
        v_blk = sb("v_blk", [P, NM, B, VB])
        q_blk = sb("q_blk", [P, 2, 2, S])
        k_blk = sb("k_blk", [P, 2, PAIR, S])
        row_max = sb("row_max", [P, 2, PAIR])
        shifted = sb("shifted", [P, 2, PAIR, S])
        probs = sb("probs", [P, 2, PAIR, S])
        probsT = sb("probsT", [P, 2, QUAD, P])
        inv_sum = sb("inv_sum", [P, 2, PAIR])
        o_norm = sb("o_norm", [P, 2, 2, PAIR, DK])
        oT = sb("oT", [65, 2, P])
        logits = sb("logits", [P, NT, 8])
        gt = sb("gt", [P, NT, 8, 8])
        eq = sb("eq", [P, NT, 8, 8])
        rank = sb("rank", [P, NT, 8])
        top = sb("top", [P, NT, 8])
        e_max = sb("e_max", [P, NT])
        e_sum = sb("e_sum", [P, NT])
        comb = sb("comb", [P, NT, 16])
        combT = sb("combT", [8, T])
        we1 = sb("we1", [P, 8, D])
        b1_col = sb("b1_col", [P, 2, 2, 8])
        w_up = sb("w_up", [P, 2, 512])
        w_dn = sb("w_dn", [P, 2, 2, D])
        xT_hi = sb("xT_hi", [P, T], F32R)
        xT_lo = sb("xT_lo", [P, T], F32R)
        w_up_hi = sb("w_up_hi", [P, 2, 512], F32R)
        w_up_lo = sb("w_up_lo", [P, 2, 512], F32R)
        w_dn_hi = sb("w_dn_hi", [P, 2, 2, D], F32R)
        w_dn_lo = sb("w_dn_lo", [P, 2, 2, D], F32R)
        comb_row = sb("comb_row", [P, 2, T])
        act_out = w_raw[:, 0:8, :].rearrange("p (s t) d -> p s (t d)", s=2)
        product = shifted[:, :, :, :].rearrange("p s h k -> p s (h k)")
        glu = k_blk[:, :, :, :].rearrange("p s h k -> p s (h k)")
        gated = probs[:, :, :, :].rearrange("p s h k -> p s (h k)")
        over = probsT[:, :, :, :].rearrange("p s i q -> p s (i q)")
        lin = sb("lin", [P, 2, HALF])
        hid = sb("hid", [P, RING, HALF])
        ctx_dup = hid[:, :, :].rearrange("p r (b d) -> p (r b) d", d=D)
        hid_hi = sb("hid_hi", [P, RING, HALF], F32R)
        hid_lo = sb("hid_lo", [P, RING, HALF], F32R)
        outT = sb("outT", [P, T])
        rw2_pad = sb("rw2_pad", [P, 8, P])
        r1 = qT
        rp = sb("rp", [P, 2, S])
        rwork = sb("rwork", [P, 2, S])
        rtop = sb("rtop", [P, 2, 8])
        rsel = sb("rsel", [P, 2, S])
        rcol = sb("rcol", [P, 2])
        s3 = rot_tmp[:, :].rearrange("p (t k) -> p t k", t=NT)
        p3 = sb("p3", [P, NT, P])
        p3T = outT[:, :].rearrange("p (t q) -> p t q", t=NT)
        m3 = sb("m3", [P, NT])

        ld_const, ld_x, ld_ctx, ld_w, ld_small, ld_late, ld_dup = (sem(n) for n in (
            "const_loaded", "x_loaded", "ctx_loaded", "proj_loaded", "small_loaded", "late_loaded", "dup_loaded"))
        k1_psum, k1_ready = sem("L1_keys_psum"), sem("L1_keys_ready")
        dve_done, pool_done, act_done = sem("dve_step_done"), sem("pool_step_done"), sem("act_step_done")
        gates_ready, consts_set, v_cleared = sem("gates_ready"), sem("consts_set"), sem("v_blocks_cleared")
        ctxT_psum, ctxT_ready = sem("ctxT_psum"), sem("ctxT_ready")
        wT_psum, wT_ready = sem("wT_psum"), sem("wT_ready")
        wo_psum, wo_ready = sem("wo_psum"), sem("wo_ready")
        rb_psum, rb_ready = sem("rot_bias_psum"), sem("rot_bias_ready")
        mask_ready, ro_psum, q_scale_ready = sem("mask_ready"), sem("row_open_psum"), sem("q_scale_ready")
        gw_psum, gw_ready = sem("gate_w_psum"), sem("gate_w_ready")
        b1_psum, b1_ready = sem("b1_psum"), sem("b1_ready")
        proj_psum, proj_ready = sem("proj_psum"), sem("proj_ready")
        v_psum, v_ready = sem("v_psum"), sem("v_ready")
        mv_ready, rstd_ready, xn_ready = sem("mv_ready"), sem("rstd_ready"), sem("xn_ready")
        xT_psum, xT_ready = sem("xT_psum"), sem("xT_ready")
        blocks_ready, scores_done, max_ready, shift_ready = (sem(n) for n in (
            "blocks_ready", "scores_done", "max_ready", "shift_ready"))
        exp_done, pT_psum, pT_ready, pv_done = (sem(n) for n in ("exp_done", "pT_psum", "pT_ready", "pv_done"))
        inv_ready, on_ready, oT_psum, oT_ready, y_psum, x_added = (sem(n) for n in (
            "inv_ready", "on_ready", "oT_psum", "oT_ready", "y_psum", "x_added"))
        logit_psum, comb_ready = sem("logit_psum"), sem("comb_ready")
        combT_psum, combT_ready, be_psum, be_added = (sem(n) for n in (
            "combT_psum", "combT_ready", "be_psum", "be_added"))
        e1_psum, e1_added = sem("expert1_psum"), sem("expert1_added")
        up_loaded = [sem("even_up_loaded"), sem("odd_up_loaded")]
        dn_loaded = [sem("even_down_loaded"), sem("odd_down_loaded")]
        x_hi_ready, x_lo_ready = sem("x_hi_ready"), sem("x_lo_ready")
        w_hi_ready, w_lo_ready = sem("w_hi_ready"), sem("w_lo_ready")
        comb_stored, comb_loaded = sem("comb_stored"), [sem("even_comb_loaded"), sem("odd_comb_loaded")]
        up_psum, silu_ready, product_ready, hid_ready, hi_ready, lo_ready, down_psum = (sem(n) for n in (
            "up_psum", "silu_ready", "product_ready", "hid_ready", "hi_ready", "lo_ready", "down_psum"))
        glu_ready, sigmoid_ready, gated_ready, over_ready, lin_ready, plain_ready = (sem(n) for n in (
            "glu_ready", "sigmoid_ready", "gated_ready", "over_ready", "lin_ready", "plain_product_ready"))
        outT_ready, out_psum, out_added = sem("outT_ready"), sem("out_psum"), sem("out_added")
        pad_ready, r1_psum, r1_ready, r2_psum, rsel_ready = (sem(n) for n in (
            "pad_ready", "r1_psum", "r1_ready", "r2_psum", "rsel_ready"))
        s3_psum, s3_ready, p3_ready, p3T_psum, p3T_ready, o3_psum = (sem(n) for n in (
            "s3_psum", "s3_ready", "p3_ready", "p3T_psum", "p3T_ready", "o3_psum"))
        dve_to_act, act_to_dve = sem("shifted_logits_ready"), sem("exp_logits_ready")
        wo_split = sem("wo_split")
        eps_added, stats_ready = sem("eps_added"), sem("stats_ready")
        v3_ready = sem("context_values_ready")
        x_final, stored = sem("x_final"), sem("stored")

        block = ctx.enter_context(nc.Block())

        def tok(ap, p=P):
            return ap.rearrange("b s d -> (b s) d").rearrange("(t p) d -> p t d", p=p)

        @block.sync
        def _(sp):
            sp.dma_start(x_tok[:, :, :], tok(a["x"])).then_inc(ld_x, 16)
            sp.dma_start(ctx_tok[:, :, 0:D], tok(a["ctx_1024"])).then_inc(ld_ctx, 16)
            sp.dma_start(w_raw[:, :, :], a["projections"]).then_inc(ld_w, 16)
            sp.dma_start(we1[:, :, :], a["L1_ffn_W_experts"].rearrange("e d f -> d e f")).then_inc(ld_late, 16)
            for half in range(2):
                sp.dma_start(ctx_dup[half * S:(half + 1) * S, :, :],
                             a["ctx_1024"].rearrange("b s d -> s b d")).then_inc(ld_dup, 16)
            states = ffn_states()
            for f in range(3):
                pair0, exp0, dma0, split0 = states[f]
                per = 2 * FFN_C[f]

                def load(e, slot):
                    after(sp, w_lo_ready, split0 + FFN_SPLITS[f] * (e - 1))
                    up, dn = w_up[:, slot, :], w_dn[:, slot, :, :]
                    if f == 0:
                        sp.dma_start(up[:, 0:2 * D], a["L0_ffn_gate_up_proj"][e, :, :]).then_inc(up_loaded[slot], 16)
                        sp.dma_start(dn[:, 0, :], a["L0_ffn_down_proj"][e, :, :]).then_inc(dn_loaded[slot], 16)
                    if f == 1:
                        sp.dma_start(up[:, 0:256], a["L2_ffn_w1"][e, :, :]).then_inc(up_loaded[slot], 16)
                        sp.dma_start(up[:, 256:512], a["L2_ffn_w2"][e, :, :]).then_inc(up_loaded[slot], 16)
                        sp.dma_start(dn, a["L2_ffn_w3"][e, :, :].rearrange("(c p) d -> p c d", p=P))\
                            .then_inc(dn_loaded[slot], 16)
                    if f == 2:
                        sp.dma_start(up, a["L3_ffn_mlp1_w"][e, :, :]).then_inc(up_loaded[slot], 16)
                        after(sp, down_psum, pair0 + per * (e - 1))
                        sp.dma_start(dn, a["L3_ffn_mlp2_w"][e, :, :].rearrange("(c p) d -> p c d", p=P))\
                            .then_inc(dn_loaded[slot], 16)

                def spread(e, slot):
                    after(sp, hid_ready, pair0 + per * (e - 1))
                    sp.dma_start(comb_row[:, slot, :], comb_dram[f][e, :].partition_broadcast(P))\
                        .then_inc(comb_loaded[slot], 16)

                after(sp, w_lo_ready, split0)
                load(0, 0)
                load(1, 1)
                if f == 1:
                    sp.wait_ge(rsel_ready, 1)
                    sp.dma_start(comb_dram[f].rearrange("e (b r) -> (e b) r", b=8),
                                 rsel[:, :, :].rearrange("p h s -> p (h s)")).then_inc(comb_stored, 16)
                else:
                    sp.wait_ge(combT_ready, (1, 0, 3)[f])
                    sp.dma_start(comb_dram[f], combT[:, :]).then_inc(comb_stored, 16)
                sp.wait_ge(comb_stored, 16 * (f + 1))
                after(sp, hid_ready, pair0)
                spread(0, 0)
                spread(1, 1)
                with sp.Fori(1, FFN_E[f] // 2) as ep:
                    for slot in range(2):
                        load(2 * ep + slot, slot)
                        spread(2 * ep + slot, slot)
            sp.wait_ge(x_final, 1)
            sp.dma_start(tok(out), x_tok[:, :, :]).then_inc(stored, 16)
            sp.wait_ge(stored, 16)

        @block.tensor
        def _(pe):
            def mm(o, l, r, start=True, stop=True):
                return nc.tensor.matmul(o, l, r, start=start, stop=stop)

            def transposes_of_x(n, src, half):
                pe.wait_ge(xn_ready, NT * n + 4 * half + 4)
                for i in range(4):
                    last = nc.tensor.transpose(bank[6 + half][:, i * P:(i + 1) * P], src[:, 4 * half + i, :], ident)
                last.then_inc(xT_psum, 4)

            pe.wait_ge(ld_const, 16)
            pe.wait_ge(ld_ctx, 16)
            for half in range(2):
                for i in range(4):
                    last = nc.tensor.transpose(bank[half][:, i * P:(i + 1) * P], ctx_tok[:, 4 * half + i, 0:D], ident)
                last.then_inc(ctxT_psum, 1)
            for half in range(2):
                transposes_of_x(0, x_norm, half)
            pe.wait_ge(ld_w, 16)
            for i, (w, rotated) in enumerate(((0, 0), (1, 0), (2, 0), (0, 1), (1, 1), (4, 0), (5, 0), (6, 0))):
                o = bank[2 + i // 4][:, (i % 4) * P:(i % 4 + 1) * P]
                if rotated:
                    last = mm(o, w_raw[:, w, :], const[:, C_ROT:C_ROT + P])
                else:
                    last = nc.tensor.transpose(o, w_raw[:, w, :], ident)
                if i % 4 == 3:
                    last.then_inc(wT_psum, 1)
            pe.wait_ge(wo_split, 1)
            for m in range(NM):
                for j2 in range(2):
                    last = nc.tensor.transpose(bank[4 + m // 2][0:64, ((m % 2) * 2 + j2) * P:((m % 2) * 2 + j2 + 1) * P],
                                               wo_by_j2[:, m, j2, :], ident)
            last.then_inc(wo_psum, 1)
            pe.wait_ge(ld_small, 16 * 4)
            pe.wait_ge(xT_ready, NT)
            for i in range(2):
                last = mm(bank[6][:, i:i + 1], const[:, C_ROT:C_ROT + P], biases[:, i:i + 1])
            last.then_inc(rb_psum, 1)
            pe.wait_ge(mask_ready, 1)
            pe.wait_ge(rb_ready, 1)
            mm(bank[6][:, 64:128], row_open[0:S, :].broadcast_to([S, P]), const[0:S, C_ID:C_ID + S]).then_inc(ro_psum, 1)
            count = [0]

            def project(w, src, half):
                n = count[0]
                after(pe, proj_ready, n - 3)
                mm(bank[n % 4][:, :], w, src[:, half * HALF:(half + 1) * HALF]).then_inc(proj_psum, 1)
                count[0] += 1

            vcount = [0]

            def values(w, src, groups):
                for g in groups:
                    n = vcount[0]
                    after(pe, v_ready, n - 1)
                    for i in range(4):
                        o, first = bank[4 + n % 2][:, i * P:(i + 1) * P], (4 * g + i) * S
                        if first + P <= T:
                            last = mm(o, src[:, first:first + P], w)
                        else:
                            mm(o[0:S, :], src[:, first:first + S], w)
                            last = mm(o[S:P, :], src[:, 0:S], w)
                    last.then_inc(v_psum, 1)
                    vcount[0] += 1

            pe.wait_ge(ctxT_ready, 2)
            pe.wait_ge(wT_ready, 2)
            for half in range(2):
                for w, src in ((wT[:, 1, :], ctxT), (wT[:, 4, :], ctxT), (wT[:, 0, :], xT), (wT[:, 3, :], xT)):
                    project(w, src, half)
            pe.wait_ge(wo_ready, 2)
            values(wT[:, 2, :], ctxT, range(4))
            pe.wait_ge(ld_late, 16 * 4)
            nc.tensor.transpose(bank[7][:, 0:8], gate_raw[:, :], const[0:8, C_ID:C_ID + 8]).then_inc(gw_psum, 1)
            pe.wait_ge(gw_ready, 1)
            for c in range(2):
                for k in range(2):
                    last = nc.tensor.transpose(bank[7][:, 16 + (2 * c + k) * 8:24 + (2 * c + k) * 8],
                                               b1_raw[:, 256 * c + k:256 * c + 256:2], const[0:8, C_ID:C_ID + 8])
            last.then_inc(b1_psum, 1)
            pe.wait_ge(q_scale_ready, 1)
            pe.wait_ge(b1_ready, 1)

            def mha(m):
                pe.wait_ge(proj_ready, count[0])
                pe.wait_ge(v_ready, vcount[0])
                if m == 3:
                    pe.wait_ge(v3_ready, 2)

                def step(b, s, steady, tau):
                    gb = B * m + b

                    def live(lag):
                        return steady or 0 <= b - lag < B
                    if live(0):
                        pe.wait_ge(blocks_ready, 2 * gb + 2)
                        after(pe, shift_ready, gb - 1)
                        if m < 2:
                            mm(bank[s][:, :], dup_bf[:, :], mask_low[:, :].unsqueeze(1).broadcast_to([P, PAIR, S]),
                               stop=False)
                        mm(bank[s][:, :], q_blk[:, s, :, :], k_blk[:, s, :, :], start=m >= 2).then_inc(scores_done, 1)
                    if live(1):
                        u = 1 - s
                        pe.wait_ge(exp_done, gb)
                        after(pe, pT_ready, gb - 1)
                        for i in range(QUAD):
                            last = nc.tensor.transpose(bank[2][:, i * P:(i + 1) * P],
                                                       probs[:, u, 2 * i:2 * i + 2, :], ident)
                        last.then_inc(pT_psum, 1)
                    if live(2):
                        pe.wait_ge(pT_ready, gb - 1)
                        after(pe, on_ready, gb - 3)
                        v = v_blk[:, m, b - 2, :].rearrange("p (i c) -> p i c", i=QUAD)
                        for i in range(QUAD):
                            last = mm(bank[4 + s][:, i * 2 * VW:(i + 1) * 2 * VW], probsT[:, s, i, :], v[:, i, :])
                        last.then_inc(pv_done, 1)
                    if live(3):
                        u = 1 - s
                        pe.wait_ge(on_ready, gb - 2)
                        after(pe, oT_ready, gb - 3)
                        nc.tensor.transpose(bank[6][:, u * P:(u + 1) * P], o_norm[:, u, :, :, :], ident)\
                            .then_inc(oT_psum, 1)
                    if s == 1 and (steady or 0 <= tau - 2 < NT):
                        pe.wait_ge(oT_ready, gb - 3)
                        after(pe, x_added, NT * m + tau - 2)
                        mm(bank[7][:, 0:D], oT[:, 0, :], w_out[:, m, 0, :], stop=False)
                        mm(bank[7][:, 0:D], oT[:, 1, :], w_out[:, m, 1, :], start=False).then_inc(y_psum, 1)

                def tile_step(tau, steady):
                    for s in range(2):
                        step(2 * tau + s, s, steady, tau)
                    if steady or 0 <= tau - 4 < NT:
                        n = NEXT_LN[m]
                        pe.wait_ge(xn_ready, NT * n + tau - 3)
                        after(pe, xT_ready, NT * n + tau - 4)
                        nc.tensor.transpose(bank[3][:, 0:P], xn_slot[:, :], ident).then_inc(xT_psum, 1)
                run_tiles(pe, tile_step)

            def router(i, w):
                for t in range(NT):
                    last = mm(bank[7][:, t * 8:(t + 1) * 8], xT[:, t * P:(t + 1) * P], w)
                last.then_inc(logit_psum, 1)

            def combine_transposed(i):
                pe.wait_ge(comb_ready, i)
                for t in range(NT):
                    last = nc.tensor.transpose(bank[6 + t // 4][0:8, (t % 4) * P:(t % 4 + 1) * P], comb[:, t, 0:8], ident)
                last.then_inc(combT_psum, 1)

            def ffn(f, state, between=None):
                chunks = FFN_C[f]
                per = 2 * chunks
                pair0, exp0, dma0, split0 = state
                acc = [False, False]
                lag = DOWN_LAG[f]

                def up(e, k, c):
                    slot, half = k // 2, k % 2
                    local = (4 * e + k) * chunks + c
                    if half == 0 and c == 0:
                        pe.wait_ge(w_lo_ready, split0 + FFN_SPLITS[f] * (2 * e + slot) + 1)
                    if f < 2:
                        after(pe, product_ready, pair0 + local - 1)
                    else:
                        after(pe, glu_ready, local - 1)
                        after(pe, over_ready, local - 1)
                    pb = 2 * ((k * chunks + c) % 2)
                    g, u = {0: (slice(0, 128), slice(128, 256)),
                            1: (slice(c * 128, c * 128 + 128), slice(256 + c * 128, 384 + c * 128)),
                            2: (slice(256 * c, 256 * c + 256, 2), slice(256 * c + 1, 256 * c + 256, 2))}[f]
                    ts = slice(half * HALF, (half + 1) * HALF)
                    for o, cols in ((bank[pb], g), (bank[pb + 1], u)):
                        hi, lo = w_up_hi[:, slot, cols], w_up_lo[:, slot, cols]
                        mm(o[:, :], lo, xT_hi[:, ts], stop=False)
                        mm(o[:, :], hi, xT_hi[:, ts], start=False, stop=False)
                        last = mm(o[:, :], hi, xT_lo[:, ts], start=False)
                    last.then_inc(up_psum, 1)

                def down(e, k, c, last_body=False):
                    local = (4 * e + k) * chunks + c
                    slot, half, u = k // 2, k % 2, (k * chunks + c) % RING
                    start = not acc[half]
                    acc[half] = True
                    stop = last_body and f < 2 and k >= 2 and c == chunks - 1
                    o = bank[6 + half][:, :]
                    if f < 2:
                        pe.wait_ge(w_lo_ready, split0 + FFN_SPLITS[f] * (2 * e + slot + 1))
                        pe.wait_ge(lo_ready, pair0 + local + 1)
                        hi, lo = w_dn_hi[:, slot, c, :], w_dn_lo[:, slot, c, :]
                        mm(o, lo, hid_hi[:, u, :], start=start, stop=False)
                        mm(o, hi, hid_hi[:, u, :], start=False, stop=False)
                        mm(o, hi, hid_lo[:, u, :], start=False, stop=stop).then_inc(down_psum, 1)
                    else:
                        if half == 0 and c == 0:
                            pe.wait_ge(dn_loaded[slot], 16 * (exp0 // 2 + 1 + e))
                        pe.wait_ge(hid_ready, pair0 + local + 1)
                        mm(o, w_dn[:, slot, c, :], hid[:, u, :], start=start, stop=stop).then_inc(down_psum, 1)

                def body(e, first, last):
                    pairs = [(k, c) for k in range(4) for c in range(chunks)]
                    for j, (k, c) in enumerate(pairs):
                        up(e, k, c)
                        if first and between:
                            between(j)
                        if j >= lag:
                            down(e, *pairs[j - lag], last)
                        elif not first:
                            down(e - 1, *pairs[j - lag])
                    if last:
                        for k, c in pairs[-lag:]:
                            down(e, k, c, last)

                for half in range(2):
                    pe.wait_ge(x_lo_ready, 2 * f + half + 1)
                run_experts(pe, f, body)
                if f == 2:
                    for half in range(2):
                        last = mm(bank[6 + half][:, :], be[:, 1, :], combT[:, half * HALF:(half + 1) * HALF], start=False)
                    last.then_inc(down_psum, 1)
                for half in range(2):
                    pe.wait_ge(outT_ready, 2 * f + half + 1)
                    for i in range(4):
                        last = nc.tensor.transpose(bank[4 + half][:, i * P:(i + 1) * P],
                                                   outT[:, (4 * half + i) * P:(4 * half + i + 1) * P], ident)
                    last.then_inc(out_psum, 1)

            states = ffn_states()

            def normed_and_projected(n, weights):
                for half in range(2):
                    transposes_of_x(n, x_norm, half)
                    pe.wait_ge(xT_ready, NT * n + 4 * half + 4)
                    for w in weights:
                        project(w, xT, half)

            mha(0)
            pe.wait_ge(xT_ready, NT * 2)
            router(0, gate_w[:, 0, :])

            for half in range(2):
                mm(bank[4 + half][:, :], wT[:, 6, :], ctxT[:, half * HALF:(half + 1) * HALF]).then_inc(k1_psum, 1)

            def values_and_weights(j):
                if j == 1:
                    pe.wait_ge(k1_ready, 2)
                    values(wT[:, 7, :], ctxT, (0, 1))
                    combine_transposed(1)
                    values(wT[:, 7, :], ctxT, (2, 3))
            ffn(0, states[0], values_and_weights)
            normed_and_projected(2, (wT[:, 5, :],))
            mha(1)
            pe.wait_ge(xT_ready, NT * 4)
            router(1, gate_w[:, 1, :])
            for half in range(2):
                project(w_qkv[:, 0:D], xT, half)
                project(w_qkv[:, D:2 * D], xT, half)
            values(w_qkv[:, 2 * D:3 * D], xT, range(4))
            combine_transposed(2)
            pe.wait_ge(combT_ready, 2)
            pe.wait_ge(v_ready, vcount[0])
            for t in range(NT):
                last = mm(bank[4 + t // 4][:, (t % 4) * D:(t % 4 + 1) * D], combT[:, t * P:(t + 1) * P], be[:, 0, :])
            last.then_inc(be_psum, 1)
            pe.wait_ge(proj_ready, count[0])
            for q in range(NT):
                pair, g = q // 2, q % 2
                after(pe, e1_added, 8 * (q - 1))
                for i in range(2):
                    t = 2 * pair + i
                    last = mm(bank[2 * i + g][:, :], xT[:, t * P:(t + 1) * P], we1[:, 4 * g:4 * g + 4, :])
                last.then_inc(e1_psum, 1)
            pe.wait_ge(e1_added, 8 * NT)
            mha(2)
            mha(3)
            pe.wait_ge(xT_ready, NT * 6)
            for half in range(2):
                mm(bank[4 + half][:, :], rw1[:, :], xT[:, half * HALF:(half + 1) * HALF]).then_inc(r1_psum, 1)

            pe.wait_ge(pad_ready, 8)
            pe.wait_ge(r1_ready, 2)
            for hf in range(2):
                for i in range(8):
                    last = mm(bank[6][:, hf * S:(hf + 1) * S], rw2_pad[:, i, :],
                              r1[:, (8 * hf + i) * S:(8 * hf + i + 1) * S], start=i == 0, stop=i == 7)
            last.then_inc(r2_psum, 1)
            ffn(1, states[1])
            for half in range(2):
                transposes_of_x(6, x_norm, half)
                pe.wait_ge(xT_ready, NT * 6 + 4 * half + 4)
                for i in range(4):
                    t = 4 * half + i
                    last = mm(bank[half][:, i * P:(i + 1) * P], xT[:, t * P:(t + 1) * P], ctxT[:, t * P:(t + 1) * P])
                last.then_inc(s3_psum, 1)
            for g in range(2):
                pe.wait_ge(p3_ready, g + 1)
                for i in range(4):
                    last = nc.tensor.transpose(bank[2 + g][:, i * P:(i + 1) * P], p3[:, 4 * g + i, :], ident)
                last.then_inc(p3T_psum, 1)
                pe.wait_ge(p3T_ready, g + 1)
                for i in range(4):
                    t = 4 * g + i
                    last = mm(bank[(4, 5, 0, 1)[t // 2]][:, (t % 2) * (D + 1):(t % 2 + 1) * (D + 1)], p3T[:, t, :], ctx_tok[:, t, :])
                    if i % 2:
                        last.then_inc(o3_psum, 1)
            for half in range(2):
                transposes_of_x(7, x_rms, half)
            pe.wait_ge(xT_ready, NT * 8)
            router(2, gate_w[:, 2, :])
            ffn(2, states[2], lambda j: combine_transposed(3) if j == 1 else None)

        @block.scalar
        def _(act):
            done = [0]

            def link(ins):
                done[0] += 1
                ins.then_inc(act_done, 1)
                act.wait_ge(act_done, done[0])

            act.dma_start(const[:, :], a["shape_constants"]).then_inc(ld_const, 16)
            act.dma_start(biases[:, 0:6], a["bias_columns"]).then_inc(ld_small, 16)
            act.dma_start(row_pack[:, :], a["rows"].partition_broadcast(P)).then_inc(ld_small, 16)
            for half in range(2):
                act.dma_start(mask_i[half * S:(half + 1) * S, :], a["mask_1x1xSxS2_ik0"][0, 0, :, :])\
                    .then_inc(ld_small, 16)
            act.dma_start(bo_row[64:65, :, :], a["output_biases"].rearrange("(o l d) -> o l d", o=1, d=D))\
                .then_inc(ld_late, 16)
            act.dma_start(by_expert[:, :], a["by_expert"]).then_inc(ld_late, 16)
            act.dma_start(by_feature[:, 8:8 + FEATURE_N], a["by_feature"]).then_inc(ld_late, 16)

            def xT_halves(n):
                for half in range(2):
                    act.wait_ge(xT_psum, NT * n + 4 * half + 4)
                    act.copy(xT[:, half * HALF:(half + 1) * HALF], bank[6 + half][:, :]).then_inc(xT_ready, 4)

            for half in range(2):
                act.wait_ge(ctxT_psum, half + 1)
                act.copy(ctxT[:, half * HALF:(half + 1) * HALF], bank[half][:, :]).then_inc(ctxT_ready, 1)
            xT_halves(0)
            for i in range(2):
                act.wait_ge(wT_psum, i + 1)
                act.copy(wT[:, 4 * i:4 * i + 4, :], bank[2 + i][:, :].rearrange("p (i d) -> p i d", i=4))\
                    .then_inc(wT_ready, 1)
            act.wait_ge(ld_small, 16 * 4)
            act.activation(gates[:, :], gates[:, :], ACT.Tanh).then_inc(gates_ready, 1)
            act.wait_ge(wo_psum, 1)
            act.wait_ge(gates_ready, 1)
            act.wait_ge(consts_set, 1)
            act.wait_ge(ld_late, 16 * 4)
            for m in range(NM):
                g = gates[0:64, MHA_GATE[m]:MHA_GATE[m] + 1]
                src = bank[4 + m // 2][0:64, (m % 2) * 256:(m % 2) * 256 + 256].rearrange("p (j d) -> p j d", j=2)
                ins = act.activation(w_out[0:64, m, :, :], src, ACT.Copy, scale=g)
                if m == 1:
                    ins.then_inc(wo_ready, 1)
            ins.then_inc(wo_ready, 1)
            for i, m in enumerate((0, 1, 3)):
                g = gates[64:65, MHA_GATE[m]:MHA_GATE[m] + 1]
                link(act.activation(w_out[64:65, m, 0, :], bo_row[64:65, i, :], ACT.Copy, scale=g))
            act.wait_ge(gw_psum, 1)
            act.copy(gate_w[:, 0, :], bank[7][:, 0:8]).then_inc(gw_ready, 1)

            def mha(m):
                def step(b, s, steady, tau):
                    gb = B * m + b

                    def live(lag):
                        return steady or 0 <= b - lag < B
                    if live(1):
                        u = 1 - s
                        act.wait_ge(pT_psum, gb)
                        after(act, pv_done, gb - 2)
                        act.copy(probsT[:, u, :, :], bank[2][:, :].rearrange("p (i q) -> p i q", i=QUAD))\
                            .then_inc(pT_ready, 1)
                    if live(0):
                        act.wait_ge(shift_ready, gb + 1)
                        after(act, pT_psum, gb - 1)
                        act.activation(probs[:, s, :, :], shifted[:, s, :, :], ACT.Exp).then_inc(exp_done, 1)
                    if live(3):
                        u = 1 - s
                        act.wait_ge(oT_psum, gb - 2)
                        if s == 1:
                            after(act, y_psum, NT * m + tau - 1)
                        act.copy(oT[0:64, :, u * S:(u + 1) * S],
                                 bank[6][0:64, u * P:(u + 1) * P].rearrange("p (j q) -> p j q", j=2)).then_inc(oT_ready, 1)

                def tile_step(tau, steady):
                    for s in range(2):
                        step(2 * tau + s, s, steady, tau)
                    if steady or 0 <= tau - 4 < NT:
                        act.wait_ge(xT_psum, NT * NEXT_LN[m] + tau - 3)
                        act.copy(xT[:, bass.ds((tau - 4) * P, P)], bank[3][:, 0:P]).then_inc(xT_ready, 1)
                run_tiles(act, tile_step)

            def ffn(f, state, router):
                chunks = FFN_C[f]
                per = 2 * chunks
                pair0, exp0, dma0, split0 = state

                def split_up(e, slot):
                    act.wait_ge(up_loaded[slot], dma0 + 16 * UP_DMA[f] * (e + 1))
                    after(act, up_psum, pair0 + per * (2 * e + slot - 1))
                    n = 256 if f == 0 else 512
                    act.copy(w_up_hi[:, slot, 0:n], w_up[:, slot, 0:n]).then_inc(w_hi_ready, 1)

                def split_down(e, slot):
                    act.wait_ge(dn_loaded[slot], 16 * (exp0 // 2 + 1 + e))
                    after(act, down_psum, pair0 + per * (2 * e + slot - 1))
                    act.copy(w_dn_hi[:, slot, 0:chunks, :], w_dn[:, slot, 0:chunks, :]).then_inc(w_hi_ready, 1)

                def leading(local, u):
                    act.wait_ge(hid_ready, pair0 + local + 1)
                    after(act, down_psum, pair0 + local - RING + 1)
                    act.copy(hid_hi[:, u, :], hid[:, u, :]).then_inc(hi_ready, 1)

                def body(e, first, last):
                    for j in range(4 * chunks):
                        local = 4 * chunks * e + j
                        n = pair0 + local
                        u, ej, slot = j % 2, j % per, j // per
                        act.wait_ge(up_psum, n + 1)
                        if f < 2:
                            after(act, product_ready, n - 1)
                            act.activation(act_out[:, u, :], bank[2 * u][:, :], ACT.Silu).then_inc(silu_ready, 1)
                            if not (first and j == 0):
                                leading(local - 1, (j - 1) % RING)
                        else:
                            c = j % chunks
                            act.wait_ge(glu_ready, local + 1)
                            after(act, lin_ready, local - 1)
                            after(act, gated_ready, local - 1)
                            act.activation(act_out[:, u, :], glu[:, u, :], ACT.Sigmoid, scale=1.702)\
                                .then_inc(sigmoid_ready, 1)
                            act.activation(over[:, u, :], bank[2 * u + 1][:, :], ACT.Relu, scale=-1.0,
                                           bias=b1_col[:, c, 1, bass.ds(2 * e + slot, 1)]).then_inc(over_ready, 1)
                            act.wait_ge(over_ready, local + 1)
                            after(act, plain_ready, local - 1)
                            act.activation(lin[:, u, :], over[:, u, :], ACT.Relu, scale=-1.0, bias=fourteen[:, :])\
                                .then_inc(lin_ready, 1)
                        if ej == SPLIT_UP_AT[f] and not (last and slot):
                            split_up(e + slot, 1 - slot)
                        if f < 2 and ej == per - 1 and not (last and slot):
                            split_down(e + slot, 1 - slot)
                    if last and f < 2:
                        leading(4 * chunks * e + 4 * chunks - 1, RING - 1)

                for half in range(2):
                    ts = slice(half * HALF, (half + 1) * HALF)
                    act.wait_ge(xT_ready, NT * (2, 6, 8)[f])
                    act.copy(xT_hi[:, ts], xT[:, ts]).then_inc(x_hi_ready, 1)
                split_up(0, 0)
                if f < 2:
                    split_down(0, 0)
                router()
                run_experts(act, f, body)
                for half in range(2):
                    act.wait_ge(down_psum, pair0 + per * FFN_E[f] + (1 if f == 2 else 0))
                    act.copy(outT[:, half * HALF:(half + 1) * HALF], bank[6 + half][:, :]).then_inc(outT_ready, 1)

            def exp_of_logits(k):
                act.wait_ge(dve_to_act, k)
                act.activation(logits[:, :, :], logits[:, :, :], ACT.Exp).then_inc(act_to_dve, 1)

            def combT_halves(i):
                act.wait_ge(combT_psum, i)
                for g in range(2):
                    ins = act.copy(combT[:, g * HALF:(g + 1) * HALF], bank[6 + g][0:8, :])
                ins.then_inc(combT_ready, 1)

            def router_2():
                act.wait_ge(dve_to_act, 3)
                act.activation(rp[:, :, :], rwork[:, :, :], ACT.Exp).then_inc(act_to_dve, 1)

            def router_of(call, transposed):
                def router():
                    exp_of_logits(call)
                    combT_halves(transposed)
                return router

            states = ffn_states()
            def biased(n, dst, half, b_col):
                act.wait_ge(proj_psum, n + 1)
                act.activation(dst[:, half * HALF:(half + 1) * HALF], bank[n % 4][:, :], ACT.Identity, bias=b_col)\
                    .then_inc(proj_ready, 1)

            mha(0)

            def router_0():
                exp_of_logits(1)
                for half in range(2):
                    act.wait_ge(k1_psum, half + 1)
                    act.activation(kT[:, 1, half * HALF:(half + 1) * HALF], bank[4 + half][:, :], ACT.Identity,
                                   bias=bk1).then_inc(k1_ready, 1)
                combT_halves(1)
            ffn(0, states[0], router_0)
            xT_halves(2)
            biased(8, qT, 0, bq1)
            biased(9, qT, 1, bq1)
            mha(1)
            exp_of_logits(2)
            for half in range(2):
                biased(10 + 2 * half, qT, half, bqs)
                biased(11 + 2 * half, kT[:, 0, :], half, bks)
            combT_halves(2)
            mha(2)
            mha(3)
            for half in range(2):
                act.wait_ge(r1_psum, half + 1)
                act.activation(r1[:, half * HALF:(half + 1) * HALF], bank[4 + half][:, :], ACT.Silu).then_inc(r1_ready, 1)
            ffn(1, states[1], router_2)
            xT_halves(6)
            for g in range(2):
                act.wait_ge(s3_ready, g + 1)
                for half in range(2):
                    rows = slice(half * S, (half + 1) * S)
                    ins = act.activation(p3[rows, 4 * g:4 * g + 4, half * S:(half + 1) * S],
                                         s3[rows, 4 * g:4 * g + 4, :], ACT.Exp, scale=float(1.0 / np.sqrt(D)))
                ins.then_inc(p3_ready, 1)
                act.wait_ge(p3T_psum, g + 1)
                act.copy(p3T[:, 4 * g:4 * g + 4, :], bank[2 + g][:, :].rearrange("p (i q) -> p i q", i=4))\
                    .then_inc(p3T_ready, 1)
            xT_halves(7)
            ffn(2, states[2], router_of(4, 3))

        @block.gpsimd
        def _(pool):
            done = [0]

            def link(ins):
                done[0] += 1
                ins.then_inc(pool_done, 1)
                pool.wait_ge(pool_done, done[0])

            link(pool.memset(minus_half[:, :], -0.5))
            link(pool.memset(eps_col[:, :], LN_EPS))
            link(pool.memset(fourteen[:, :], 14.0))
            link(pool.memset(oT[64:65, :, :], 1.0))
            link(pool.memset(ctx_tok[:, :, D:D + 1], 1.0))
            link(pool.memset(o_norm[:, :, :, :, :], 0.0))
            link(pool.memset(p3[:, :, :], 0.0))
            link(pool.memset(rw2_pad[:, :, :], 0.0))
            pool.memset(w_out[64:65, :, :, :], 0.0).then_inc(consts_set, 1)
            pool.wait_ge(consts_set, 1)

            def rstd_of(n):
                for half in range(2):
                    ts = slice(4 * half, 4 * half + 4)
                    pool.wait_ge(mv_ready, NT * n + 4 * half + 4)
                    link(pool.tensor_scalar(var_eps[:, ts], mv[:, ts, 1], LN_EPS, None, ALU.add))
                    pool.tensor_tensor(rstd[:, ts], var_eps[:, ts], minus_half[:, ts], ALU.pow).then_inc(rstd_ready, 4)

            def mha(m, q_src, k_src, ready):
                def step(b, s):
                    gb = B * m + b
                    cols = bass.ds(b * S, S)
                    after(pool, scores_done, gb - 1)
                    pool.tensor_tensor(q_blk[:, s, :, :], q_src[:, cols].unsqueeze(1).broadcast_to([P, 2, S]),
                                       q_scale[:, 0 if m < 2 else 1, :, :], ALU.mult).then_inc(blocks_ready, 1)
                    pool.tensor_tensor(k_blk[:, s, :, :], k_src[:, cols].unsqueeze(1).broadcast_to([P, PAIR, S]),
                                       const[:, C_PM:C_PM + PAIR].unsqueeze(2).broadcast_to([P, PAIR, S]), ALU.mult)\
                        .then_inc(blocks_ready, 1)

                def tile_step(tau, steady):
                    if steady or tau < NT:
                        step(2 * tau, 0)
                    if steady or 0 <= tau - 4 < NT:
                        pool.wait_ge(mv_ready, NT * NEXT_LN[m] + tau - 3)
                        pool.tensor_tensor(var_slot[:, :], mv_slot[:, 1:2], eps_col[:, :], ALU.add).then_inc(eps_added, 1)
                        pool.wait_ge(eps_added, NT * m + tau - 3)
                        pool.tensor_tensor(rstd_slot[:, :], var_slot[:, :], minus_half[:, 0:1], ALU.pow)\
                            .then_inc(rstd_ready, 1)
                    if steady or tau < NT:
                        step(2 * tau + 1, 1)
                ready(0)
                for tau in range(FILL):
                    tile_step(tau, False)
                ready(1)
                with pool.Fori(FILL, NT) as tau:
                    tile_step(tau, True)
                for tau in range(NT, NT + DRAIN):
                    tile_step(tau, False)

            def ffn(f, state):
                chunks = FFN_C[f]
                per = 2 * chunks
                pair0, exp0, dma0, split0 = state

                def weights_of(slot, half):
                    row = comb_row[:, slot, :]
                    if f == 0:
                        return row[:, half * HALF:(half + 1) * HALF].rearrange("p (b s) -> p b s", s=S)
                    return row.rearrange("p (b h s) -> p b h s", b=8, h=2)[:, :, half, :]

                def split_up(e, slot, n):
                    pool.wait_ge(w_hi_ready, split0 + n)
                    m = 256 if f == 0 else 512
                    pool.tensor_tensor(w_up_lo[:, slot, 0:m], w_up[:, slot, 0:m], w_up_hi[:, slot, 0:m].bitcast(F32),
                                       ALU.subtract).then_inc(w_lo_ready, 1)

                def split_down(e, slot, n):
                    pool.wait_ge(w_hi_ready, split0 + n)
                    pool.tensor_tensor(w_dn_lo[:, slot, 0:chunks, :], w_dn[:, slot, 0:chunks, :],
                                       w_dn_hi[:, slot, 0:chunks, :].bitcast(F32), ALU.subtract).then_inc(w_lo_ready, 1)

                def body(e, first, last):
                    for j in range(4 * chunks):
                        local = 4 * chunks * e + j
                        n = pair0 + local
                        u, ej, slot = j % 2, j % per, j // per
                        half = ej // chunks
                        if f < 2:
                            if ej == 0:
                                pool.wait_ge(comb_loaded[slot], 16 * (exp0 // 2 + 1 + e))
                            pool.wait_ge(product_ready, n + 1)
                            after(pool, lo_ready, n - RING + 1)
                            pool.tensor_tensor(hid[:, j % RING, :].rearrange("p (b s) -> p b s", s=S),
                                               product[:, u, :].rearrange("p (b s) -> p b s", s=S),
                                               weights_of(slot, half), ALU.mult).then_inc(hid_ready, 1)
                        else:
                            pool.wait_ge(sigmoid_ready, local + 1)
                            after(pool, plain_ready, local - 1)
                            pool.tensor_tensor(gated[:, u, :], glu[:, u, :], act_out[:, u, :], ALU.mult)\
                                .then_inc(gated_ready, 1)
                        before = FFN_SPLITS[f] * (2 * e + slot + 1)
                        if ej == SPLIT_UP_AT[f] and not (last and slot):
                            split_up(e + slot, 1 - slot, before + 1)
                        if f < 2 and ej == per - 1 and not (last and slot):
                            split_down(e + slot, 1 - slot, before + 2)

                split_up(0, 0, 1)
                if f < 2:
                    split_down(0, 0, 2)
                run_experts(pool, f, body)

            states = ffn_states()

            def ready_by_count(first, second, own_keys=False):
                def wait(half):
                    pool.wait_ge(proj_ready, (first, second)[half])
                    pool.wait_ge(q_scale_ready, 1)
                    if own_keys:
                        pool.wait_ge(k1_ready, 2)
                return wait
            rstd_of(0)
            pool.memset(v_blk[:, :, :, :], 0.0).then_inc(v_cleared, 1)
            pool.wait_ge(v_cleared, 1)
            ones = v_blk[:, :, :, :].rearrange("p m b (i j c) -> p (m b i) j c", i=QUAD, j=2)
            for j in range(2):
                pool.memset(ones[j * S:(j + 1) * S, :, j, VW - 1:VW], 1.0).then_inc(v_cleared, 1)
                pool.wait_ge(v_cleared, j + 2)
            pool.wait_ge(ld_dup, 32)
            for j in range(2):
                rows = slice(j * S, (j + 1) * S)
                dst = v_blk[rows, 3, :, :].rearrange("p b (i j c) -> p b i j c", i=QUAD, j=2)[:, :, :, j, 0:2 * DK]
                src = ctx_dup[rows, :, :].rearrange("p b (i j c) -> p b i j c", i=QUAD, j=2)[:, :, :, j, :]
                pool.tensor_copy(dst, src).then_inc(v3_ready, 1)
                pool.wait_ge(v3_ready, j + 1)
            pool.wait_ge(ld_late, 16 * 4)
            for i in range(8):
                pool.tensor_copy(rw2_pad[:, i, i::8], rw2[:, :]).then_inc(pad_ready, 1)
            mha(0, qT, kT[:, 0, :], ready_by_count(4, 8))
            ffn(0, states[0])
            rstd_of(2)
            mha(1, qT, kT[:, 1, :], ready_by_count(9, 10, True))
            mha(2, qT, kT[:, 0, :], ready_by_count(12, 14))
            mha(3, xT, ctxT, lambda half: pool.wait_ge(xT_ready, NT * 5))
            ffn(1, states[1])
            rstd_of(6)
            rstd_of(7)
            for half in range(2):
                ts = slice(4 * half, 4 * half + 4)
                pool.wait_ge(mv_ready, 8 * NT + 4 * half + 4)
                link(pool.tensor_tensor(var_eps[:, ts], mv[:, ts, 0], mv[:, ts, 0], ALU.mult))
                link(pool.tensor_tensor(var_eps[:, ts], var_eps[:, ts], mv[:, ts, 1], ALU.add))
                link(pool.tensor_scalar(var_eps[:, ts], var_eps[:, ts], LN_EPS, None, ALU.add))
                pool.tensor_tensor(rstd[:, ts], var_eps[:, ts], minus_half[:, ts], ALU.pow).then_inc(rstd_ready, 4)

            ffn(2, states[2])

        @block.vector
        def _(dve):
            v = nc.vector
            done = [0]

            def link(ins):
                done[0] += 1
                ins.then_inc(dve_done, 1)
                dve.wait_ge(dve_done, done[0])

            count = [0]

            def rotated(dst, half, b_col, r_col):
                def table(c):
                    return const[:, c:c + S].unsqueeze(1).broadcast_to([P, HALF // S, S])

                def split(ap):
                    return ap.rearrange("p (b s) -> p b s", s=S)
                d = dst[:, half * HALF:(half + 1) * HALF]
                n = count[0]
                dve.wait_ge(proj_psum, n + 1)
                link(v.scalar_tensor_tensor(split(d), split(bank[n % 4][:, :]), b_col, table(C_COS), ALU.add, ALU.mult))
                dve.wait_ge(proj_psum, n + 2)
                link(v.scalar_tensor_tensor(split(rot_tmp[:, :]), split(bank[(n + 1) % 4][:, :]), r_col, table(C_SIN),
                                            ALU.add, ALU.mult))
                v.tensor_tensor(d, d, rot_tmp[:, :], ALU.add).then_inc(proj_ready, 2)
                count[0] += 2

            vcount = [0]

            def values(m, bias_i):
                dve.wait_ge(v_cleared, 3)
                for g in range(4):
                    n = vcount[0]
                    dve.wait_ge(v_psum, n + 1)
                    src = bank[4 + n % 2][:, :].rearrange("p (b i j c) -> p b i j c", b=4, i=QUAD, j=2)
                    for j in range(2):
                        rows = slice(j * S, (j + 1) * S)
                        bias = v_bias[rows, bias_i, :].rearrange("p (i j c) -> p i j c", i=QUAD, j=2)[:, :, j, :]
                        parts = ((0, 4, 4 * g),) if j == 0 else ((0, 4, 4 * g + 1),) if g < 3 else ((0, 3, 13), (3, 4, 0))
                        for i0, i1, b0 in parts:
                            dst = v_blk[rows, m, b0:b0 + i1 - i0, :].rearrange("p b (i j c) -> p b i j c", i=QUAD, j=2)
                            ins = v.tensor_tensor(dst[:, :, :, j, 0:2 * DK], src[rows, i0:i1, :, j, :],
                                                  bias.unsqueeze(1).broadcast_to([S, i1 - i0, QUAD, 2 * DK]), ALU.add)
                    ins.then_inc(v_ready, 1)
                    vcount[0] += 1

            def statistics(n, src, half):
                for t in range(4 * half, 4 * half + 4):
                    ins = v.bn_stats(stats[:, t, :], src[:, t, :])
                link(ins)
                for t in range(4 * half, 4 * half + 4):
                    v.bn_aggr(mv[:, t, :], stats[:, t, :]).then_inc(mv_ready, 1)

            def normed(n, half, counted=True):
                dve.wait_ge(mv_ready, NT * n + 4 * half + 4)
                dve.wait_ge(rstd_ready, NT * n + 4 * half + 4)
                for t in range(4 * half, 4 * half + 4):
                    ins = v.tensor_scalar(x_norm[:, t, :], x_tok[:, t, :], mv[:, t, 0:1], rstd[:, t:t + 1],
                                          ALU.subtract, ALU.mult)
                    if counted:
                        ins.then_inc(xn_ready, 1)
                if not counted:
                    link(ins)

            def layer_norm(n):
                statistics(n, x_tok, 0)
                statistics(n, x_tok, 1)
                normed(n, 0)
                normed(n, 1)

            def mha(m):
                def step(b, s, steady):
                    gb = B * m + b

                    def live(lag):
                        return steady or 0 <= b - lag < B
                    if live(0):
                        scores = bank[s][:, :].rearrange("p (h k) -> p h k", h=PAIR)
                        dve.wait_ge(scores_done, gb + 1)
                        v.reduce_max(row_max[:, s, :], scores, AX).then_inc(max_ready, 1)
                        dve.wait_ge(max_ready, gb + 1)
                        after(dve, exp_done, gb - 1)
                        v.tensor_tensor(shifted[:, s, :, :], scores,
                                        row_max[:, s, :].unsqueeze(2).broadcast_to([P, PAIR, S]), ALU.subtract)\
                            .then_inc(shift_ready, 1)

                def normalise(b, s, steady):
                    gb = B * m + b
                    if steady or 0 <= b - 2 < B:
                        dve.wait_ge(pv_done, gb - 1)
                        o = bank[4 + s][:, 0:VB].rearrange("p (h c) -> p h c", h=PAIR)
                        v.reciprocal(inv_sum[:, s, :], o[:, :, VW - 1]).then_inc(inv_ready, 1)
                        dve.wait_ge(inv_ready, gb - 1)
                        after(dve, oT_psum, gb - 3)
                        for j2 in range(2):
                            rows = slice(j2 * S, (j2 + 1) * S)
                            ins = v.tensor_tensor(o_norm[rows, s, 0, :, :], o[rows, :, j2 * DK:(j2 + 1) * DK],
                                                  inv_sum[rows, s, :].unsqueeze(2).broadcast_to([S, PAIR, DK]), ALU.mult)
                        ins.then_inc(on_ready, 1)

                def tile_step(tau, steady):
                    def live(lag):
                        return steady or 0 <= tau - lag < NT
                    n = NEXT_LN[m]
                    if live(3):
                        dve.wait_ge(x_added, NT * m + tau - 2)
                    step(2 * tau, 0, steady)
                    if live(3):
                        v.bn_stats(stats_slot[:, :], x_tok[:, bass.ds(tau - 3, 1), :].rearrange("p o d -> p (o d)"))\
                            .then_inc(stats_ready, 1)
                    normalise(2 * tau, 0, steady)
                    if live(4):
                        dve.wait_ge(rstd_ready, NT * n + tau - 3)
                        dve.wait_ge(xT_psum, NT * n + tau - 4)
                        v.tensor_scalar(xn_slot[:, :], x_tok[:, bass.ds(tau - 4, 1), :].rearrange("p o d -> p (o d)"),
                                        mv_slot[:, 0:1], rstd_slot[:, :], ALU.subtract, ALU.mult).then_inc(xn_ready, 1)
                    if live(3):
                        dve.wait_ge(stats_ready, NT * m + tau - 2)
                        dve.wait_ge(xn_ready, NT * n + tau - 3)
                    step(2 * tau + 1, 1, steady)
                    if live(3):
                        v.bn_aggr(mv_slot[:, :], stats_slot[:, :]).then_inc(mv_ready, 1)
                    normalise(2 * tau + 1, 1, steady)
                    if live(2):
                        xs = x_tok[:, bass.ds(tau - 2, 1), :].rearrange("p o d -> p (o d)")
                        dve.wait_ge(y_psum, NT * m + tau - 1)
                        v.tensor_tensor(xs, xs, bank[7][:, 0:D], ALU.add).then_inc(x_added, 1)
                run_tiles(dve, tile_step)
                dve.wait_ge(xn_ready, NT * (NEXT_LN[m] + 1))

            def top2_router(i, k, bias_i):
                dve.wait_ge(logit_psum, i + 1)
                src = bank[7][:, 0:NT * 8].rearrange("p (t e) -> p t e", t=NT)
                if bias_i is None:
                    link(v.tensor_copy(logits[:, :, :], src))
                else:
                    link(v.tensor_tensor(logits[:, :, :], src,
                                         gate_b[:, bias_i, :].unsqueeze(1).broadcast_to([P, NT, 8]), ALU.add))
                mine = logits[:, :, :].unsqueeze(3).broadcast_to([P, NT, 8, 8])
                other = logits[:, :, :].unsqueeze(2).broadcast_to([P, NT, 8, 8])
                tri = const[:, C_TRI:C_TRI + 64].rearrange("p (e f) -> p e f", e=8).unsqueeze(1).broadcast_to([P, NT, 8, 8])
                v.tensor_tensor(gt[:, :, :, :], other, mine, ALU.is_gt)
                v.reduce_max(e_max[:, :], logits[:, :, :], AX)
                link(v.tensor_tensor(eq[:, :, :, :], other, mine, ALU.is_equal))
                v.tensor_tensor(logits[:, :, :], logits[:, :, :], e_max[:, :].unsqueeze(2).broadcast_to([P, NT, 8]),
                                ALU.subtract).then_inc(dve_to_act, 1)
                link(v.tensor_tensor(eq[:, :, :, :], eq[:, :, :, :], tri, ALU.mult))
                link(v.tensor_tensor(gt[:, :, :, :], gt[:, :, :, :], eq[:, :, :, :], ALU.add))
                link(v.reduce_sum(rank[:, :, :], gt[:, :, :, :], AX))
                link(v.tensor_scalar(top[:, :, :], rank[:, :, :], 1.5, None, ALU.is_lt))
                dve.wait_ge(act_to_dve, k)

                def share(eps):
                    link(v.reduce_sum(e_sum[:, :], logits[:, :, :], AX))
                    if eps:
                        link(v.tensor_scalar(e_sum[:, :], e_sum[:, :], eps, None, ALU.add))
                    link(v.reciprocal(e_sum[:, :], e_sum[:, :]))
                    link(v.tensor_tensor(logits[:, :, :], logits[:, :, :],
                                         e_sum[:, :].unsqueeze(2).broadcast_to([P, NT, 8]), ALU.mult))
                if i < 2:
                    share(0)
                link(v.tensor_tensor(logits[:, :, :], logits[:, :, :], top[:, :, :], ALU.mult))
                if i == 0:
                    share(1e-9)
                    share(1e-9)
                if i == 2:
                    share(0)
                gate = gates[:, (4, 5, 7)[i]:(4, 5, 7)[i] + 1]
                ins = v.tensor_scalar(comb[:, :, 0:8], logits[:, :, :], gate, None, ALU.mult)
                ins.then_inc(comb_ready, 1)
                dve.wait_ge(comb_ready, i + 1)

            def add_biases(i):
                dve.wait_ge(be_psum, i)
                for g in range(2):
                    xs = x_tok[:, 4 * g:4 * g + 4, :]
                    ins = v.tensor_tensor(xs, xs, bank[4 + g][:, :].rearrange("p (t d) -> p t d", t=4), ALU.add)
                ins.then_inc(be_added, 1)
                dve.wait_ge(be_added, i)

            def ffn(f, state, router):
                chunks = FFN_C[f]
                per = 2 * chunks
                pair0, exp0, dma0, split0 = state

                def trailing(local, u):
                    dve.wait_ge(hi_ready, pair0 + local + 1)
                    after(dve, down_psum, pair0 + local - RING + 1)
                    v.tensor_tensor(hid_lo[:, u, :], hid[:, u, :], hid_hi[:, u, :].bitcast(F32), ALU.subtract)\
                        .then_inc(lo_ready, 1)

                def weighted(e, local, j):
                    u, ej, slot = j % 2, j % per, j // per
                    half = ej // chunks
                    dve.wait_ge(gated_ready, local + 1)
                    dve.wait_ge(lin_ready, local + 1)
                    after(dve, hid_ready, pair0 + local - 1)
                    v.scalar_tensor_tensor(product[:, u, :], lin[:, u, :], -6.0, gated[:, u, :], ALU.add, ALU.mult)\
                        .then_inc(plain_ready, 1)
                    if ej == 0:
                        dve.wait_ge(comb_loaded[slot], 16 * (exp0 // 2 + 1 + e))
                    dve.wait_ge(plain_ready, local + 1)
                    after(dve, down_psum, pair0 + local - RING + 1)
                    v.tensor_tensor(hid[:, j % RING, :], product[:, u, :],
                                    comb_row[:, slot, half * HALF:(half + 1) * HALF], ALU.mult).then_inc(hid_ready, 1)

                def body(e, first, last):
                    pairs = 4 * chunks
                    for j in range(pairs):
                        local = pairs * e + j
                        n = pair0 + local
                        u = j % 2
                        if f < 2:
                            dve.wait_ge(silu_ready, n + 1)
                            after(dve, hid_ready, n - 1)
                            v.tensor_tensor(product[:, u, :], act_out[:, u, :], bank[2 * u + 1][:, :], ALU.mult)\
                                .then_inc(product_ready, 1)
                            if not (first and j == 0):
                                trailing(local - 1, (j - 1) % RING)
                        else:
                            ej, slot = j % per, j // per
                            dve.wait_ge(up_psum, n + 1)
                            after(dve, gated_ready, local - 1)
                            v.tensor_scalar(glu[:, u, :], bank[2 * u][:, :],
                                            b1_col[:, j % chunks, 0, bass.ds(2 * e + slot, 1)], 7.0, ALU.add, ALU.min)\
                                .then_inc(glu_ready, 1)
                            if j > 0:
                                weighted(e, local - 1, j - 1)
                            elif not first:
                                weighted(e - 1, local - 1, pairs - 1)
                    if last:
                        if f < 2:
                            trailing(pairs * e + pairs - 1, RING - 1)
                        else:
                            weighted(e, pairs * e + pairs - 1, pairs - 1)

                for half in range(2):
                    ts = slice(half * HALF, (half + 1) * HALF)
                    dve.wait_ge(x_hi_ready, 2 * f + half + 1)
                    v.tensor_tensor(xT_lo[:, ts], xT[:, ts], xT_hi[:, ts].bitcast(F32), ALU.subtract)\
                        .then_inc(x_lo_ready, 1)
                router()
                run_experts(dve, f, body)
                for half in range(2):
                    dve.wait_ge(out_psum, 2 * f + half + 1)
                    xs = x_tok[:, 4 * half:4 * half + 4, :]
                    v.tensor_tensor(xs, xs, bank[4 + half][:, :].rearrange("p (t d) -> p t d", t=4), ALU.add)\
                        .then_inc(out_added, 1)
                dve.wait_ge(out_added, 2 * (f + 1))

            states = ffn_states()
            dve.wait_ge(ld_x, 16)
            layer_norm(0)
            dve.wait_ge(ld_const, 16)
            v.tensor_copy(dup_bf[:, :], const[:, C_DUP:C_DUP + P])
            dve.wait_ge(ld_w, 16)
            for m, w in enumerate((w_raw[:, 3, :], w_raw[:, 7, :], ident, w_raw[:, 8, :])):
                ins = v.tensor_copy(wo_by_j2[:, m, :, :].rearrange("n j (p d) -> n j p d", d=DK),
                                    w.rearrange("n (p j d) -> n j p d", j=2, d=DK))
            ins.then_inc(wo_split, 1)
            dve.wait_ge(ld_small, 16 * 4)
            link(v.tensor_scalar(mask_open[:, :], mask_i[:, :], 0, None, ALU.not_equal))
            v.tensor_scalar(mask_low[:, :], mask_open[:, :], -1.0, BIG, ALU.add, ALU.mult)
            v.reduce_max(row_open[:, :], mask_open[:, :], AX).then_inc(mask_ready, 1)
            dve.wait_ge(rb_psum, 1)
            v.tensor_copy(biases[:, 6:8], bank[6][:, 0:2]).then_inc(rb_ready, 1)
            dve.wait_ge(rb_ready, 1)
            dve.wait_ge(ro_psum, 1)
            for j2 in range(2):
                v.tensor_scalar(q_scale[:, 0, j2, :], bank[6][:, 64:128], const[:, C_JM + j2:C_JM + j2 + 1], None, ALU.mult)
            for j2 in range(2):
                ins = v.tensor_copy(q_scale[:, 1, j2, :], const[:, C_JM + j2:C_JM + j2 + 1].broadcast_to([P, S]))
            ins.then_inc(q_scale_ready, 1)
            for half in range(2):
                rotated(kT[:, 0, :], half, bk0, rk0)
                rotated(qT, half, bq0, rq0)
            values(0, 0)
            dve.wait_ge(ld_late, 16 * 4)
            dve.wait_ge(b1_psum, 1)
            b1_src = bank[7][:, 16:48].rearrange("p (c k e) -> p c k e", c=2, k=2)
            v.tensor_copy(b1_col[:, :, 0, :], b1_src[:, :, 0, :])
            v.tensor_scalar(b1_col[:, :, 1, :], b1_src[:, :, 1, :], -1.0, 7.0, ALU.mult, ALU.add).then_inc(b1_ready, 1)

            mha(0)

            def first_router():
                top2_router(0, 1, None)
                values(1, 1)
            ffn(0, states[0], first_router)
            layer_norm(2)
            mha(1)
            top2_router(1, 2, 0)
            values(2, 2)
            add_biases(1)
            n = 0
            for q in range(NT):
                pair, g = q // 2, q % 2
                dve.wait_ge(e1_psum, q + 1)
                for e in range(4):
                    for i in range(2):
                        t = 2 * pair + i
                        after(dve, e1_added, n - 1)
                        v.scalar_tensor_tensor(x_tok[:, t, :], bank[2 * i + g][:, e * D:(e + 1) * D],
                                               comb[:, t, 4 * g + e:4 * g + e + 1], x_tok[:, t, :], ALU.mult, ALU.add)\
                            .then_inc(e1_added, 1)
                        n += 1
            dve.wait_ge(e1_added, n)
            mha(2)
            mha(3)

            def choice_router():
                dve.wait_ge(r2_psum, 1)
                src = bank[6][:, 0:2 * S].rearrange("p (f s) -> p f s", f=2)

                def over_tokens(ap):
                    return ap.unsqueeze(2).broadcast_to([P, 2, S])
                link(v.reduce_max(rcol[:, :], src, AX))
                v.tensor_tensor(rwork[:, :, :], src, over_tokens(rcol[:, :]), ALU.subtract).then_inc(dve_to_act, 1)
                dve.wait_ge(act_to_dve, 3)
                link(v.reduce_sum(rcol[:, :], rp[:, :, :], AX))
                link(v.reciprocal(rcol[:, :], rcol[:, :]))
                link(v.tensor_tensor(rp[:, :, :], rp[:, :, :], over_tokens(rcol[:, :]), ALU.mult))
                link(v.tensor_copy(rwork[:, :, :], rp[:, :, :]))
                for _ in range(TOP_C // 8):
                    for f in range(2):
                        ins = v.max(rtop[:, f, :], rwork[:, f, :])
                    link(ins)
                    for f in range(2):
                        ins = v.match_replace(rwork[:, f, :], rtop[:, f, :], rwork[:, f, :], -1.0)
                    link(ins)
                link(v.tensor_scalar(rwork[:, :, :], rwork[:, :, :], 0.0, None, ALU.is_lt))
                link(v.tensor_tensor(rp[:, :, :], rp[:, :, :], rwork[:, :, :], ALU.mult))
                link(v.reduce_sum(rcol[:, :], rp[:, :, :], AX))
                link(v.tensor_scalar(rcol[:, :], rcol[:, :], 1e-9, None, ALU.add))
                link(v.reciprocal(rcol[:, :], rcol[:, :]))
                link(v.tensor_scalar(rcol[:, :], rcol[:, :], gates[:, 6:7], None, ALU.mult))
                v.tensor_tensor(rsel[:, :, :], rp[:, :, :], over_tokens(rcol[:, :]), ALU.mult).then_inc(rsel_ready, 1)
            ffn(1, states[1], choice_router)
            layer_norm(6)
            for g in range(2):
                dve.wait_ge(s3_psum, g + 1)
                src = bank[g][:, :].rearrange("p (t k) -> p t k", t=4)
                for half in range(2):
                    rows = slice(half * S, (half + 1) * S)
                    ins = v.reduce_max(m3[rows, 4 * g:4 * g + 4], src[rows, :, half * S:(half + 1) * S], AX)
                link(ins)
                for half in range(2):
                    rows = slice(half * S, (half + 1) * S)
                    ins = v.tensor_tensor(s3[rows, 4 * g:4 * g + 4, :], src[rows, :, half * S:(half + 1) * S],
                                          m3[rows, 4 * g:4 * g + 4].unsqueeze(2).broadcast_to([S, 4, S]), ALU.subtract)
                ins.then_inc(s3_ready, 1)
            for g in range(2):
                for c in range(2):
                    dve.wait_ge(o3_psum, 2 * g + c + 1)
                    o = bank[(4, 5, 0, 1)[2 * g + c]][:, 0:2 * (D + 1)].rearrange("p (t c) -> p t c", t=2)
                    ts = slice(4 * g + 2 * c, 4 * g + 2 * c + 2)
                    link(v.reciprocal(m3[:, ts], o[:, :, D]))
                    link(v.tensor_scalar(m3[:, ts], m3[:, ts], gates[:, 3:4], None, ALU.mult))
                    for i in range(2):
                        t = 4 * g + 2 * c + i
                        ins = v.scalar_tensor_tensor(x_tok[:, t, :], o[:, i, 0:D], m3[:, t:t + 1], x_tok[:, t, :],
                                                     ALU.mult, ALU.add)
                link(ins)
                statistics(7, x_tok, g)
            for half in range(2):
                normed(7, half, counted=False)
                statistics(8, x_norm, half)
            for half in range(2):
                dve.wait_ge(rstd_ready, NT * 8 + 4 * half + 4)
                for t in range(4 * half, 4 * half + 4):
                    v.scalar_tensor_tensor(x_rms[:, t, :], x_norm[:, t, :], rstd[:, t:t + 1], ns_row[:, :],
                                           ALU.mult, ALU.mult).then_inc(xn_ready, 1)

            def last_router():
                for t in range(NT):
                    ins = v.scalar_tensor_tensor(x_tok[:, t, :], x_norm[:, t, :], gates[:, 7:8], x_tok[:, t, :],
                                                 ALU.mult, ALU.add)
                link(ins)
                top2_router(2, 4, 1)
            ffn(2, states[2], last_router)
            v.tensor_copy(row_open[:, :], x_tok[:, 0, 0:1]).then_inc(x_final, 1)


def kernel(**inputs):
    import concourse.bacc as bacc
    from concourse.bass_utils import run_bass_kernel_spmd

    nc = bacc.Bacc("TRN2", target_bir_lowering=False, num_devices=1)
    arrays, aps = {}, {}
    data = {name: np.ascontiguousarray(inputs[name]) for name in UNPACKED}
    data.update(packs(inputs))
    data["shape_constants"] = shape_constants()
    for name, array in data.items():
        arrays[f"in_{name}"] = array
        aps[name] = nc.dram_tensor(f"in_{name}", array.shape, mybir.dt.from_np(array.dtype), kind="ExternalInput").ap()
    out = nc.dram_tensor("out_x", (B, S, D), F32, kind="ExternalOutput").ap()
    comb_dram = [nc.dram_tensor(f"combine_{f}", (FFN_E[f], T), F32, kind="Internal").ap() for f in range(3)]
    build(nc, aps, comb_dram, out)
    result = run_bass_kernel_spmd(nc, [arrays], core_ids=[0])
    return result.results[0]["out_x"]
```

```python
from contextlib import ExitStack

import numpy as np

import concourse.bass as bass
from concourse import mybir

ALU = mybir.AluOpType
ACT = mybir.ActivationFunctionType
AX = mybir.AxisListType.X
F32 = mybir.dt.float32
F32R = mybir.dt.float32r
BF16 = mybir.dt.bfloat16
I32 = mybir.dt.int32

P = 128
B, S, D = 16, 64, 128
T = B * S
NT = T // P
HALF = T // 2
H, DK = 16, 8
PAIR = H // 2
VW = 2 * DK + 1
QUAD = PAIR // 2
VB = QUAD * 2 * VW
BIG = float(2 ** 30)
LN_EPS = 1e-5

MHA_GATE = (0, 1, 5, 2)
NM = len(MHA_GATE)
NEXT_LN = (1, 3, 4, 5)
FILL, DRAIN = 4, 4
FFN_E = (8, 16, 8)
FFN_C = (1, 2, 2)
FFN_LN = (1, 5, 7)
UP_DMA = (1, 2, 1)
FFN_SPLITS = (2, 2, 1)
SPLIT_UP_AT = (0, 1, 1)
RING = 4
DOWN_LAG = 3
TOP_C = 32

C_ID, C_ROT, C_DUP, C_PM, C_JM, C_COS, C_SIN, C_TRI = 0, 128, 256, 384, 392, 394, 458, 522
C_N = 586


ROWS_N = 24 + 4 * D
FEATURE_N = 32 + 4 * D
EXPERT_N = 3 * D + 512


def packs(inp):
    def cat(arrays):
        return np.ascontiguousarray(np.concatenate(arrays, axis=-1))
    b_qkv = inp["L1_ffn_b_qkv"]
    return {
        "projections": np.ascontiguousarray(np.stack(
            [inp[n] for n in ("L0_xattn_w_q", "L0_xattn_w_k", "L0_xattn_w_v", "L0_xattn_w_o", "L1_xattn_w_q",
                              "L1_xattn_w_k", "L1_xattn_w_v", "L1_xattn_w_o", "L2_xattn_W_proj")], axis=1)),
        "bias_columns": np.ascontiguousarray(np.stack(
            [inp[n] for n in ("L0_xattn_b_q", "L0_xattn_b_k", "L1_xattn_b_q", "L1_xattn_b_k")]
            + [b_qkv[0:D], b_qkv[D:2 * D]], axis=1)),
        "rows": cat([inp["g_xattn"], inp["g_ffn"], inp["L1_ffn_b_gate"], inp["L3_ffn_gate_b"],
                     inp["L3_ffn_norm_scale"], inp["L0_xattn_b_v"], inp["L1_xattn_b_v"], b_qkv[2 * D:3 * D]]),
        "output_biases": cat([inp["L0_xattn_b_o"], inp["L1_xattn_b_o"], inp["L2_xattn_b_proj"]]),
        "by_feature": cat([inp["L1_ffn_W_gate"], inp["L3_ffn_gate_w"], inp["L2_ffn_router_w2"],
                           inp["L2_ffn_router_w1"], inp["L1_ffn_W_qkv"]]),
        "by_expert": cat([inp["L0_ffn_gate_w"], inp["L1_ffn_b_experts"], inp["L3_ffn_mlp2_b"], inp["L3_ffn_mlp1_b"]]),
    }


UNPACKED = ("x", "ctx_1024", "mask_1x1xSxS2_ik0", "L0_ffn_gate_up_proj", "L0_ffn_down_proj", "L1_ffn_W_experts",
            "L2_ffn_w1", "L2_ffn_w2", "L2_ffn_w3", "L3_ffn_mlp1_w", "L3_ffn_mlp2_w")


def shape_constants():
    c = np.zeros((P, C_N), np.float32)
    c[:, C_ID:C_ID + P] = np.eye(P)
    for h in range(H):
        for j in range(DK // 2):
            c[h * DK + 2 * j + 1, C_ROT + h * DK + j] = -1.0
            c[h * DK + 2 * j, C_ROT + h * DK + DK // 2 + j] = 1.0
    for q in range(S):
        c[q, C_DUP + q] = c[q, C_DUP + S + q] = 1.0
    rows = np.arange(P)
    for pair in range(PAIR):
        c[:, C_PM + pair] = rows // (2 * DK) == pair
    for j2 in range(2):
        c[:, C_JM + j2] = ((rows // DK) % 2 == j2) / np.sqrt(np.float32(DK))
    inv = (1.0 / 10000.0 ** (np.arange(0, DK, 2, dtype=np.float32) / DK)).astype(np.float32)
    ang = np.arange(S, dtype=np.float32)[:, None] * inv[None, :]
    ang = np.concatenate([ang, ang], axis=-1).astype(np.float32)
    c[:, C_COS:C_COS + S] = np.cos(ang).T[rows % DK]
    c[:, C_SIN:C_SIN + S] = np.sin(ang).T[rows % DK]
    c[:, C_TRI:C_TRI + 64] = np.tril(np.ones((8, 8)), -1).reshape(1, 64)
    return c


def ffn_states():
    out, pairs, experts, dmas, splits = [], 0, 0, 0, 0
    for f in range(3):
        out.append((pairs, experts, dmas, splits))
        pairs += 2 * FFN_E[f] * FFN_C[f]
        experts += FFN_E[f]
        dmas += 16 * UP_DMA[f] * FFN_E[f] // 2
        splits += FFN_SPLITS[f] * FFN_E[f]
    return out


def run_experts(eng, f, body):
    body(0, True, False)
    with eng.Fori(1, FFN_E[f] // 2 - 1) as e:
        body(e, False, False)
    body(FFN_E[f] // 2 - 1, False, True)


def place(calls, i, pos, n, steady):
    if steady:
        return calls[i], pos, n * calls[i] + pos
    at = i * n + pos
    if not 0 <= at < n * len(calls):
        return None
    return calls[at // n], at % n, n * calls[0] + at


def run_tiles(eng, calls, tile_step, before_loop=None, while_draining=None):
    for i in range(len(calls)):
        for tau in range(FILL):
            tile_step(tau, i, False)
        if before_loop:
            before_loop(calls[i])
        with eng.Fori(FILL, NT) as tau:
            tile_step(tau, i, True)
    for tau in range(NT, NT + DRAIN):
        tile_step(tau, len(calls) - 1, False)
        if while_draining:
            while_draining(tau - NT)


def after(eng, sem, value):
    if not (isinstance(value, int) and value <= 0):
        eng.wait_ge(sem, value)


def build(nc, a, comb_dram, out):
    with ExitStack() as ctx:
        def sb(name, shape, dt=F32):
            return ctx.enter_context(nc.sbuf_tensor(name, shape, dt))

        def sem(name):
            return ctx.enter_context(nc.semaphore(name))

        bank = [ctx.enter_context(nc.psum_tensor(f"bank{i}", [P, 512], F32)) for i in range(8)]

        const = sb("const", [P, C_N])
        ident = const[:, C_ID:C_ID + P]
        zero_bf = sb("zero_bf", [P, 1], BF16)
        dup_bf = sb("dup_bf", [P, P], BF16)
        x_tok = sb("x_tok", [P, NT, D])
        x_norm = sb("x_norm", [P, NT, D])
        xn_slot = sb("xn_slot", [P, D])
        xT = sb("xT", [P, T])
        stats = sb("stats", [P, NT, 6])
        mv = sb("mv", [P, NT, 2])
        var_eps = sb("var_eps", [P, NT])
        rstd = sb("rstd", [P, NT])
        rstd_rms = sb("rstd_rms", [P, NT])
        stats_slot = sb("stats_slot", [P, 6])
        mv_slot = sb("mv_slot", [P, 2])
        eps_col = sb("eps_col", [P, 1])
        fourteen = sb("fourteen", [P, 1])
        var_slot = sb("var_slot", [P, 1])
        rstd_slot = sb("rstd_slot", [P, 1])
        minus_half = sb("minus_half", [P, NT])
        ctx_tok = sb("ctx_tok", [P, NT, D + 1])
        ctxT = sb("ctxT", [P, T])
        row_pack = sb("row_pack", [P, ROWS_N])
        gates = row_pack[:, 0:8]
        gate_b = row_pack[:, 8:24].rearrange("p (l e) -> p l e", l=2)
        ns_row = row_pack[:, 24:24 + D]
        v_bias = row_pack[:, 24 + D:24 + 4 * D].rearrange("p (l d) -> p l d", l=3)
        by_feature = sb("by_feature", [P, 8 + FEATURE_N])
        gate_w = by_feature[:, 0:24].rearrange("p (l e) -> p l e", l=3)
        rw2 = by_feature[:, 24:40]
        rw1 = by_feature[:, 40:40 + D]
        w_qkv = by_feature[:, 40 + D:40 + 4 * D]
        by_expert = sb("by_expert", [8, EXPERT_N])
        gate_raw = by_expert[:, 0:D]
        be = by_expert[:, D:3 * D].rearrange("e (l d) -> e l d", l=2)
        b1_raw = by_expert[:, 3 * D:3 * D + 512]
        biases = sb("biases", [P, 10])
        bq0, bk0, bq1, bk1, bqs, bks, rq0, rk0 = (biases[:, i:i + 1] for i in range(8))
        w_raw = sb("w_raw", [P, 9, D])
        wT = sb("wT", [P, 8, D])
        wo_by_j2 = sb("wo_by_j2", [P, NM, 2, 64])
        w_out = sb("w_out", [65, NM, 2, D])
        bo_row = sb("bo_row", [65, 3, D])
        mask_i = sb("mask_i", [P, S], I32)
        mask_open = sb("mask_open", [P, S])
        row_open = sb("row_open", [P, 1])
        mask_low = sb("mask_low", [P, S], BF16)
        q_scale = sb("q_scale", [P, 2, 2, S])
        kT = sb("kT", [P, 2, T])
        qT = sb("qT", [P, T])
        x_rms = kT[:, 1, :].rearrange("p (t d) -> p t d", d=D)
        rot_tmp = sb("rot_tmp", [P, HALF])
        v_blk = sb("v_blk", [P, NM, B, VB])
        q_blk = sb("q_blk", [P, 2, 2, S])
        k_blk = sb("k_blk", [P, 2, PAIR, S])
        row_max = sb("row_max", [P, 2, PAIR])
        shifted = sb("shifted", [P, 2, PAIR, S])
        probs = sb("probs", [P, 2, PAIR, S])
        probsT = sb("probsT", [P, 2, QUAD, P])
        inv_sum = sb("inv_sum", [P, 2, PAIR])
        o_norm = sb("o_norm", [P, 2, 2, PAIR, DK])
        oT = sb("oT", [65, 2, P])
        logits = sb("logits", [P, NT, 8])
        gt = sb("gt", [P, NT, 8, 8])
        eq = sb("eq", [P, NT, 8, 8])
        rank = sb("rank", [P, NT, 8])
        top = sb("top", [P, NT, 8])
        e_max = sb("e_max", [P, NT])
        e_sum = sb("e_sum", [P, NT])
        comb = sb("comb", [P, NT, 16])
        combT = sb("combT", [8, T])
        we1 = sb("we1", [P, 8, D])
        b1_col = sb("b1_col", [P, 2, 2, 8])
        w_up = sb("w_up", [P, 2, 512])
        w_dn = sb("w_dn", [P, 2, 2, D])
        xT_hi = sb("xT_hi", [P, T], F32R)
        xT_lo = sb("xT_lo", [P, T], F32R)
        w_up_hi = sb("w_up_hi", [P, 2, 512], F32R)
        w_up_lo = sb("w_up_lo", [P, 2, 512], F32R)
        w_dn_hi = sb("w_dn_hi", [P, 2, 2, D], F32R)
        w_dn_lo = sb("w_dn_lo", [P, 2, 2, D], F32R)
        comb_row = sb("comb_row", [P, 2, T])
        act_out = w_raw[:, 0:8, :].rearrange("p (s t) d -> p s (t d)", s=2)
        product = shifted[:, :, :, :].rearrange("p s h k -> p s (h k)")
        glu = k_blk[:, :, :, :].rearrange("p s h k -> p s (h k)")
        gated = probs[:, :, :, :].rearrange("p s h k -> p s (h k)")
        over = probsT[:, :, :, :].rearrange("p s i q -> p s (i q)")
        lin = sb("lin", [P, 2, HALF])
        hid = sb("hid", [P, RING, HALF])
        ctx_dup = hid[:, :, :].rearrange("p r (b d) -> p (r b) d", d=D)
        hid_hi = sb("hid_hi", [P, RING, HALF], F32R)
        hid_lo = sb("hid_lo", [P, RING, HALF], F32R)
        outT = sb("outT", [P, T])
        r2 = sb("r2", [P, 16, NT])
        r1 = qT
        rp = sb("rp", [P, 2, S])
        rwork = sb("rwork", [P, 2, S])
        rtop = sb("rtop", [P, 2, 8])
        rsel = sb("rsel", [P, 2, S])
        rcol = sb("rcol", [P, 2])
        s3 = rot_tmp[:, :].rearrange("p (t k) -> p t k", t=NT)
        p3 = sb("p3", [P, NT, P])
        p3T = outT[:, :].rearrange("p (t q) -> p t q", t=NT)
        m3 = sb("m3", [P, NT])

        ld_const, ld_x, ld_ctx, ld_w, ld_small, ld_late, ld_dup = (sem(n) for n in (
            "const_loaded", "x_loaded", "ctx_loaded", "proj_loaded", "small_loaded", "late_loaded", "dup_loaded"))
        k1_psum, k1_ready = sem("L1_keys_psum"), sem("L1_keys_ready")
        dve_done, pool_done, act_done = sem("dve_step_done"), sem("pool_step_done"), sem("act_step_done")
        gates_ready, consts_set, v_cleared = sem("gates_ready"), sem("consts_set"), sem("v_blocks_cleared")
        ctxT_psum, ctxT_ready = sem("ctxT_psum"), sem("ctxT_ready")
        wT_psum, wT_ready = sem("wT_psum"), sem("wT_ready")
        wo_psum, wo_ready = sem("wo_psum"), sem("wo_ready")
        rb_psum, rb_ready = sem("rot_bias_psum"), sem("rot_bias_ready")
        mask_ready, ro_psum, q_scale_ready = sem("mask_ready"), sem("row_open_psum"), sem("q_scale_ready")
        gw_psum, gw_ready = sem("gate_w_psum"), sem("gate_w_ready")
        b1_psum, b1_ready = sem("b1_psum"), sem("b1_ready")
        proj_psum, proj_ready = sem("proj_psum"), sem("proj_ready")
        v_psum, v_ready = sem("v_psum"), sem("v_ready")
        mv_ready, rstd_ready, xn_ready = sem("mv_ready"), sem("rstd_ready"), sem("xn_ready")
        xT_psum, xT_ready = sem("xT_psum"), sem("xT_ready")
        blocks_ready, scores_done, max_ready, shift_ready = (sem(n) for n in (
            "blocks_ready", "scores_done", "max_ready", "shift_ready"))
        exp_done, pT_psum, pT_ready, pv_done = (sem(n) for n in ("exp_done", "pT_psum", "pT_ready", "pv_done"))
        inv_ready, on_ready, oT_psum, oT_ready, y_psum, x_added = (sem(n) for n in (
            "inv_ready", "on_ready", "oT_psum", "oT_ready", "y_psum", "x_added"))
        logit_psum, comb_ready = sem("logit_psum"), sem("comb_ready")
        combT_psum, combT_ready, be_psum, be_added = (sem(n) for n in (
            "combT_psum", "combT_ready", "be_psum", "be_added"))
        e1_psum, e1_added = sem("expert1_psum"), sem("expert1_added")
        up_loaded = [sem("even_up_loaded"), sem("odd_up_loaded")]
        dn_loaded = [sem("even_down_loaded"), sem("odd_down_loaded")]
        x_hi_ready, x_lo_ready = sem("x_hi_ready"), sem("x_lo_ready")
        w_hi_ready = sem("w_hi_ready")
        w_lo_ready = [sem(f"w_lo_ready_{f}") for f in range(3)]
        row_psum, row_ready = sem("first_row_psum"), sem("first_row_ready")
        comb_stored, comb_loaded = sem("comb_stored"), [sem("even_comb_loaded"), sem("odd_comb_loaded")]
        up_psum, silu_ready, product_ready, hid_ready, hi_ready, lo_ready, down_psum = (sem(n) for n in (
            "up_psum", "silu_ready", "product_ready", "hid_ready", "hi_ready", "lo_ready", "down_psum"))
        glu_ready, sigmoid_ready, gated_ready, over_ready, lin_ready, plain_ready = (sem(n) for n in (
            "glu_ready", "sigmoid_ready", "gated_ready", "over_ready", "lin_ready", "plain_product_ready"))
        outT_ready, out_psum, out_added = sem("outT_ready"), sem("out_psum"), sem("out_added")
        logits_read = sem("logits_read")
        r1_psum, r1_ready, r2_psum, r2_ready, r2T_psum, rsel_ready = (sem(n) for n in (
            "r1_psum", "r1_ready", "r2_psum", "r2_ready", "r2T_psum", "rsel_ready"))
        s3_psum, s3_ready, p3_ready, p3T_psum, p3T_ready, o3_psum = (sem(n) for n in (
            "s3_psum", "s3_ready", "p3_ready", "p3T_psum", "p3T_ready", "o3_psum"))
        dve_to_act, act_to_dve = sem("shifted_logits_ready"), sem("exp_logits_ready")
        wo_split = sem("wo_split")
        eps_added, stats_ready = sem("eps_added"), sem("stats_ready")
        v3_ready = sem("context_values_ready")
        stored = sem("stored")

        def wait_for_weights(eng, f, e, ej, slot, first):
            if first and slot == 0:
                if ej % FFN_C[f] == 0:
                    eng.wait_ge(row_ready, 2 * f + ej // FFN_C[f] + 1)
            elif ej == 0:
                before = ffn_states()[f][1] // 2
                eng.wait_ge(comb_loaded[slot], 16 * (before + 1 + e if slot else before - f + e))

        block = ctx.enter_context(nc.Block())

        def tok(ap, p=P):
            return ap.rearrange("b s d -> (b s) d").rearrange("(t p) d -> p t d", p=p)

        @block.sync
        def _(sp):
            sp.dma_start(x_tok[:, :, :], tok(a["x"])).then_inc(ld_x, 16)
            sp.dma_start(ctx_tok[:, :, 0:D], tok(a["ctx_1024"])).then_inc(ld_ctx, 16)
            sp.dma_start(w_raw[:, :, :], a["projections"]).then_inc(ld_w, 16)
            sp.dma_start(we1[:, :, :], a["L1_ffn_W_experts"].rearrange("e d f -> d e f")).then_inc(ld_late, 16)
            for half in range(2):
                sp.dma_start(ctx_dup[half * S:(half + 1) * S, :, :],
                             a["ctx_1024"].rearrange("b s d -> s b d")).then_inc(ld_dup, 16)
            states = ffn_states()
            for f in range(3):
                pair0, exp0, dma0, split0 = states[f]
                per = 2 * FFN_C[f]

                def load(e, slot):
                    after(sp, w_lo_ready[f], FFN_SPLITS[f] * (e - 1))
                    up, dn = w_up[:, slot, :], w_dn[:, slot, :, :]
                    if f == 0:
                        sp.dma_start(up[:, 0:2 * D], a["L0_ffn_gate_up_proj"][e, :, :]).then_inc(up_loaded[slot], 16)
                        sp.dma_start(dn[:, 0, :], a["L0_ffn_down_proj"][e, :, :]).then_inc(dn_loaded[slot], 16)
                    if f == 1:
                        sp.dma_start(up[:, 0:256], a["L2_ffn_w1"][e, :, :]).then_inc(up_loaded[slot], 16)
                        sp.dma_start(up[:, 256:512], a["L2_ffn_w2"][e, :, :]).then_inc(up_loaded[slot], 16)
                        sp.dma_start(dn, a["L2_ffn_w3"][e, :, :].rearrange("(c p) d -> p c d", p=P))\
                            .then_inc(dn_loaded[slot], 16)
                    if f == 2:
                        sp.dma_start(up, a["L3_ffn_mlp1_w"][e, :, :]).then_inc(up_loaded[slot], 16)
                        after(sp, down_psum, pair0 + per * (e - 1))
                        sp.dma_start(dn, a["L3_ffn_mlp2_w"][e, :, :].rearrange("(c p) d -> p c d", p=P))\
                            .then_inc(dn_loaded[slot], 16)

                def spread(e, slot):
                    after(sp, hid_ready, pair0 + per * (e - 1))
                    sp.dma_start(comb_row[:, slot, :], comb_dram[f][e, :].partition_broadcast(P))\
                        .then_inc(comb_loaded[slot], 16)

                if f > 0:
                    sp.wait_ge(w_lo_ready[f - 1], FFN_SPLITS[f - 1] * FFN_E[f - 1])
                load(0, 0)
                load(1, 1)
                if f == 1:
                    sp.wait_ge(rsel_ready, 1)
                    sp.dma_start(comb_dram[f].rearrange("e (t r) -> (e t) r", t=NT),
                                 rsel[:, :, :].rearrange("p f s -> p (f s)")).then_inc(comb_stored, 16)
                else:
                    sp.wait_ge(combT_ready, (1, 0, 3)[f])
                    sp.dma_start(comb_dram[f], combT[:, :]).then_inc(comb_stored, 16)
                sp.wait_ge(comb_stored, 16 * (f + 1))
                after(sp, hid_ready, pair0)
                spread(1, 1)
                with sp.Fori(1, FFN_E[f] // 2) as ep:
                    for slot in range(2):
                        load(2 * ep + slot, slot)
                        spread(2 * ep + slot, slot)
            for half in range(2):
                sp.wait_ge(out_added, 5 + half)
                ts = slice(4 * half, 4 * half + 4)
                sp.dma_start(tok(out)[:, ts, :], x_tok[:, ts, :]).then_inc(stored, 16)
            sp.wait_ge(stored, 32)

        @block.tensor
        def _(pe):
            def mm(o, l, r, start=True, stop=True):
                return nc.tensor.matmul(o, l, r, start=start, stop=stop)

            def transposes_of_x(n, src, half):
                pe.wait_ge(xn_ready, NT * n + 4 * half + 4)
                for i in range(4):
                    last = nc.tensor.transpose(bank[6 + half][:, i * P:(i + 1) * P], src[:, 4 * half + i, :], ident)
                last.then_inc(xT_psum, 4)

            pe.wait_ge(ld_const, 16)
            pe.wait_ge(ld_ctx, 16)
            for half in range(2):
                for i in range(4):
                    last = nc.tensor.transpose(bank[half][:, i * P:(i + 1) * P], ctx_tok[:, 4 * half + i, 0:D], ident)
                last.then_inc(ctxT_psum, 1)
            for half in range(2):
                transposes_of_x(0, x_norm, half)
            pe.wait_ge(ld_w, 16)
            for i, (w, rotated) in enumerate(((0, 0), (1, 0), (2, 0), (0, 1), (1, 1), (4, 0), (5, 0), (6, 0))):
                o = bank[2 + i // 4][:, (i % 4) * P:(i % 4 + 1) * P]
                if rotated:
                    last = mm(o, w_raw[:, w, :], const[:, C_ROT:C_ROT + P])
                else:
                    last = nc.tensor.transpose(o, w_raw[:, w, :], ident)
                if i % 4 == 3:
                    last.then_inc(wT_psum, 1)
            pe.wait_ge(wo_split, 1)
            for m in range(NM):
                for j2 in range(2):
                    last = nc.tensor.transpose(bank[4 + m // 2][0:64, ((m % 2) * 2 + j2) * P:((m % 2) * 2 + j2 + 1) * P],
                                               wo_by_j2[:, m, j2, :], ident)
            last.then_inc(wo_psum, 1)
            pe.wait_ge(ld_small, 16 * 4)
            pe.wait_ge(xT_ready, NT)
            for i in range(2):
                last = mm(bank[6][:, i:i + 1], const[:, C_ROT:C_ROT + P], biases[:, i:i + 1])
            last.then_inc(rb_psum, 1)
            pe.wait_ge(mask_ready, 1)
            pe.wait_ge(rb_ready, 1)
            mm(bank[6][:, 64:128], row_open[0:S, :].broadcast_to([S, P]), const[0:S, C_ID:C_ID + S]).then_inc(ro_psum, 1)
            count = [0]

            def project(w, src, half):
                n = count[0]
                after(pe, proj_ready, n - 3)
                mm(bank[n % 4][:, :], w, src[:, half * HALF:(half + 1) * HALF]).then_inc(proj_psum, 1)
                count[0] += 1

            vcount = [0]

            def values(w, src, groups):
                for g in groups:
                    n = vcount[0]
                    after(pe, v_ready, n - 1)
                    for i in range(4):
                        o, first = bank[4 + n % 2][:, i * P:(i + 1) * P], (4 * g + i) * S
                        if first + P <= T:
                            last = mm(o, src[:, first:first + P], w)
                        else:
                            mm(o[0:S, :], src[:, first:first + S], w)
                            last = mm(o[S:P, :], src[:, 0:S], w)
                    last.then_inc(v_psum, 1)
                    vcount[0] += 1

            pe.wait_ge(ctxT_ready, 2)
            pe.wait_ge(wT_ready, 2)
            for half in range(2):
                for w, src in ((wT[:, 1, :], ctxT), (wT[:, 4, :], ctxT), (wT[:, 0, :], xT), (wT[:, 3, :], xT)):
                    project(w, src, half)
            pe.wait_ge(ld_late, 16 * 4)
            nc.tensor.transpose(bank[7][:, 0:8], gate_raw[:, :], const[0:8, C_ID:C_ID + 8]).then_inc(gw_psum, 1)
            pe.wait_ge(gw_ready, 1)
            for c in range(2):
                for k in range(2):
                    last = nc.tensor.transpose(bank[7][:, 16 + (2 * c + k) * 8:24 + (2 * c + k) * 8],
                                               b1_raw[:, 256 * c + k:256 * c + 256:2], const[0:8, C_ID:C_ID + 8])
            last.then_inc(b1_psum, 1)
            pe.wait_ge(wo_ready, 2)
            values(wT[:, 2, :], ctxT, range(4))
            pe.wait_ge(q_scale_ready, 1)
            pe.wait_ge(b1_ready, 1)

            def mha(*calls, while_draining=None):
                pe.wait_ge(proj_ready, count[0])

                def step(tau, s, i, steady):
                    u = 1 - s
                    at = place(calls, i, 2 * tau + s, B, steady)
                    if at:
                        m, b, g = at
                        pe.wait_ge(blocks_ready, 2 * g + 2)
                        after(pe, shift_ready, g - 1)
                        if m < 2:
                            mm(bank[s][:, :], dup_bf[:, :], mask_low[:, :].unsqueeze(1).broadcast_to([P, PAIR, S]),
                               stop=False)
                        mm(bank[s][:, :], q_blk[:, s, :, :], k_blk[:, s, :, :], start=m >= 2).then_inc(scores_done, 1)
                    at = place(calls, i, 2 * tau + s - 2, B, steady)
                    if at:
                        m, b, g = at
                        if not steady and g == B * calls[0]:
                            pe.wait_ge(v_ready, vcount[0])
                            if m == 2:
                                pe.wait_ge(be_added, 1)
                            if 3 in calls:
                                pe.wait_ge(v3_ready, 2)
                        pe.wait_ge(pT_ready, g + 1)
                        after(pe, on_ready, g - 1)
                        v = v_blk[:, m, b, :].rearrange("p (i c) -> p i c", i=QUAD)
                        for c in range(QUAD):
                            last = mm(bank[4 + s][:, c * 2 * VW:(c + 1) * 2 * VW], probsT[:, s, c, :], v[:, c, :])
                        last.then_inc(pv_done, 1)
                    at = place(calls, i, 2 * tau + s - 1, B, steady)
                    if at:
                        m, b, g = at
                        pe.wait_ge(exp_done, g + 1)
                        after(pe, pT_ready, g)
                        for c in range(QUAD):
                            last = nc.tensor.transpose(bank[2][:, c * P:(c + 1) * P],
                                                       probs[:, u, 2 * c:2 * c + 2, :], ident)
                        last.then_inc(pT_psum, 1)
                    at = place(calls, i, 2 * tau + s - 3, B, steady)
                    if at:
                        m, b, g = at
                        pe.wait_ge(on_ready, g + 1)
                        after(pe, oT_ready, g)
                        nc.tensor.transpose(bank[6][:, u * P:(u + 1) * P], o_norm[:, u, :, :, :], ident)\
                            .then_inc(oT_psum, 1)

                def tile_step(tau, i, steady):
                    step(tau, 0, i, steady)
                    step(tau, 1, i, steady)
                    at = place(calls, i, tau - 2, NT, steady)
                    if at:
                        m, t, g = at
                        pe.wait_ge(oT_ready, 2 * g + 2)
                        after(pe, x_added, g)
                        mm(bank[7][:, 0:D], oT[:, 0, :], w_out[:, m, 0, :], stop=False)
                        mm(bank[7][:, 0:D], oT[:, 1, :], w_out[:, m, 1, :], start=False).then_inc(y_psum, 1)
                    at = place(calls, i, tau - 4, NT, steady)
                    if at:
                        m, t, g = at
                        n = NEXT_LN[m]
                        pe.wait_ge(xn_ready, NT * n + t + 1)
                        after(pe, xT_ready, NT * n + t)
                        nc.tensor.transpose(bank[3][:, 0:P], xn_slot[:, :], ident).then_inc(xT_psum, 1)
                run_tiles(pe, calls, tile_step, while_draining=while_draining)

            def router(i, w, tiles):
                for t in tiles:
                    last = mm(bank[0][:, t * 8:(t + 1) * 8], xT[:, t * P:(t + 1) * P], w)
                if t == NT - 1:
                    last.then_inc(logit_psum, 1)

            def first_row(f):
                if f == 1:
                    pe.wait_ge(rsel_ready, 1)
                    for t in range(NT):
                        last = mm(bank[6 + t // 4][:, (t % 4) * P:(t % 4 + 1) * P],
                                  const[:, C_ID + t:C_ID + t + 1].broadcast_to([P, P]), rsel[:, :, :])
                else:
                    pe.wait_ge(combT_ready, (1, 0, 3)[f])
                    for half in range(2):
                        last = mm(bank[6 + half][:, :], const[0:8, C_ID:C_ID + 1].broadcast_to([8, P]),
                                  combT[:, half * HALF:(half + 1) * HALF])
                last.then_inc(row_psum, 1)

            def early_router(i, m):
                def hook(k):
                    if k == 0:
                        pe.wait_ge(shift_ready, B * (m + 1))
                    pe.wait_ge(xT_ready, NT * NEXT_LN[m] + 4 + k)
                    router(i, gate_w[:, i, :], range(4) if k == 0 else (3 + k,))
                return hook

            def router_hidden(half):
                pe.wait_ge(xT_ready, NT * 5 + 4 * half + 4)
                mm(bank[half][:, :], rw1[:, :], xT[:, half * HALF:(half + 1) * HALF]).then_inc(r1_psum, 1)

            def early_hidden(k):
                if k == 0:
                    pe.wait_ge(shift_ready, B * 4)
                    router_hidden(0)

            def combine_transposed(i):
                pe.wait_ge(comb_ready, i)
                for t in range(NT):
                    last = nc.tensor.transpose(bank[6 + t // 4][0:8, (t % 4) * P:(t % 4 + 1) * P], comb[:, t, 0:8], ident)
                last.then_inc(combT_psum, 1)

            def ffn(f, state, between=None):
                chunks = FFN_C[f]
                per = 2 * chunks
                pair0, exp0, dma0, split0 = state
                acc = [f == 2, f != 1]
                lag = DOWN_LAG

                def up(e, k, c):
                    slot, half = k // 2, k % 2
                    local = (4 * e + k) * chunks + c
                    if half == 0 and c == 0:
                        pe.wait_ge(w_lo_ready[f], FFN_SPLITS[f] * (2 * e + slot) + 1)
                    if f < 2:
                        after(pe, product_ready, pair0 + local - 1)
                    else:
                        after(pe, glu_ready, local - 1)
                        after(pe, over_ready, local - 1)
                    pb = 2 * ((k * chunks + c) % 2)
                    g, u = {0: (slice(0, 128), slice(128, 256)),
                            1: (slice(c * 128, c * 128 + 128), slice(256 + c * 128, 384 + c * 128)),
                            2: (slice(256 * c, 256 * c + 256, 2), slice(256 * c + 1, 256 * c + 256, 2))}[f]
                    ts = slice(half * HALF, (half + 1) * HALF)
                    for o, cols in ((bank[pb], g), (bank[pb + 1], u)):
                        hi, lo = w_up_hi[:, slot, cols], w_up_lo[:, slot, cols]
                        mm(o[:, :], lo, xT_hi[:, ts], stop=False)
                        mm(o[:, :], hi, xT_hi[:, ts], start=False, stop=False)
                        last = mm(o[:, :], hi, xT_lo[:, ts], start=False)
                    last.then_inc(up_psum, 1)

                def down(e, k, c, last_body=False):
                    local = (4 * e + k) * chunks + c
                    slot, half, u = k // 2, k % 2, (k * chunks + c) % RING
                    start = not acc[half]
                    acc[half] = True
                    stop = last_body and k >= 2 and c == chunks - 1
                    o = bank[6 + half][:, :]
                    if f < 2:
                        pe.wait_ge(w_lo_ready[f], FFN_SPLITS[f] * (2 * e + slot + 1))
                        pe.wait_ge(lo_ready, pair0 + local + 1)
                        hi, lo = w_dn_hi[:, slot, c, :], w_dn_lo[:, slot, c, :]
                        mm(o, lo, hid_hi[:, u, :], start=start, stop=False)
                        mm(o, hi, hid_hi[:, u, :], start=False, stop=False)
                        mm(o, hi, hid_lo[:, u, :], start=False, stop=stop).then_inc(down_psum, 1)
                    else:
                        if half == 0 and c == 0:
                            pe.wait_ge(dn_loaded[slot], 16 * (exp0 // 2 + 1 + e))
                        pe.wait_ge(hid_ready, pair0 + local + 1)
                        mm(o, w_dn[:, slot, c, :], hid[:, u, :], start=start, stop=stop).then_inc(down_psum, 1)

                def body(e, first, last):
                    pairs = [(k, c) for k in range(4) for c in range(chunks)]
                    for j, (k, c) in enumerate(pairs):
                        up(e, k, c)
                        if first and between:
                            between(j)
                        if j >= lag:
                            down(e, *pairs[j - lag], last)
                        elif not first:
                            down(e - 1, *pairs[j - lag])
                    if last:
                        for k, c in pairs[-lag:]:
                            down(e, k, c, last)

                for half in range(2):
                    pe.wait_ge(x_lo_ready, 2 * f + half + 1)
                run_experts(pe, f, body)
                for half in range(2):
                    pe.wait_ge(outT_ready, 2 * f + half + 1)
                    for i in range(4):
                        last = nc.tensor.transpose(bank[4 + half][:, i * P:(i + 1) * P],
                                                   outT[:, (4 * half + i) * P:(4 * half + i + 1) * P], ident)
                    last.then_inc(out_psum, 1)

            states = ffn_states()

            def normed_and_projected(n, weights):
                for half in range(2):
                    transposes_of_x(n, x_norm, half)
                for half in range(2):
                    pe.wait_ge(xT_ready, NT * n + 4 * half + 4)
                    for w in weights:
                        project(w, xT, half)

            mha(0, while_draining=early_router(0, 0))
            pe.wait_ge(xT_ready, NT * 2)
            router(0, gate_w[:, 0, :], (NT - 1,))

            for half in range(2):
                mm(bank[4 + half][:, :], wT[:, 6, :], ctxT[:, half * HALF:(half + 1) * HALF]).then_inc(k1_psum, 1)

            def values_and_weights(j):
                if j == 1:
                    pe.wait_ge(k1_ready, 2)
                    values(wT[:, 7, :], ctxT, (0, 1))
                    combine_transposed(1)
                    first_row(0)
                    values(wT[:, 7, :], ctxT, (2, 3))
                if j == 2:
                    pe.wait_ge(row_ready, 2)
                    mm(bank[7][:, :], dup_bf[:, :], zero_bf[:, :].broadcast_to([P, HALF]), stop=False)
            pe.wait_ge(logits_read, 1)
            ffn(0, states[0], values_and_weights)
            normed_and_projected(2, (wT[:, 5, :],))
            mha(1, while_draining=early_router(1, 1))
            pe.wait_ge(xT_ready, NT * 4)
            router(1, gate_w[:, 1, :], (NT - 1,))
            values(w_qkv[:, 2 * D:3 * D], xT, (0, 1))
            pe.wait_ge(logits_read, 2)
            for half in range(2):
                project(w_qkv[:, 0:D], xT, half)
                project(w_qkv[:, D:2 * D], xT, half)
            pe.wait_ge(proj_ready, count[0])
            for q in range(NT):
                if q == 2:
                    values(w_qkv[:, 2 * D:3 * D], xT, (2, 3))
                    combine_transposed(2)
                pair, g = q // 2, q % 2
                after(pe, e1_added, 8 * (q - 1))
                for i in range(2):
                    t = 2 * pair + i
                    last = mm(bank[2 * i + g][:, :], xT[:, t * P:(t + 1) * P], we1[:, 4 * g:4 * g + 4, :])
                last.then_inc(e1_psum, 1)
            pe.wait_ge(combT_ready, 2)
            pe.wait_ge(v_ready, vcount[0])
            for t in range(NT):
                last = mm(bank[4 + t // 4][:, (t % 4) * D:(t % 4 + 1) * D], combT[:, t * P:(t + 1) * P], be[:, 0, :])
            last.then_inc(be_psum, 1)
            pe.wait_ge(e1_added, 8 * NT)
            mha(2, 3, while_draining=early_hidden)
            router_hidden(1)
            for half in range(2):
                pe.wait_ge(r1_ready, half + 1)
                for t in range(4 * half, 4 * half + 4):
                    last = mm(bank[0][:, t * 16:(t + 1) * 16], r1[:, t * P:(t + 1) * P], rw2[:, :])
            last.then_inc(r2_psum, 1)
            pe.wait_ge(r2_ready, 1)
            nc.tensor.transpose(bank[1][:, 0:P], r2[:, :, :], ident).then_inc(r2T_psum, 1)
            pe.wait_ge(dve_to_act, 3)
            ffn(1, states[1], lambda j: first_row(1) if j == 1 else None)
            for half in range(2):
                transposes_of_x(6, x_norm, half)
            for half in range(2):
                pe.wait_ge(xT_ready, NT * 6 + 4 * half + 4)
                for i in range(4):
                    t = 4 * half + i
                    last = mm(bank[half][:, i * P:(i + 1) * P], xT[:, t * P:(t + 1) * P], ctxT[:, t * P:(t + 1) * P])
                last.then_inc(s3_psum, 1)
            for g in range(2):
                pe.wait_ge(p3_ready, g + 1)
                for i in range(4):
                    last = nc.tensor.transpose(bank[2 + g][:, i * P:(i + 1) * P], p3[:, 4 * g + i, :], ident)
                last.then_inc(p3T_psum, 1)
                pe.wait_ge(p3T_ready, g + 1)
                for i in range(4):
                    t = 4 * g + i
                    last = mm(bank[(4, 5, 0, 1)[t // 2]][:, (t % 2) * (D + 1):(t % 2 + 1) * (D + 1)], p3T[:, t, :], ctx_tok[:, t, :])
                    if i % 2:
                        last.then_inc(o3_psum, 1)
            for half in range(2):
                transposes_of_x(7, x_rms, half)
            pe.wait_ge(xT_ready, NT * 7 + 4)
            router(2, gate_w[:, 2, :], range(4))
            pe.wait_ge(xT_ready, NT * 8)
            router(2, gate_w[:, 2, :], range(4, NT))

            def weights_and_biases(j):
                if j == 1:
                    combine_transposed(3)
                    first_row(2)
                if j == 3:
                    pe.wait_ge(row_ready, 6)
                    for half in range(2):
                        mm(bank[6 + half][:, :], be[:, 1, :], combT[:, half * HALF:(half + 1) * HALF], stop=False)
            pe.wait_ge(logits_read, 3)
            ffn(2, states[2], weights_and_biases)

        @block.scalar
        def _(act):
            done = [0]

            def link(ins):
                done[0] += 1
                ins.then_inc(act_done, 1)
                act.wait_ge(act_done, done[0])

            act.dma_start(const[:, :], a["shape_constants"]).then_inc(ld_const, 16)
            act.dma_start(biases[:, 0:6], a["bias_columns"]).then_inc(ld_small, 16)
            act.dma_start(row_pack[:, :], a["rows"].partition_broadcast(P)).then_inc(ld_small, 16)
            for half in range(2):
                act.dma_start(mask_i[half * S:(half + 1) * S, :], a["mask_1x1xSxS2_ik0"][0, 0, :, :])\
                    .then_inc(ld_small, 16)
            act.dma_start(bo_row[64:65, :, :], a["output_biases"].rearrange("(o l d) -> o l d", o=1, d=D))\
                .then_inc(ld_late, 16)
            act.dma_start(by_expert[:, :], a["by_expert"]).then_inc(ld_late, 16)
            act.dma_start(by_feature[:, 8:8 + FEATURE_N], a["by_feature"]).then_inc(ld_late, 16)

            def xT_halves(n):
                for half in range(2):
                    act.wait_ge(xT_psum, NT * n + 4 * half + 4)
                    act.copy(xT[:, half * HALF:(half + 1) * HALF], bank[6 + half][:, :]).then_inc(xT_ready, 4)

            for half in range(2):
                act.wait_ge(ctxT_psum, half + 1)
                act.copy(ctxT[:, half * HALF:(half + 1) * HALF], bank[half][:, :]).then_inc(ctxT_ready, 1)
            xT_halves(0)
            for i in range(2):
                act.wait_ge(wT_psum, i + 1)
                act.copy(wT[:, 4 * i:4 * i + 4, :], bank[2 + i][:, :].rearrange("p (i d) -> p i d", i=4))\
                    .then_inc(wT_ready, 1)
            act.wait_ge(ld_small, 16 * 4)
            act.activation(gates[:, :], gates[:, :], ACT.Tanh).then_inc(gates_ready, 1)
            act.wait_ge(wo_psum, 1)
            act.wait_ge(gates_ready, 1)
            act.wait_ge(consts_set, 1)
            act.wait_ge(ld_late, 16 * 4)
            for m in range(NM):
                g = gates[0:64, MHA_GATE[m]:MHA_GATE[m] + 1]
                src = bank[4 + m // 2][0:64, (m % 2) * 256:(m % 2) * 256 + 256].rearrange("p (j d) -> p j d", j=2)
                ins = act.activation(w_out[0:64, m, :, :], src, ACT.Copy, scale=g)
                if m == 1:
                    ins.then_inc(wo_ready, 1)
            ins.then_inc(wo_ready, 1)
            for i, m in enumerate((0, 1, 3)):
                g = gates[64:65, MHA_GATE[m]:MHA_GATE[m] + 1]
                link(act.activation(w_out[64:65, m, 0, :], bo_row[64:65, i, :], ACT.Copy, scale=g))
            act.wait_ge(gw_psum, 1)
            act.copy(gate_w[:, 0, :], bank[7][:, 0:8]).then_inc(gw_ready, 1)

            def mha(*calls, while_draining=None):
                def step(tau, s, i, steady):
                    u = 1 - s
                    at = place(calls, i, 2 * tau + s - 1, B, steady)
                    if at:
                        m, b, g = at
                        act.wait_ge(pT_psum, g + 1)
                        after(act, pv_done, g - 1)
                        act.copy(probsT[:, u, :, :], bank[2][:, :].rearrange("p (i q) -> p i q", i=QUAD))\
                            .then_inc(pT_ready, 1)
                    at = place(calls, i, 2 * tau + s, B, steady)
                    if at:
                        m, b, g = at
                        act.wait_ge(shift_ready, g + 1)
                        after(act, pT_psum, g - 1)
                        act.activation(probs[:, s, :, :], shifted[:, s, :, :], ACT.Exp).then_inc(exp_done, 1)
                    at = place(calls, i, 2 * tau + s - 3, B, steady)
                    if at:
                        m, b, g = at
                        act.wait_ge(oT_psum, g + 1)
                        if s == 1:
                            after(act, y_psum, place(calls, i, tau - 1, NT, steady)[2])
                        act.copy(oT[0:64, :, u * S:(u + 1) * S],
                                 bank[6][0:64, u * P:(u + 1) * P].rearrange("p (j q) -> p j q", j=2)).then_inc(oT_ready, 1)

                def tile_step(tau, i, steady):
                    step(tau, 0, i, steady)
                    step(tau, 1, i, steady)
                    at = place(calls, i, tau - 4, NT, steady)
                    if at:
                        m, t, g = at
                        act.wait_ge(xT_psum, NT * NEXT_LN[m] + t + 1)
                        act.copy(xT[:, bass.ds(t * P, P)], bank[3][:, 0:P]).then_inc(xT_ready, 1)
                run_tiles(act, calls, tile_step, while_draining=while_draining)

            def split_up(f, e, slot):
                pair0, exp0, dma0, split0 = ffn_states()[f]
                act.wait_ge(up_loaded[slot], dma0 + 16 * UP_DMA[f] * (e + 1))
                after(act, up_psum, pair0 + 2 * FFN_C[f] * (2 * e + slot - 1))
                n = 256 if f == 0 else 512
                act.copy(w_up_hi[:, slot, 0:n], w_up[:, slot, 0:n]).then_inc(w_hi_ready, 1)

            def split_down(f, e, slot):
                pair0, exp0, dma0, split0 = ffn_states()[f]
                chunks = FFN_C[f]
                act.wait_ge(dn_loaded[slot], 16 * (exp0 // 2 + 1 + e))
                after(act, down_psum, pair0 + 2 * chunks * (2 * e + slot - 1))
                act.copy(w_dn_hi[:, slot, 0:chunks, :], w_dn[:, slot, 0:chunks, :]).then_inc(w_hi_ready, 1)

            def split_x(f, half):
                ts = slice(half * HALF, (half + 1) * HALF)
                act.wait_ge(xT_ready, NT * FFN_LN[f] + 4 * half + 4)
                act.copy(xT_hi[:, ts], xT[:, ts]).then_inc(x_hi_ready, 1)

            def early_splits(f):
                def hook(k):
                    if k == 0:
                        split_x(f, 0)
                    if k == 1 and f == 1:
                        router_hidden(0)
                    if k == 2:
                        split_up(f, 0, 0)
                        split_down(f, 0, 0)
                return hook

            def router_hidden(half):
                act.wait_ge(r1_psum, half + 1)
                act.activation(r1[:, half * HALF:(half + 1) * HALF], bank[half][:, :], ACT.Silu).then_inc(r1_ready, 1)

            def ffn(f, state, router):
                chunks = FFN_C[f]
                per = 2 * chunks
                pair0, exp0, dma0, split0 = state

                def leading(local, u):
                    act.wait_ge(hid_ready, pair0 + local + 1)
                    after(act, down_psum, pair0 + local - RING + 1)
                    act.copy(hid_hi[:, u, :], hid[:, u, :]).then_inc(hi_ready, 1)

                def body(e, first, last):
                    for j in range(4 * chunks):
                        local = 4 * chunks * e + j
                        n = pair0 + local
                        u, ej, slot = j % 2, j % per, j // per
                        act.wait_ge(up_psum, n + 1)
                        if f < 2:
                            after(act, product_ready, n - 1)
                            act.activation(act_out[:, u, :], bank[2 * u][:, :], ACT.Silu).then_inc(silu_ready, 1)
                            if first and j == 1:
                                if f == 0:
                                    combT_halves(1)
                                row_halves(f)
                            if not (first and j == 0):
                                leading(local - 1, (j - 1) % RING)
                        else:
                            c = j % chunks
                            act.wait_ge(glu_ready, local + 1)
                            after(act, lin_ready, local - 1)
                            after(act, gated_ready, local - 1)
                            act.activation(act_out[:, u, :], glu[:, u, :], ACT.Sigmoid, scale=1.702)\
                                .then_inc(sigmoid_ready, 1)
                            act.activation(over[:, u, :], bank[2 * u + 1][:, :], ACT.Relu, scale=-1.0,
                                           bias=b1_col[:, c, 1, bass.ds(2 * e + slot, 1)]).then_inc(over_ready, 1)
                            act.wait_ge(over_ready, local + 1)
                            after(act, plain_ready, local - 1)
                            act.activation(lin[:, u, :], over[:, u, :], ACT.Relu, scale=-1.0, bias=fourteen[:, :])\
                                .then_inc(lin_ready, 1)
                            if first and j == 0:
                                row_halves(f)
                        if f == 0 and ej == 0 and not (first and slot == 0):
                            split_down(f, e, slot)
                        if ej == SPLIT_UP_AT[f] and not (last and slot):
                            split_up(f, e + slot, 1 - slot)
                        if f == 1 and ej == per - 1 and not (last and slot):
                            split_down(f, e + slot, 1 - slot)
                    if last and f < 2:
                        leading(4 * chunks * e + 4 * chunks - 1, RING - 1)

                if f == 2:
                    split_x(f, 0)
                split_x(f, 1)
                if f == 2:
                    split_up(f, 0, 0)
                router()
                run_experts(act, f, body)
                for half in range(2):
                    act.wait_ge(down_psum, pair0 + per * FFN_E[f] - chunks * (1 - half))
                    act.copy(outT[:, half * HALF:(half + 1) * HALF], bank[6 + half][:, :]).then_inc(outT_ready, 1)

            def exp_of_logits(k):
                act.wait_ge(dve_to_act, k)
                act.activation(logits[:, :, :], logits[:, :, :], ACT.Exp).then_inc(act_to_dve, 1)

            def row_halves(f):
                act.wait_ge(row_psum, f + 1)
                for half in range(2):
                    act.copy(comb_row[:, 0, half * HALF:(half + 1) * HALF], bank[6 + half][:, :]).then_inc(row_ready, 1)

            def combT_halves(i):
                act.wait_ge(combT_psum, i)
                for g in range(2):
                    ins = act.copy(combT[:, g * HALF:(g + 1) * HALF], bank[6 + g][0:8, :])
                ins.then_inc(combT_ready, 1)

            def router_2():
                act.wait_ge(dve_to_act, 3)
                act.activation(rp[:, :, :], rwork[:, :, :], ACT.Exp).then_inc(act_to_dve, 1)

            states = ffn_states()
            def biased(n, dst, half, b_col):
                act.wait_ge(proj_psum, n + 1)
                act.activation(dst[:, half * HALF:(half + 1) * HALF], bank[n % 4][:, :], ACT.Identity, bias=b_col)\
                    .then_inc(proj_ready, 1)

            mha(0, while_draining=early_splits(0))

            def router_0():
                exp_of_logits(1)
                for half in range(2):
                    act.wait_ge(k1_psum, half + 1)
                    act.activation(kT[:, 1, half * HALF:(half + 1) * HALF], bank[4 + half][:, :], ACT.Identity,
                                   bias=bk1).then_inc(k1_ready, 1)
            ffn(0, states[0], router_0)
            xT_halves(2)
            biased(8, qT, 0, bq1)
            biased(9, qT, 1, bq1)
            mha(1)
            exp_of_logits(2)
            for half in range(2):
                biased(10 + 2 * half, qT, half, bqs)
                biased(11 + 2 * half, kT[:, 0, :], half, bks)
            combT_halves(2)
            mha(2, 3, while_draining=early_splits(1))
            router_hidden(1)
            ffn(1, states[1], router_2)
            xT_halves(6)
            for g in range(2):
                act.wait_ge(s3_ready, g + 1)
                for half in range(2):
                    rows = slice(half * S, (half + 1) * S)
                    ins = act.activation(p3[rows, 4 * g:4 * g + 4, half * S:(half + 1) * S],
                                         s3[rows, 4 * g:4 * g + 4, :], ACT.Exp, scale=float(1.0 / np.sqrt(D)))
                ins.then_inc(p3_ready, 1)
                act.wait_ge(p3T_psum, g + 1)
                act.copy(p3T[:, 4 * g:4 * g + 4, :], bank[2 + g][:, :].rearrange("p (i q) -> p i q", i=4))\
                    .then_inc(p3T_ready, 1)
            xT_halves(7)
            
            def router_3():
                exp_of_logits(4)
                combT_halves(3)
            ffn(2, states[2], router_3)

        @block.gpsimd
        def _(pool):
            done = [0]

            def link(ins):
                done[0] += 1
                ins.then_inc(pool_done, 1)
                pool.wait_ge(pool_done, done[0])

            link(pool.memset(minus_half[:, :], -0.5))
            link(pool.memset(zero_bf[:, :], 0.0))
            link(pool.memset(eps_col[:, :], LN_EPS))
            link(pool.memset(fourteen[:, :], 14.0))
            link(pool.memset(oT[64:65, :, :], 1.0))
            link(pool.memset(ctx_tok[:, :, D:D + 1], 1.0))
            link(pool.memset(o_norm[:, :, :, :, :], 0.0))
            link(pool.memset(p3[:, :, :], 0.0))
            pool.memset(w_out[64:65, :, :, :], 0.0).then_inc(consts_set, 1)
            pool.wait_ge(consts_set, 1)

            def rstd_of(n):
                for half in range(2):
                    ts = slice(4 * half, 4 * half + 4)
                    pool.wait_ge(mv_ready, NT * n + 4 * half + 4)
                    link(pool.tensor_scalar(var_eps[:, ts], mv[:, ts, 1], LN_EPS, None, ALU.add))
                    pool.tensor_tensor(rstd[:, ts], var_eps[:, ts], minus_half[:, ts], ALU.pow).then_inc(rstd_ready, 4)

            def mha(*calls, while_draining=None):
                def step(tau, s, i, steady):
                    at = place(calls, i, 2 * tau + s, B, steady)
                    if not at:
                        return
                    m, b, g = at
                    q_src, k_src = ((qT, kT[:, 0, :]), (qT, kT[:, 1, :]), (qT, kT[:, 0, :]), (xT, ctxT))[m]
                    cols = bass.ds(b * S, S)
                    if m == 3 and not steady:
                        pool.wait_ge(xT_ready, NT * NEXT_LN[2] + b // 2 + 1)
                    after(pool, scores_done, g - 1)
                    pool.tensor_tensor(q_blk[:, s, :, :], q_src[:, cols].unsqueeze(1).broadcast_to([P, 2, S]),
                                       q_scale[:, 0 if m < 2 else 1, :, :], ALU.mult).then_inc(blocks_ready, 1)
                    pool.tensor_tensor(k_blk[:, s, :, :], k_src[:, cols].unsqueeze(1).broadcast_to([P, PAIR, S]),
                                       const[:, C_PM:C_PM + PAIR].unsqueeze(2).broadcast_to([P, PAIR, S]), ALU.mult)\
                        .then_inc(blocks_ready, 1)

                def tile_step(tau, i, steady):
                    step(tau, 0, i, steady)
                    at = place(calls, i, tau - 4, NT, steady)
                    if at:
                        m, t, g = at
                        pool.wait_ge(mv_ready, NT * NEXT_LN[m] + t + 1)
                        pool.tensor_tensor(var_slot[:, :], mv_slot[:, 1:2], eps_col[:, :], ALU.add).then_inc(eps_added, 1)
                        pool.wait_ge(eps_added, g + 1)
                        pool.tensor_tensor(rstd_slot[:, :], var_slot[:, :], minus_half[:, 0:1], ALU.pow)\
                            .then_inc(rstd_ready, 1)
                    step(tau, 1, i, steady)

                def halves_ready(m):
                    if m == 3:
                        pool.wait_ge(xT_ready, NT * (NEXT_LN[2] + 1))
                    else:
                        pool.wait_ge(proj_ready, (8, 10, 14)[m])
                pool.wait_ge(q_scale_ready, 1)
                pool.wait_ge(proj_ready, (4, 9, 12)[calls[0]])
                if calls[0] == 1:
                    pool.wait_ge(k1_ready, 2)
                run_tiles(pool, calls, tile_step, halves_ready, while_draining)

            def split_up(f, slot, n):
                pool.wait_ge(w_hi_ready, ffn_states()[f][3] + n)
                m = 256 if f == 0 else 512
                pool.tensor_tensor(w_up_lo[:, slot, 0:m], w_up[:, slot, 0:m], w_up_hi[:, slot, 0:m].bitcast(F32),
                                   ALU.subtract).then_inc(w_lo_ready[f], 1)

            def split_down(f, slot, n):
                chunks = FFN_C[f]
                pool.wait_ge(w_hi_ready, ffn_states()[f][3] + n)
                pool.tensor_tensor(w_dn_lo[:, slot, 0:chunks, :], w_dn[:, slot, 0:chunks, :],
                                   w_dn_hi[:, slot, 0:chunks, :].bitcast(F32), ALU.subtract).then_inc(w_lo_ready[f], 1)

            def early_splits(f):
                def hook(k):
                    if k == 3:
                        split_up(f, 0, 1)
                        split_down(f, 0, 2)
                return hook

            def ffn(f, state):
                chunks = FFN_C[f]
                per = 2 * chunks
                pair0, exp0, dma0, split0 = state

                def body(e, first, last):
                    for j in range(4 * chunks):
                        local = 4 * chunks * e + j
                        n = pair0 + local
                        u, ej, slot = j % 2, j % per, j // per
                        half = ej // chunks
                        if f < 2:
                            wait_for_weights(pool, f, e, ej, slot, first)
                            pool.wait_ge(product_ready, n + 1)
                            after(pool, lo_ready, n - RING + 1)
                            pool.tensor_tensor(hid[:, j % RING, :], product[:, u, :],
                                               comb_row[:, slot, half * HALF:(half + 1) * HALF], ALU.mult)\
                                .then_inc(hid_ready, 1)
                        else:
                            pool.wait_ge(sigmoid_ready, local + 1)
                            after(pool, plain_ready, local - 1)
                            pool.tensor_tensor(gated[:, u, :], glu[:, u, :], act_out[:, u, :], ALU.mult)\
                                .then_inc(gated_ready, 1)
                        before = FFN_SPLITS[f] * (2 * e + slot + 1)
                        if f == 1 and not (last and slot):
                            if ej == SPLIT_UP_AT[f]:
                                split_up(f, 1 - slot, before + 1)
                            if ej == per - 1:
                                split_down(f, 1 - slot, before + 2)

                run_experts(pool, f, body)

            states = ffn_states()

            rstd_of(0)
            pool.memset(v_blk[:, :, :, :], 0.0).then_inc(v_cleared, 1)
            pool.wait_ge(v_cleared, 1)
            ones = v_blk[:, :, :, :].rearrange("p m b (i j c) -> p (m b i) j c", i=QUAD, j=2)
            for j in range(2):
                pool.memset(ones[j * S:(j + 1) * S, :, j, VW - 1:VW], 1.0).then_inc(v_cleared, 1)
                pool.wait_ge(v_cleared, j + 2)
            mha(0)
            pool.wait_ge(ld_dup, 32)
            for j in range(2):
                rows = slice(j * S, (j + 1) * S)
                dst = v_blk[rows, 3, :, :].rearrange("p b (i j c) -> p b i j c", i=QUAD, j=2)[:, :, :, j, 0:2 * DK]
                src = ctx_dup[rows, :, :].rearrange("p b (i j c) -> p b i j c", i=QUAD, j=2)[:, :, :, j, :]
                pool.tensor_copy(dst, src).then_inc(v3_ready, 1)
                pool.wait_ge(v3_ready, j + 1)
            ffn(0, states[0])
            rstd_of(2)
            mha(1)
            mha(2, 3, while_draining=early_splits(1))
            ffn(1, states[1])
            rstd_of(6)
            for half in range(2):
                ts = slice(4 * half, 4 * half + 4)
                pool.wait_ge(mv_ready, NT * 7 + 4 * half + 4)
                link(pool.tensor_scalar(var_eps[:, ts], mv[:, ts, 1], LN_EPS, None, ALU.add))
                pool.tensor_tensor(rstd[:, ts], var_eps[:, ts], minus_half[:, ts], ALU.pow).then_inc(rstd_ready, 4)
                pool.wait_ge(rstd_ready, NT * 7 + 8 * half + 4)
                link(pool.tensor_tensor(var_eps[:, ts], rstd[:, ts], rstd[:, ts], ALU.mult))
                link(pool.tensor_tensor(var_eps[:, ts], var_eps[:, ts], mv[:, ts, 1], ALU.mult))
                link(pool.tensor_scalar(var_eps[:, ts], var_eps[:, ts], LN_EPS, None, ALU.add))
                pool.tensor_tensor(rstd_rms[:, ts], var_eps[:, ts], minus_half[:, ts], ALU.pow).then_inc(rstd_ready, 4)
            ffn(2, states[2])

        @block.vector
        def _(dve):
            v = nc.vector
            done = [0]

            def link(ins):
                done[0] += 1
                ins.then_inc(dve_done, 1)
                dve.wait_ge(dve_done, done[0])

            count = [0]

            def rotated(dst, half, b_col, r_col):
                def table(c):
                    return const[:, c:c + S].unsqueeze(1).broadcast_to([P, HALF // S, S])

                def split(ap):
                    return ap.rearrange("p (b s) -> p b s", s=S)
                d = dst[:, half * HALF:(half + 1) * HALF]
                n = count[0]
                dve.wait_ge(proj_psum, n + 1)
                link(v.scalar_tensor_tensor(split(d), split(bank[n % 4][:, :]), b_col, table(C_COS), ALU.add, ALU.mult))
                dve.wait_ge(proj_psum, n + 2)
                link(v.scalar_tensor_tensor(split(rot_tmp[:, :]), split(bank[(n + 1) % 4][:, :]), r_col, table(C_SIN),
                                            ALU.add, ALU.mult))
                v.tensor_tensor(d, d, rot_tmp[:, :], ALU.add).then_inc(proj_ready, 2)
                count[0] += 2

            vcount = [0]

            def values(m, bias_i, groups=range(4)):
                dve.wait_ge(v_cleared, 3)
                for g in groups:
                    n = vcount[0]
                    dve.wait_ge(v_psum, n + 1)
                    src = bank[4 + n % 2][:, :].rearrange("p (b i j c) -> p b i j c", b=4, i=QUAD, j=2)
                    for j in range(2):
                        rows = slice(j * S, (j + 1) * S)
                        bias = v_bias[rows, bias_i, :].rearrange("p (i j c) -> p i j c", i=QUAD, j=2)[:, :, j, :]
                        parts = ((0, 4, 4 * g),) if j == 0 else ((0, 4, 4 * g + 1),) if g < 3 else ((0, 3, 13), (3, 4, 0))
                        for i0, i1, b0 in parts:
                            dst = v_blk[rows, m, b0:b0 + i1 - i0, :].rearrange("p b (i j c) -> p b i j c", i=QUAD, j=2)
                            ins = v.tensor_tensor(dst[:, :, :, j, 0:2 * DK], src[rows, i0:i1, :, j, :],
                                                  bias.unsqueeze(1).broadcast_to([S, i1 - i0, QUAD, 2 * DK]), ALU.add)
                    ins.then_inc(v_ready, 1)
                    vcount[0] += 1

            def statistics(n, src, half):
                for t in range(4 * half, 4 * half + 4):
                    ins = v.bn_stats(stats[:, t, :], src[:, t, :])
                link(ins)
                for t in range(4 * half, 4 * half + 4):
                    v.bn_aggr(mv[:, t, :], stats[:, t, :]).then_inc(mv_ready, 1)

            def normed(n, half):
                dve.wait_ge(mv_ready, NT * n + 4 * half + 4)
                dve.wait_ge(rstd_ready, NT * n + 4 * half + 4)
                for t in range(4 * half, 4 * half + 4):
                    ins = v.tensor_scalar(x_norm[:, t, :], x_tok[:, t, :], mv[:, t, 0:1], rstd[:, t:t + 1],
                                          ALU.subtract, ALU.mult)
                    ins.then_inc(xn_ready, 1)

            def layer_norm(n):
                statistics(n, x_tok, 0)
                statistics(n, x_tok, 1)
                normed(n, 0)
                normed(n, 1)

            def mha(*calls, while_draining=None):
                def subtract_max(tau, s, i, steady):
                    at = place(calls, i, 2 * tau + s, B, steady)
                    if at:
                        m, b, g = at
                        scores = bank[s][:, :].rearrange("p (h k) -> p h k", h=PAIR)
                        dve.wait_ge(scores_done, g + 1)
                        v.reduce_max(row_max[:, s, :], scores, AX).then_inc(max_ready, 1)
                        dve.wait_ge(max_ready, g + 1)
                        after(dve, exp_done, g - 1)
                        v.tensor_tensor(shifted[:, s, :, :], scores,
                                        row_max[:, s, :].unsqueeze(2).broadcast_to([P, PAIR, S]), ALU.subtract)\
                            .then_inc(shift_ready, 1)

                def normalise(tau, s, i, steady):
                    at = place(calls, i, 2 * tau + s - 2, B, steady)
                    if at:
                        m, b, g = at
                        dve.wait_ge(pv_done, g + 1)
                        o = bank[4 + s][:, 0:VB].rearrange("p (h c) -> p h c", h=PAIR)
                        v.reciprocal(inv_sum[:, s, :], o[:, :, VW - 1]).then_inc(inv_ready, 1)
                        dve.wait_ge(inv_ready, g + 1)
                        after(dve, oT_psum, g - 1)
                        for j2 in range(2):
                            rows = slice(j2 * S, (j2 + 1) * S)
                            ins = v.tensor_tensor(o_norm[rows, s, 0, :, :], o[rows, :, j2 * DK:(j2 + 1) * DK],
                                                  inv_sum[rows, s, :].unsqueeze(2).broadcast_to([S, PAIR, DK]), ALU.mult)
                        ins.then_inc(on_ready, 1)

                def tile_step(tau, i, steady):
                    stat = place(calls, i, tau - 3, NT, steady)
                    norm = place(calls, i, tau - 4, NT, steady)
                    if stat:
                        dve.wait_ge(x_added, stat[2] + 1)
                    subtract_max(tau, 0, i, steady)
                    if stat:
                        v.bn_stats(stats_slot[:, :], x_tok[:, bass.ds(stat[1], 1), :].rearrange("p o d -> p (o d)"))\
                            .then_inc(stats_ready, 1)
                    normalise(tau, 0, i, steady)
                    if norm:
                        m, t, g = norm
                        dve.wait_ge(rstd_ready, NT * NEXT_LN[m] + t + 1)
                        dve.wait_ge(xT_psum, NT * NEXT_LN[m] + t)
                        v.tensor_scalar(xn_slot[:, :], x_tok[:, bass.ds(t, 1), :].rearrange("p o d -> p (o d)"),
                                        mv_slot[:, 0:1], rstd_slot[:, :], ALU.subtract, ALU.mult).then_inc(xn_ready, 1)
                    if stat:
                        m, t, g = stat
                        dve.wait_ge(stats_ready, g + 1)
                        dve.wait_ge(xn_ready, NT * NEXT_LN[m] + t)
                    subtract_max(tau, 1, i, steady)
                    if stat:
                        v.bn_aggr(mv_slot[:, :], stats_slot[:, :]).then_inc(mv_ready, 1)
                    normalise(tau, 1, i, steady)
                    at = place(calls, i, tau - 2, NT, steady)
                    if at:
                        m, t, g = at
                        xs = x_tok[:, bass.ds(t, 1), :].rearrange("p o d -> p (o d)")
                        dve.wait_ge(y_psum, g + 1)
                        v.tensor_tensor(xs, xs, bank[7][:, 0:D], ALU.add).then_inc(x_added, 1)
                run_tiles(dve, calls, tile_step, while_draining=while_draining)
                dve.wait_ge(xn_ready, NT * (NEXT_LN[calls[-1]] + 1))

            def top2_router(i, k, bias_i):
                dve.wait_ge(logit_psum, i + 1)
                src = bank[0][:, 0:NT * 8].rearrange("p (t e) -> p t e", t=NT)
                if bias_i is None:
                    ins = v.tensor_copy(logits[:, :, :], src)
                else:
                    ins = v.tensor_tensor(logits[:, :, :], src,
                                          gate_b[:, bias_i, :].unsqueeze(1).broadcast_to([P, NT, 8]), ALU.add)
                ins.then_inc(logits_read, 1)
                dve.wait_ge(logits_read, i + 1)
                mine = logits[:, :, :].unsqueeze(3).broadcast_to([P, NT, 8, 8])
                other = logits[:, :, :].unsqueeze(2).broadcast_to([P, NT, 8, 8])
                tri = const[:, C_TRI:C_TRI + 64].rearrange("p (e f) -> p e f", e=8).unsqueeze(1).broadcast_to([P, NT, 8, 8])
                v.tensor_tensor(gt[:, :, :, :], other, mine, ALU.is_gt)
                v.reduce_max(e_max[:, :], logits[:, :, :], AX)
                link(v.tensor_tensor(eq[:, :, :, :], other, mine, ALU.is_equal))
                v.tensor_tensor(logits[:, :, :], logits[:, :, :], e_max[:, :].unsqueeze(2).broadcast_to([P, NT, 8]),
                                ALU.subtract).then_inc(dve_to_act, 1)
                link(v.tensor_tensor(eq[:, :, :, :], eq[:, :, :, :], tri, ALU.mult))
                link(v.tensor_tensor(gt[:, :, :, :], gt[:, :, :, :], eq[:, :, :, :], ALU.add))
                link(v.reduce_sum(rank[:, :, :], gt[:, :, :, :], AX))
                link(v.tensor_scalar(top[:, :, :], rank[:, :, :], 1.5, None, ALU.is_lt))
                dve.wait_ge(act_to_dve, k)

                def share(eps):
                    link(v.reduce_sum(e_sum[:, :], logits[:, :, :], AX))
                    if eps:
                        link(v.tensor_scalar(e_sum[:, :], e_sum[:, :], eps, None, ALU.add))
                    link(v.reciprocal(e_sum[:, :], e_sum[:, :]))
                    link(v.tensor_tensor(logits[:, :, :], logits[:, :, :],
                                         e_sum[:, :].unsqueeze(2).broadcast_to([P, NT, 8]), ALU.mult))
                if i < 2:
                    share(0)
                link(v.tensor_tensor(logits[:, :, :], logits[:, :, :], top[:, :, :], ALU.mult))
                if i == 0:
                    share(1e-9)
                    share(1e-9)
                if i == 2:
                    share(0)
                gate = gates[:, (4, 5, 7)[i]:(4, 5, 7)[i] + 1]
                ins = v.tensor_scalar(comb[:, :, 0:8], logits[:, :, :], gate, None, ALU.mult)
                ins.then_inc(comb_ready, 1)
                dve.wait_ge(comb_ready, i + 1)

            def add_biases(i):
                dve.wait_ge(be_psum, i)
                for g in range(2):
                    xs = x_tok[:, 4 * g:4 * g + 4, :]
                    ins = v.tensor_tensor(xs, xs, bank[4 + g][:, :].rearrange("p (t d) -> p t d", t=4), ALU.add)
                ins.then_inc(be_added, 1)
                dve.wait_ge(be_added, i)

            def split_x(f, half):
                ts = slice(half * HALF, (half + 1) * HALF)
                dve.wait_ge(x_hi_ready, 2 * f + half + 1)
                v.tensor_tensor(xT_lo[:, ts], xT[:, ts], xT_hi[:, ts].bitcast(F32), ALU.subtract)\
                    .then_inc(x_lo_ready, 1)

            def split_up(f, slot, n):
                m = 256 if f == 0 else 512
                dve.wait_ge(w_hi_ready, ffn_states()[f][3] + n)
                v.tensor_tensor(w_up_lo[:, slot, 0:m], w_up[:, slot, 0:m], w_up_hi[:, slot, 0:m].bitcast(F32),
                                ALU.subtract).then_inc(w_lo_ready[f], 1)

            def split_down(f, slot, n):
                dve.wait_ge(w_hi_ready, ffn_states()[f][3] + n)
                v.tensor_tensor(w_dn_lo[:, slot, 0, :], w_dn[:, slot, 0, :], w_dn_hi[:, slot, 0, :].bitcast(F32),
                                ALU.subtract).then_inc(w_lo_ready[f], 1)

            def early_splits(f):
                def hook(k):
                    if k == 1:
                        split_x(f, 0)
                    if k == 3 and f == 0:
                        split_up(0, 0, 1)
                        split_down(0, 0, 2)
                return hook

            def ffn(f, state, router, meanwhile=None):
                chunks = FFN_C[f]
                per = 2 * chunks
                pair0, exp0, dma0, split0 = state

                def trailing(local, u):
                    dve.wait_ge(hi_ready, pair0 + local + 1)
                    after(dve, down_psum, pair0 + local - RING + 1)
                    v.tensor_tensor(hid_lo[:, u, :], hid[:, u, :], hid_hi[:, u, :].bitcast(F32), ALU.subtract)\
                        .then_inc(lo_ready, 1)

                def weighted(e, local, j, first=False):
                    u, ej, slot = j % 2, j % per, j // per
                    half = ej // chunks
                    dve.wait_ge(gated_ready, local + 1)
                    dve.wait_ge(lin_ready, local + 1)
                    after(dve, hid_ready, pair0 + local - 1)
                    v.scalar_tensor_tensor(product[:, u, :], lin[:, u, :], -6.0, gated[:, u, :], ALU.add, ALU.mult)\
                        .then_inc(plain_ready, 1)
                    wait_for_weights(dve, f, e, ej, slot, first)
                    dve.wait_ge(plain_ready, local + 1)
                    after(dve, down_psum, pair0 + local - RING + 1)
                    v.tensor_tensor(hid[:, j % RING, :], product[:, u, :],
                                    comb_row[:, slot, half * HALF:(half + 1) * HALF], ALU.mult).then_inc(hid_ready, 1)

                def body(e, first, last):
                    pairs = 4 * chunks
                    for j in range(pairs):
                        local = pairs * e + j
                        n = pair0 + local
                        u = j % 2
                        if f < 2:
                            dve.wait_ge(silu_ready, n + 1)
                            after(dve, hid_ready, n - 1)
                            v.tensor_tensor(product[:, u, :], act_out[:, u, :], bank[2 * u + 1][:, :], ALU.mult)\
                                .then_inc(product_ready, 1)
                            if first and j == 1 and meanwhile:
                                meanwhile()
                            if not (first and j == 0):
                                trailing(local - 1, (j - 1) % RING)
                        else:
                            ej, slot = j % per, j // per
                            dve.wait_ge(up_psum, n + 1)
                            after(dve, gated_ready, local - 1)
                            v.tensor_scalar(glu[:, u, :], bank[2 * u][:, :],
                                            b1_col[:, j % chunks, 0, bass.ds(2 * e + slot, 1)], 7.0, ALU.add, ALU.min)\
                                .then_inc(glu_ready, 1)
                            if first and j == 1:
                                meanwhile()
                            if j > 0:
                                weighted(e, local - 1, j - 1, first)
                            elif not first:
                                weighted(e - 1, local - 1, pairs - 1)
                        ej, slot = j % per, j // per
                        before = FFN_SPLITS[f] * (2 * e + slot + 1)
                        if f == 0 and ej == 0 and not (first and slot == 0):
                            split_down(f, slot, before)
                        if f != 1 and ej == (0, 0, 2)[f] and not (last and slot):
                            split_up(f, 1 - slot, before + 1)
                    if last:
                        if f < 2:
                            trailing(pairs * e + pairs - 1, RING - 1)
                        else:
                            weighted(e, pairs * e + pairs - 1, pairs - 1)

                if f == 2:
                    split_x(f, 0)
                split_x(f, 1)
                if f == 2:
                    split_up(f, 0, 1)
                router()
                run_experts(dve, f, body)
                for half in range(2):
                    dve.wait_ge(out_psum, 2 * f + half + 1)
                    xs = x_tok[:, 4 * half:4 * half + 4, :]
                    v.tensor_tensor(xs, xs, bank[4 + half][:, :].rearrange("p (t d) -> p t d", t=4), ALU.add)\
                        .then_inc(out_added, 1)
                dve.wait_ge(out_added, 2 * (f + 1))

            states = ffn_states()
            dve.wait_ge(ld_x, 16)
            layer_norm(0)
            dve.wait_ge(ld_const, 16)
            v.tensor_copy(dup_bf[:, :], const[:, C_DUP:C_DUP + P])
            dve.wait_ge(ld_w, 16)
            for m, w in enumerate((w_raw[:, 3, :], w_raw[:, 7, :], ident, w_raw[:, 8, :])):
                ins = v.tensor_copy(wo_by_j2[:, m, :, :].rearrange("n j (p d) -> n j p d", d=DK),
                                    w.rearrange("n (p j d) -> n j p d", j=2, d=DK))
            ins.then_inc(wo_split, 1)
            dve.wait_ge(ld_small, 16 * 4)
            link(v.tensor_scalar(mask_open[:, :], mask_i[:, :], 0, None, ALU.not_equal))
            v.tensor_scalar(mask_low[:, :], mask_open[:, :], -1.0, BIG, ALU.add, ALU.mult)
            v.reduce_max(row_open[:, :], mask_open[:, :], AX).then_inc(mask_ready, 1)
            dve.wait_ge(rb_psum, 1)
            v.tensor_copy(biases[:, 6:8], bank[6][:, 0:2]).then_inc(rb_ready, 1)
            dve.wait_ge(rb_ready, 1)
            dve.wait_ge(ro_psum, 1)
            for j2 in range(2):
                v.tensor_scalar(q_scale[:, 0, j2, :], bank[6][:, 64:128], const[:, C_JM + j2:C_JM + j2 + 1], None, ALU.mult)
            for j2 in range(2):
                ins = v.tensor_copy(q_scale[:, 1, j2, :], const[:, C_JM + j2:C_JM + j2 + 1].broadcast_to([P, S]))
            ins.then_inc(q_scale_ready, 1)
            for half in range(2):
                rotated(kT[:, 0, :], half, bk0, rk0)
                rotated(qT, half, bq0, rq0)
            dve.wait_ge(ld_late, 16 * 4)
            dve.wait_ge(b1_psum, 1)
            b1_src = bank[7][:, 16:48].rearrange("p (c k e) -> p c k e", c=2, k=2)
            v.tensor_copy(b1_col[:, :, 0, :], b1_src[:, :, 0, :])
            v.tensor_scalar(b1_col[:, :, 1, :], b1_src[:, :, 1, :], -1.0, 7.0, ALU.mult, ALU.add).then_inc(b1_ready, 1)

            values(0, 0)
            mha(0, while_draining=early_splits(0))

            ffn(0, states[0], lambda: top2_router(0, 1, None), lambda: values(1, 1))
            layer_norm(2)
            mha(1)
            top2_router(1, 2, 0)
            values(2, 2, (0, 1))
            n = 0
            for q in range(NT):
                if q == 2:
                    values(2, 2, (2, 3))
                pair, g = q // 2, q % 2
                dve.wait_ge(e1_psum, q + 1)
                for e in range(4):
                    for i in range(2):
                        t = 2 * pair + i
                        after(dve, e1_added, n - 1)
                        v.scalar_tensor_tensor(x_tok[:, t, :], bank[2 * i + g][:, e * D:(e + 1) * D],
                                               comb[:, t, 4 * g + e:4 * g + e + 1], x_tok[:, t, :], ALU.mult, ALU.add)\
                            .then_inc(e1_added, 1)
                        n += 1
            dve.wait_ge(e1_added, n)
            add_biases(1)
            mha(2, 3, while_draining=early_splits(1))

            def choice_router():
                dve.wait_ge(r2_psum, 1)
                v.tensor_copy(r2[:, :, :], bank[0][:, 0:NT * 16].rearrange("p (t e) -> p e t", t=NT)).then_inc(r2_ready, 1)
                dve.wait_ge(r2T_psum, 1)
                src = bank[1][:, 0:P].rearrange("p (f s) -> p f s", f=2)

                def over_tokens(ap):
                    return ap.unsqueeze(2).broadcast_to([P, 2, S])
                link(v.reduce_max(rcol[:, :], src, AX))
                v.tensor_tensor(rwork[:, :, :], src, over_tokens(rcol[:, :]), ALU.subtract).then_inc(dve_to_act, 1)
                dve.wait_ge(act_to_dve, 3)
                link(v.reduce_sum(rcol[:, :], rp[:, :, :], AX))
                link(v.reciprocal(rcol[:, :], rcol[:, :]))
                link(v.tensor_tensor(rp[:, :, :], rp[:, :, :], over_tokens(rcol[:, :]), ALU.mult))
                link(v.tensor_copy(rwork[:, :, :], rp[:, :, :]))
                for _ in range(TOP_C // 8):
                    for f in range(2):
                        ins = v.max(rtop[:, f, :], rwork[:, f, :])
                    link(ins)
                    for f in range(2):
                        ins = v.match_replace(rwork[:, f, :], rtop[:, f, :], rwork[:, f, :], -1.0)
                    link(ins)
                link(v.tensor_scalar(rwork[:, :, :], rwork[:, :, :], 0.0, None, ALU.is_lt))
                link(v.tensor_tensor(rp[:, :, :], rp[:, :, :], rwork[:, :, :], ALU.mult))
                link(v.reduce_sum(rcol[:, :], rp[:, :, :], AX))
                link(v.tensor_scalar(rcol[:, :], rcol[:, :], 1e-9, None, ALU.add))
                link(v.reciprocal(rcol[:, :], rcol[:, :]))
                link(v.tensor_scalar(rcol[:, :], rcol[:, :], gates[:, 6:7], None, ALU.mult))
                v.tensor_tensor(rsel[:, :, :], rp[:, :, :], over_tokens(rcol[:, :]), ALU.mult).then_inc(rsel_ready, 1)
            ffn(1, states[1], choice_router)
            layer_norm(6)
            for g in range(2):
                dve.wait_ge(s3_psum, g + 1)
                src = bank[g][:, :].rearrange("p (t k) -> p t k", t=4)
                for half in range(2):
                    rows = slice(half * S, (half + 1) * S)
                    ins = v.reduce_max(m3[rows, 4 * g:4 * g + 4], src[rows, :, half * S:(half + 1) * S], AX)
                link(ins)
                for half in range(2):
                    rows = slice(half * S, (half + 1) * S)
                    ins = v.tensor_tensor(s3[rows, 4 * g:4 * g + 4, :], src[rows, :, half * S:(half + 1) * S],
                                          m3[rows, 4 * g:4 * g + 4].unsqueeze(2).broadcast_to([S, 4, S]), ALU.subtract)
                ins.then_inc(s3_ready, 1)
            for g in range(2):
                for c in range(2):
                    dve.wait_ge(o3_psum, 2 * g + c + 1)
                    o = bank[(4, 5, 0, 1)[2 * g + c]][:, 0:2 * (D + 1)].rearrange("p (t c) -> p t c", t=2)
                    ts = slice(4 * g + 2 * c, 4 * g + 2 * c + 2)
                    link(v.reciprocal(m3[:, ts], o[:, :, D]))
                    link(v.tensor_scalar(m3[:, ts], m3[:, ts], gates[:, 3:4], None, ALU.mult))
                    for i in range(2):
                        t = 4 * g + 2 * c + i
                        ins = v.scalar_tensor_tensor(x_tok[:, t, :], o[:, i, 0:D], m3[:, t:t + 1], x_tok[:, t, :],
                                                     ALU.mult, ALU.add)
                link(ins)
                statistics(7, x_tok, g)
            for half in range(2):
                dve.wait_ge(rstd_ready, NT * 7 + 8 * half + 4)
                for t in range(4 * half, 4 * half + 4):
                    ins = v.tensor_scalar(x_norm[:, t, :], x_tok[:, t, :], mv[:, t, 0:1], rstd[:, t:t + 1],
                                          ALU.subtract, ALU.mult)
                link(ins)
                dve.wait_ge(rstd_ready, NT * 7 + 8 * half + 8)
                for t in range(4 * half, 4 * half + 4):
                    v.scalar_tensor_tensor(x_rms[:, t, :], x_norm[:, t, :], rstd_rms[:, t:t + 1], ns_row[:, :],
                                           ALU.mult, ALU.mult).then_inc(xn_ready, 1)

            def add_normed():
                for t in range(NT):
                    ins = v.scalar_tensor_tensor(x_tok[:, t, :], x_norm[:, t, :], gates[:, 7:8], x_tok[:, t, :],
                                                 ALU.mult, ALU.add)
                link(ins)
            ffn(2, states[2], lambda: top2_router(2, 4, 1), add_normed)


def kernel(**inputs):
    import concourse.bacc as bacc
    from concourse.bass_utils import run_bass_kernel_spmd

    nc = bacc.Bacc("TRN2", target_bir_lowering=False, num_devices=1)
    arrays, aps = {}, {}
    data = {name: np.ascontiguousarray(inputs[name]) for name in UNPACKED}
    data.update(packs(inputs))
    data["shape_constants"] = shape_constants()
    for name, array in data.items():
        arrays[f"in_{name}"] = array
        aps[name] = nc.dram_tensor(f"in_{name}", array.shape, mybir.dt.from_np(array.dtype), kind="ExternalInput").ap()
    out = nc.dram_tensor("out_x", (B, S, D), F32, kind="ExternalOutput").ap()
    comb_dram = [nc.dram_tensor(f"combine_{f}", (FFN_E[f], T), F32, kind="Internal").ap() for f in range(3)]
    build(nc, aps, comb_dram, out)
    result = run_bass_kernel_spmd(nc, [arrays], core_ids=[0])
    return result.results[0]["out_x"]
```
